# Optimizing a Trainium2 kernel written in Bass

```python
import numpy as np
import jax
import jax.numpy as jnp

def _softmax(x, axis=-1):
    return jax.nn.softmax(x, axis=axis)

def _gelu(x):
    return jax.nn.gelu(x, approximate=True)

def _silu(x):
    return jax.nn.silu(x)

def _sigmoid(x):
    return jax.nn.sigmoid(x)

def _layernorm(x, axis=-1, eps=1e-05):
    m = jnp.mean(x, axis=axis, keepdims=True)
    v = jnp.var(x, axis=axis, keepdims=True)
    return (x - m) / jnp.sqrt(v + eps)

def _scatter_add(tgt, idx, src, axis=0):
    return tgt.at[idx].add(src)

def _segment_sum(src, seg, n):
    return jax.ops.segment_sum(src, seg, n)
kernel_name = 'mk_macaron_d1_jaxref_r8_9a9d88'

def setup_inputs(seed: int=0):
    np.random.seed(seed)
    _w = jnp.asarray

    def _L0_attn_setup():
        import jax, jax.numpy as jnp
        import numpy as np
        B, T, C = (2, 256, 256)
        NH, NKV, HD = (16, 8, 32)
        SOFTCAP = 50.0
        ROPE_BASE = 10000.0

        def _rotate_half(x):
            x1, x2 = (x[..., :x.shape[-1] // 2], x[..., x.shape[-1] // 2:])
            return jnp.concatenate((-x2, x1), axis=-1)

        def _rope_cos_sin(t, head_dim, dtype):
            inv_freq = 1.0 / ROPE_BASE ** (jnp.arange(0, head_dim, 2, dtype=jnp.int32).astype(jnp.float32) / head_dim)
            pos = jnp.arange(t, dtype=jnp.float32)
            freqs = pos[:, None] * inv_freq[None, :]
            emb = jnp.concatenate((freqs, freqs), axis=-1)
            return (jnp.cos(emb).astype(dtype)[None, None], jnp.sin(emb).astype(dtype)[None, None])
        key = jax.random.key(seed)
        ks = jax.random.split(key, 5)
        s = 0.02
        return {'X': jax.random.normal(ks[0], (B, T, C), dtype=jnp.float32), 'Wq': jax.random.normal(ks[1], (C, NH * HD), dtype=jnp.float32) * s, 'Wk': jax.random.normal(ks[2], (C, NKV * HD), dtype=jnp.float32) * s, 'Wv': jax.random.normal(ks[3], (C, NKV * HD), dtype=jnp.float32) * s, 'Wo': jax.random.normal(ks[4], (NH * HD, C), dtype=jnp.float32) * s}
    _L0_attn_in = _L0_attn_setup()

    def _L0_ffn_setup():
        import jax, jax.numpy as jnp
        import numpy as np
        B, S, H = (2, 256, 256)
        E, K, F = (32, 4, 176)
        FS = 704
        EPS = 1e-06
        CAP = 128
        key = jax.random.key(seed)
        ks = jax.random.split(key, 10)
        s = 0.02
        return {'hidden_states': jax.random.normal(ks[0], (B, S, H), jnp.float32), 'w_norm': 1.0 + 0.02 * jax.random.normal(ks[1], (H,), jnp.float32), 'w_router': s * jax.random.normal(ks[2], (H, E), jnp.float32), 'w_gate': s * jax.random.normal(ks[3], (E, H, F), jnp.float32), 'w_up': s * jax.random.normal(ks[4], (E, H, F), jnp.float32), 'w_down': s * jax.random.normal(ks[5], (E, F, H), jnp.float32), 'sw_gate': s * jax.random.normal(ks[6], (H, FS), jnp.float32), 'sw_up': s * jax.random.normal(ks[7], (H, FS), jnp.float32), 'sw_down': s * jax.random.normal(ks[8], (FS, H), jnp.float32), 'w_shared_gate': s * jax.random.normal(ks[9], (H, 1), jnp.float32)}
    _L0_ffn_in = _L0_ffn_setup()
    _d = {'L0_attn_X': _L0_attn_in['X'], 'L0_attn_Wq': _L0_attn_in['Wq'], 'L0_attn_Wk': _L0_attn_in['Wk'], 'L0_attn_Wv': _L0_attn_in['Wv'], 'L0_attn_Wo': _L0_attn_in['Wo'], 'L0_ffn_w_norm': _L0_ffn_in['w_norm'], 'L0_ffn_w_router': _L0_ffn_in['w_router'], 'L0_ffn_w_gate': _L0_ffn_in['w_gate'], 'L0_ffn_w_up': _L0_ffn_in['w_up'], 'L0_ffn_w_down': _L0_ffn_in['w_down'], 'L0_ffn_sw_gate': _L0_ffn_in['sw_gate'], 'L0_ffn_sw_up': _L0_ffn_in['sw_up'], 'L0_ffn_sw_down': _L0_ffn_in['sw_down'], 'L0_ffn_w_shared_gate': _L0_ffn_in['w_shared_gate']}
    _x0 = _d['L0_attn_X']
    _d['L0_attn_X'] = jax.random.normal(jax.random.fold_in(jax.random.key(seed), 1), (16, 256, 256), dtype=_x0.dtype)
    del _x0
    return _d

def reference(L0_attn_X, L0_attn_Wq, L0_attn_Wk, L0_attn_Wv, L0_attn_Wo, L0_ffn_w_norm, L0_ffn_w_router, L0_ffn_w_gate, L0_ffn_w_up, L0_ffn_w_down, L0_ffn_sw_gate, L0_ffn_sw_up, L0_ffn_sw_down, L0_ffn_w_shared_gate):

    def _L0_attn_ref(X, Wq, Wk, Wv, Wo):
        import jax, jax.numpy as jnp
        import numpy as np
        B, T, C = (2, 256, 256)
        NH, NKV, HD = (16, 8, 32)
        SOFTCAP = 50.0
        ROPE_BASE = 10000.0

        def _rotate_half(x):
            x1, x2 = (x[..., :x.shape[-1] // 2], x[..., x.shape[-1] // 2:])
            return jnp.concatenate((-x2, x1), axis=-1)

        def _rope_cos_sin(t, head_dim, dtype):
            inv_freq = 1.0 / ROPE_BASE ** (jnp.arange(0, head_dim, 2, dtype=jnp.int32).astype(jnp.float32) / head_dim)
            pos = jnp.arange(t, dtype=jnp.float32)
            freqs = pos[:, None] * inv_freq[None, :]
            emb = jnp.concatenate((freqs, freqs), axis=-1)
            return (jnp.cos(emb).astype(dtype)[None, None], jnp.sin(emb).astype(dtype)[None, None])
        b, t, c = X.shape
        n_rep = NH // NKV
        q = (X @ Wq).reshape(b, t, NH, HD).transpose(0, 2, 1, 3)
        k = (X @ Wk).reshape(b, t, NKV, HD).transpose(0, 2, 1, 3)
        v = (X @ Wv).reshape(b, t, NKV, HD).transpose(0, 2, 1, 3)
        cos, sin = _rope_cos_sin(t, HD, X.dtype)
        q = q * cos + _rotate_half(q) * sin
        k = k * cos + _rotate_half(k) * sin
        k = jnp.repeat(k, n_rep, axis=1)
        v = jnp.repeat(v, n_rep, axis=1)
        scale = 256.0 ** (-0.5)
        att = jnp.einsum('bhqd,bhkd->bhqk', q, k) * scale
        att = SOFTCAP * jnp.tanh(att / SOFTCAP)
        causal = jnp.tril(jnp.ones((t, t), dtype=bool))
        att = jnp.where(causal[None, None], att, -jnp.inf)
        att = jax.nn.softmax(att, axis=-1)
        y = jnp.einsum('bhqk,bhkd->bhqd', att, v)
        y = y.transpose(0, 2, 1, 3).reshape(b, t, NH * HD)
        return y @ Wo

    def _L0_ffn_ref(hidden_states, w_norm, w_router, w_gate, w_up, w_down, sw_gate, sw_up, sw_down, w_shared_gate):
        import jax, jax.numpy as jnp
        import numpy as np
        B, S, H = (2, 256, 256)
        E, K, F = (32, 4, 176)
        FS = 704
        EPS = 1e-06
        CAP = 128
        inp = hidden_states
        xf = inp.astype(jnp.float32)
        var = jnp.mean(xf * xf, axis=-1, keepdims=True)
        x = (w_norm * (xf * jax.lax.rsqrt(var + EPS))).astype(inp.dtype)
        Bq, Sq, Hq = x.shape
        x = x.reshape(-1, Hq)
        T = Bq * Sq
        logits = x @ w_router
        probs = jax.nn.softmax(logits.astype(jnp.float32), axis=-1)
        w_topk, sel = jax.lax.top_k(probs, K)
        w_topk = w_topk.astype(x.dtype)
        flat_e = sel.reshape(-1)
        order = jnp.argsort(flat_e)
        sorted_e = flat_e[order]
        counts = jnp.zeros((E,), jnp.int32).at[flat_e].add(1)
        starts = jnp.cumsum(counts) - counts
        pos = jnp.arange(T * K) - starts[sorted_e]
        tok = order // K
        valid = pos < CAP
        dest = jnp.where(valid, pos, CAP)
        buf = jnp.zeros((E, CAP + 1, Hq), x.dtype).at[sorted_e, dest].set(x[tok])
        buf = buf[:, :CAP]
        g = jnp.einsum('ech,ehf->ecf', buf, w_gate)
        u = jnp.einsum('ech,ehf->ecf', buf, w_up)
        y = jnp.einsum('ecf,efh->ech', jax.nn.silu(g) * u, w_down)
        wv = w_topk.reshape(-1)[order] * valid.astype(x.dtype)
        gath = y[sorted_e, jnp.minimum(pos, CAP - 1)]
        out = jnp.zeros((T, Hq), x.dtype).at[tok].add(gath * wv[:, None])
        sh = jax.nn.silu(x @ sw_gate) * (x @ sw_up) @ sw_down
        sh = jax.nn.sigmoid(x @ w_shared_gate) * sh
        out = out + sh
        return inp + out.reshape(Bq, Sq, Hq)
    x = L0_attn_X
    x = x + 0.5 * _L0_ffn_ref(_layernorm(x, axis=-1), L0_ffn_w_norm, L0_ffn_w_router, L0_ffn_w_gate, L0_ffn_w_up, L0_ffn_w_down, L0_ffn_sw_gate, L0_ffn_sw_up, L0_ffn_sw_down, L0_ffn_w_shared_gate)
    x = x + _L0_attn_ref(_layernorm(x, axis=-1), L0_attn_Wq, L0_attn_Wk, L0_attn_Wv, L0_attn_Wo)
    x = x + 0.5 * _L0_ffn_ref(_layernorm(x, axis=-1), L0_ffn_w_norm, L0_ffn_w_router, L0_ffn_w_gate, L0_ffn_w_up, L0_ffn_w_down, L0_ffn_sw_gate, L0_ffn_sw_up, L0_ffn_sw_down, L0_ffn_w_shared_gate)
    return x

_drawn_inputs = setup_inputs


def setup_inputs(seed=0):
    import zlib

    import numpy as np

    out = dict(_drawn_inputs(seed))
    spreads = {}
    factors = {'L0_attn_Wq': 8.0,
     'L0_attn_Wk': 8.0,
     'L0_attn_Wv': 3.769,
     'L0_attn_Wo': 3.772,
     'L0_ffn_w_norm': 8.0,
     'L0_ffn_w_router': 8.0,
     'L0_ffn_w_gate': 8.0,
     'L0_ffn_w_up': 8.0,
     'L0_ffn_w_down': 8.0,
     'L0_ffn_sw_gate': 6.956,
     'L0_ffn_sw_up': 6.87,
     'L0_ffn_sw_down': 6.856,
     'L0_ffn_w_shared_gate': 8.0}
    for name, (base, spread) in spreads.items():
        noise = np.random.default_rng([zlib.crc32(name.encode()), seed]).standard_normal(out[name].shape)
        drawn = base * np.exp(spread * noise) if base else spread * noise
        out[name] = jnp.asarray(drawn.astype(out[name].dtype))
    for name, factor in factors.items():
        out[name] = (out[name] * factor).astype(out[name].dtype)
    return out
```

```python
from contextlib import ExitStack

import numpy as np

import concourse.bass as bass
from concourse import mybir

P = 128
F32 = mybir.dt.float32
F32R = mybir.dt.float32r
BF16 = mybir.dt.bfloat16
I32 = mybir.dt.int32
U32 = mybir.dt.uint32
ALU = mybir.AluOpType
ACT = mybir.ActivationFunctionType
AX = mybir.AxisListType

SEQS, SEQ, C = 16, 256, 256
T = SEQS * SEQ
KC = C // P
HEADS, KV_HEADS, HD = 16, 8, 32
REP = HEADS // KV_HEADS
E, TOPK, FE = 32, 4, 176
FS = 704
CAP = 128
LN_EPS, RMS_EPS = 1e-5, 1e-6
BLK = 512
NB = T // BLK
TJ = BLK // P
MT = 6
LAST = FS - 5 * P
GU = 2 * MT - 1
RW = E + 2
PAD = P
NO_SLOT = float(2 * E * CAP)
UNDERFLOW = -104.0
SOFTCAP = 50.0
QK_SCALE = 256.0 ** -0.5
FD = FE // 2


class Memory:
    pass


CREDIT = 1


def at_least(engine, sem, value, credit=0):
    if isinstance(value, int) and value <= 0:
        return
    engine.wait_ge(sem, value + credit)


def give_credit(engine, *sems):
    for sem in sems:
        engine.sem_inc(sem, CREDIT)


def wait_apart(engine, sem, value, marks):
    engine.wait_ge(sem, value)
    engine.sem_inc(marks, 1)


def split_matmul(nc, out, w_hi, w_lo, x_hi, x_lo, first, last):
    nc.tensor.matmul(out, w_hi, x_hi, start=first, stop=False)
    nc.tensor.matmul(out, w_lo, x_hi, start=False, stop=False)
    return nc.tensor.matmul(out, w_hi, x_lo, start=False, stop=last)


def setup(nc, m, ins):
    ctx = ExitStack()
    with ctx:
        def sb(name, shape, dt):
            return ctx.enter_context(nc.sbuf_tensor(name, shape, dt))

        raw_gate = sb("raw_gate", [P, KC, FS], F32)
        raw_up = sb("raw_up", [P, KC, FS], F32)
        raw_down = sb("raw_down", [P, MT, C], F32)
        raw_q = sb("raw_q", [P, KC, HEADS * HD], F32)
        raw_k = sb("raw_k", [P, KC, KV_HEADS * HD], F32)
        raw_v = sb("raw_v", [P, KC, KV_HEADS * HD], F32)
        raw_o = sb("raw_o", [P, 4, C], F32)
        raw_router = sb("raw_router", [P, KC, RW], F32)
        zeros = sb("zeros", [P, C], F32)
        empty = sb("empty", [P, E, 2], I32)
        iota_i = sb("iota_i", [P, E], I32)
        tok_i = sb("tok_i", [P, TJ * TOPK], I32)
        loaded = ctx.enter_context(nc.semaphore("setup_loaded"))
        pool_made = ctx.enter_context(nc.semaphore("setup_pool_made"))
        padded = ctx.enter_context(nc.semaphore("setup_padded"))
        cleared = ctx.enter_context(nc.semaphore("setup_cleared"))
        hi_made = ctx.enter_context(nc.semaphore("setup_hi_made"))
        lo_made = ctx.enter_context(nc.semaphore("setup_lo_made"))

        g, u = raw_gate[:], raw_up[:]
        splits = []
        for c in range(GU):
            mt = c // 2
            if mt < MT - 1:
                src = (g, u)[c % 2][:, :, mt * P:(mt + 1) * P]
                splits.append((m.gu_hi[:, :, c, :], m.gu_lo[:, :, c, :], src))
            else:
                for half, src in enumerate((g, u)):
                    at = slice(half * LAST, (half + 1) * LAST)
                    splits.append((m.gu_hi[:, :, c, at], m.gu_lo[:, :, c, at], src[:, :, mt * P:FS]))
        splits.append((m.down_hi[:, 0:MT - 1, :], m.down_lo[:, 0:MT - 1, :], raw_down[:, 0:MT - 1, :]))
        splits.append((m.down_hi[0:LAST, MT - 1, :], m.down_lo[0:LAST, MT - 1, :], raw_down[0:LAST, MT - 1, :]))
        splits.append((m.router_hi[:], m.router_lo[:], raw_router[:]))
        for k in range(KC):
            for group in range(2):
                for r in range(REP):
                    q = raw_q[:, k, :].rearrange("p (g j r d) -> p g r j d", g=2, r=REP, d=HD)[:, group, r]
                    n = REP * group + r
                    hi = m.qk_hi[:, k, n, :].rearrange("p (j d) -> p j d", d=HD)
                    lo = m.qk_lo[:, k, n, :].rearrange("p (j d) -> p j d", d=HD)
                    splits.append((hi, lo, q))
            kk = raw_k[:, k, :].rearrange("p (n c) -> p n c", n=2)
            splits.append((m.qk_hi[:, k, 4:6, :], m.qk_lo[:, k, 4:6, :], kk))
        splits.append((m.v_hi[:], m.v_lo[:], raw_v[:]))
        splits.append((m.o_hi[:], m.o_lo[:], raw_o[:]))

        with nc.Block() as block:
            @block.sync
            def _(sp):
                loads = [
                    (raw_gate[:], ins["sw_gate"].rearrange("(k p) f -> p k f", p=P)),
                    (raw_up[:], ins["sw_up"].rearrange("(k p) f -> p k f", p=P)),
                    (raw_down[:, 0:MT - 1, :], ins["sw_down"][0:(MT - 1) * P, :].rearrange("(c p) n -> p c n", p=P)),
                    (raw_down[0:LAST, MT - 1, :], ins["sw_down"][(MT - 1) * P:FS, :]),
                    (raw_q[:], ins["Wq"].rearrange("(k p) n -> p k n", p=P)),
                    (raw_k[:], ins["Wk"].rearrange("(k p) n -> p k n", p=P)),
                    (raw_v[:], ins["Wv"].rearrange("(k p) n -> p k n", p=P)),
                    (m.cos[:], ins["cos"]),
                    (m.sin[:], ins["sin"]),
                ]
                for k in range(KC):
                    loads.append((m.w_norm[:, k:k + 1], ins["w_norm"][k * P:(k + 1) * P].rearrange("(p a) -> p a", a=1)))
                wo = ins["Wo"].rearrange("(g j r d) n -> g r j d n", g=2, r=REP, d=HD)
                for group in range(2):
                    for r in range(REP):
                        for j in range(4):
                            loads.append((raw_o[j * HD:(j + 1) * HD, REP * group + r, :], wo[group, r, j]))
                for dst, src in loads:
                    sp.dma_start(dst, src, allow_slow_non_contiguous=True).then_inc(loaded, 16)
                sp.wait_ge(padded, 1)
                sp.dma_start(raw_router[:, :, 0:E], ins["w_router"].rearrange("(k p) n -> p k n", p=P)).then_inc(loaded, 16)
                sp.dma_start(raw_router[:, :, E:E + 1], ins["w_sgate"].rearrange("(k p) n -> p k n", p=P),
                             allow_slow_non_contiguous=True).then_inc(loaded, 16)
                m.n_loads = len(loads) + 2
                sp.wait_ge(pool_made, 3)
                for rows in (m.z_rows, m.acc1, m.acc2):
                    sp.dma_start(rows[T:T + PAD, :], zeros[:]).then_inc(cleared, 16)
                for table in (m.table1, m.table2):
                    sp.dma_start(table.rearrange("(c e) w -> c e w", e=E), empty[:]).then_inc(cleared, 16)
                sp.wait_ge(cleared, 5 * 16)

            @block.gpsimd
            def _(pool):
                pool.memset(raw_router[:], 0.0).then_inc(padded, 1)
                pool.memset(zeros[:], 0.0).then_inc(pool_made, 1)
                pool.iota(empty[:, :, 0], [[0, E]], base=T, channel_multiplier=1).then_inc(pool_made, 1)
                pool.memset(empty[:, :, 1], 0).then_inc(pool_made, 1)
                pool.iota(iota_i[:], [[1, E]], base=0, channel_multiplier=0).then_inc(pool_made, 1)
                pool.iota(tok_i[:].rearrange("p (j k) -> p j k", k=TOPK), [[P, TJ], [0, TOPK]], base=0,
                          channel_multiplier=1).then_inc(pool_made, 1)
                pool.memset(m.ident[:], 0.0).then_inc(pool_made, 1)
                pool.memset(m.before[:], 1.0).then_inc(pool_made, 1)
                pool.memset(m.ones_b[:], 1.0).then_inc(pool_made, 1)
                pool.memset(m.ones_f[:], 1.0).then_inc(pool_made, 1)
                pool.memset(m.neg_half[:], -0.5).then_inc(pool_made, 1)
                pool.wait_ge(pool_made, 7)
                pool.affine_select(out=m.ident[:], in_=m.ident[:], compare_op=ALU.not_equal, fill=1.0, base=0,
                                   pattern=[[-1, P]], channel_multiplier=1).then_inc(pool_made, 1)
                pool.affine_select(out=m.before[:], in_=m.before[:], compare_op=ALU.is_gt, fill=0.0, base=0,
                                   pattern=[[1, P]], channel_multiplier=-1).then_inc(pool_made, 1)

            @block.scalar
            def _(act):
                act.wait_ge(loaded, 16 * m.n_loads)
                for hi, lo, raw in splits:
                    act.copy(hi, raw).then_inc(hi_made, 1)

            @block.vector
            def _(dve):
                dve.wait_ge(pool_made, 5)
                dve.tensor_copy(m.iota_e[:], iota_i[:])
                for n in range(2):
                    dve.tensor_copy(m.tok_f[:, n, :], tok_i[:])
                dve.wait_ge(loaded, 16 * m.n_loads)
                for n, (hi, lo, raw) in enumerate(splits):
                    dve.wait_ge(hi_made, n + 1)
                    dve.tensor_tensor(lo, raw, hi.bitcast(F32), ALU.subtract)


def route_and_shared(nc, m, tag, src, acc, table):
    ctx = ExitStack()
    with ctx:
        def sb(name, shape, dt):
            return ctx.enter_context(nc.sbuf_tensor(f"{name}_{tag}", shape, dt))

        def psum(name, shape):
            return ctx.enter_context(nc.psum_tensor(f"{name}_{tag}", shape, F32))

        def sem(name):
            return ctx.enter_context(nc.semaphore(f"{name}_{tag}"))

        x = sb("x", [P, 2, TJ, C], F32)
        h = sb("h", [P, TJ, C], F32)
        z = sb("z", [P, 2, TJ, C], F32)
        base = sb("base", [P, 2, TJ, C], F32)
        x_hi = sb("x_hi", [P, 2, KC, BLK], F32R)
        x_lo = sb("x_lo", [P, 2, KC, BLK], F32R)
        stats = sb("stats", [P, TJ, 6], F32)
        moments = sb("moments", [P, 2, TJ, 2], F32)
        var_in = sb("var_in", [P, 2, 2, TJ], F32)
        rstd = sb("rstd", [P, 2, 2, TJ], F32)
        row_max = sb("row_max", [P, TJ], F32)
        d = sb("d", [P, TJ, E], F32)
        top = sb("top", [P, TJ, 8], F32)
        top_at = sb("top_at", [P, TJ, 8], U32)
        top_f = sb("top_f", [P, TJ, TOPK], F32)
        chosen = sb("chosen", [P, TJ * TOPK, E], F32)
        mask = sb("mask", [P, TJ, E], BF16)
        mask_sum = sb("mask_sum", [P, E], F32)
        seen = sb("seen", [P, E], BF16)
        exps = sb("exps", [P, TJ, E], F32)
        exp_top = sb("exp_top", [P, TJ, 8], F32)
        gate_in = sb("gate_in", [P, TJ], F32)
        exp_gate = sb("exp_gate", [P, TJ], F32)
        total = sb("total", [P, TJ], F32)
        inv_total = sb("inv_total", [P, TJ], F32)
        gate_den = sb("gate_den", [P, TJ], F32)
        half_gate = sb("half_gate", [P, 2, TJ], F32)
        past = sb("past", [P, TJ, E], F32)
        place = sb("place", [P, TJ, E], F32)
        place_all = sb("place_all", [P, TJ, E], F32)
        picked = sb("picked", [P, TJ * TOPK, E], F32)
        slot_f = sb("slot_f", [P, TJ * TOPK], F32)
        slot = sb("slot", [P, 2, TJ * TOPK], I32)
        entry = sb("entry", [P, 2, TJ * TOPK, 2], I32)
        silu = sb("silu", [P, 2, BLK], F32)
        act_gu = sb("act_gu", [P, 2, BLK], F32)
        a_hi = sb("a_hi", [P, MT, BLK], F32R)
        a_lo = sb("a_lo", [P, MT, BLK], F32R)

        zT = [psum(f"zT{k}", [P, BLK]) for k in range(KC)]
        small = psum("small", [P, BLK])
        logits = small[:, 0:TJ * RW].rearrange("p (j e) -> p j e", e=RW)
        pos = small[:, 256:256 + TJ * E].rearrange("p (j e) -> p j e", e=E)
        gu = [psum(f"gu{n}", [P, BLK]) for n in range(3)]
        down = [psum(f"down{n}", [P, 2, C]) for n in range(2)]

        x_loaded = [sem("x_loaded0"), sem("x_loaded1")]
        stat = sem("stat")
        marks = sem("marks")
        pool_marks = sem("pool_marks")
        vars_ready = sem("vars_ready")
        rstd_ready = sem("rstd_ready")
        h_ready = sem("h_ready")
        base_ready = sem("base_ready")
        z_ready = sem("z_ready")
        z_stored = [sem("z_stored0"), sem("z_stored1")]
        zT_ready = sem("zT_ready")
        hi_ready = sem("hi_ready")
        lo_ready = sem("lo_ready")
        logits_ready = sem("logits_ready")
        d_ready = sem("d_ready")
        top_ready = sem("top_ready")
        mask_ready = sem("mask_ready")
        exps_ready = sem("exps_ready")
        pos_ready = sem("pos_ready")
        pos_used = sem("pos_used")
        entry_ready = sem("entry_ready")
        gates_ready = sem("gates_ready")
        scattered = [sem("scattered0"), sem("scattered1")]
        gu_ready = sem("gu_ready")
        silu_ready = sem("silu_ready")
        prod_ready = sem("prod_ready")
        a_hi_ready = sem("a_hi_ready")
        a_lo_ready = sem("a_lo_ready")
        down_ready = sem("down_ready")
        out_ready = sem("out_ready")
        out_stored = [sem("out_stored0"), sem("out_stored1")]
        base_free = sem("base_free")

        def rows(b):
            return bass.ds(b * BLK, BLK)

        block = ctx.enter_context(nc.Block())

        @block.sync
        def _(sp):
            def load(b, q):
                at_least(sp, base_ready, TJ * (b - 1))
                sp.dma_start(x[:, q], src[rows(b), :].rearrange("(j p) c -> p j c", p=P)).then_inc(x_loaded[q], 16)

            def z_has_been_stored(q, n):
                sp.wait_ge(z_stored[q], 16 * n)

            def free_base(q, n):
                sp.wait_ge(out_stored[q], 16 * n)
                sp.sem_inc(base_free, 1)

            def store_z(b, q):
                sp.wait_ge(z_ready, TJ * (b + 1))
                sp.dma_start(m.z_rows[rows(b), :].rearrange("(j p) c -> p j c", p=P), z[:, q]).then_inc(z_stored[q], 16)

            def store_out(b, q):
                sp.wait_ge(out_ready, CREDIT + TJ * (b + 1))
                sp.dma_start(acc[rows(b), :].rearrange("(j p) c -> p j c", p=P), base[:, q]).then_inc(out_stored[q], 16)

            give_credit(sp, base_free)
            load(0, 0)
            load(1, 1)
            store_z(0, 0)
            with sp.Fori(0, NB // 2 - 1) as i:
                for q in range(2):
                    b = i * 2 + q
                    z_has_been_stored(q, i + 1)
                    load(b + 2, q)
                    store_z(b + 1, 1 - q)
                    store_out(b, q)
                    free_base(q, i + 1)
            store_z(NB - 1, 1)
            store_out(NB - 2, 0)
            store_out(NB - 1, 1)
            for q in range(2):
                sp.wait_ge(z_stored[q], 16 * (NB // 2))
                sp.wait_ge(out_stored[q], 16 * (NB // 2))

        @block.gpsimd
        def _(pool):
            def roots(b, q, n=0):
                at_least(pool, scattered[q], 16 * TJ * TOPK * n)
                pool.wait_ge(vars_ready, b + 1)
                pool.tensor_tensor(rstd[:, q], var_in[:, q], m.neg_half[:], ALU.pow).then_inc(rstd_ready, 1)

            def scatter(b, q):
                wait_apart(pool, entry_ready, b + 1, pool_marks)
                for n in range(TJ * TOPK):
                    pool.indirect_dma_start(
                        out=table, out_offset=bass.IndirectOffsetOnAxis(ap=slot[:, q, n:n + 1], axis=0),
                        in_=entry[:, q, n, :], in_offset=None, bounds_check=last_slot, oob_is_err=False,
                    ).then_inc(scattered[q], 16)

            last_slot = pool.to_reg(E * CAP - 1)
            roots(0, 0)
            roots(1, 1)
            scatter(0, 0)
            with pool.Fori(0, NB // 2 - 1) as i:
                for q in range(2):
                    b = i * 2 + q
                    roots(b + 2, q, i + 1)
                    scatter(b + 1, 1 - q)
            scatter(NB - 1, 1)
            for q in range(2):
                pool.wait_ge(scattered[q], 16 * TJ * TOPK * (NB // 2))

        @block.tensor
        def _(pe):
            def transposes(b, q):
                pe.wait_ge(z_ready, TJ * (b + 1))
                at_least(pe, lo_ready, KC * b)
                for k in range(KC):
                    for j in range(TJ):
                        last = nc.tensor.transpose(zT[k][:, j * P:(j + 1) * P], z[:, q, j, k * P:(k + 1) * P], m.ident[:])
                    last.then_inc(zT_ready, 1)

            def router(b, q):
                pe.wait_ge(lo_ready, KC * (b + 1))
                at_least(pe, pos_used, b)
                for j in range(TJ):
                    for k in range(KC):
                        at = slice(j * P, (j + 1) * P)
                        last = split_matmul(nc, logits[:, j, :], x_hi[:, q, k, at], x_lo[:, q, k, at],
                                            m.router_hi[:, k, :], m.router_lo[:, k, :], k == 0, k == KC - 1)
                last.then_inc(logits_ready, 1)

            def positions(b):
                pe.wait_ge(mask_ready, b + 1)
                for j in range(TJ):
                    nc.tensor.matmul(pos[:, j, :], m.before[:], mask[:, j, :], start=True, stop=False)
                    for i in range(j):
                        nc.tensor.matmul(pos[:, j, :], m.ones_b[:], mask[:, i, :], start=False, stop=False)
                    last = nc.tensor.matmul(pos[:, j, :], m.ones_b[:], seen[:], start=False, stop=True)
                last.then_inc(pos_ready, 1)

            def gate_up(b, q, c):
                if c < 3:
                    at_least(pe, prod_ready, MT * b, CREDIT)
                elif c % 2:
                    pe.wait_ge(silu_ready, b * MT + (c - 3) // 2 + 1)
                else:
                    pe.wait_ge(prod_ready, CREDIT + b * MT + (c - 3) // 2 + 1)
                for k in range(KC):
                    last = split_matmul(nc, gu[c % 3][:], m.gu_hi[:, k, c, :], m.gu_lo[:, k, c, :],
                                        x_hi[:, q, k, :], x_lo[:, q, k, :], k == 0, k == KC - 1)
                last.then_inc(gu_ready, 1)

            def down_proj(b, j):
                at_least(pe, out_ready, TJ * b, CREDIT)
                for mt in range(MT):
                    if j == 0:
                        pe.wait_ge(a_lo_ready, CREDIT + b * MT + mt + 1)
                    rows_ = slice(0, P if mt < MT - 1 else LAST)
                    at = slice(j * P, (j + 1) * P)
                    last = split_matmul(nc, down[j // 2][:, j % 2, :], a_hi[rows_, mt, at], a_lo[rows_, mt, at],
                                        m.down_hi[rows_, mt, :], m.down_lo[rows_, mt, :], mt == 0, mt == MT - 1)
                last.then_inc(down_ready, 1)

            def slot_of(b, q, ahead):
                for c in range(GU):
                    gate_up(b, q, c)
                    if ahead and c == 3:
                        transposes(b + 1, 1 - q)
                    if ahead and c == 6:
                        router(b + 1, 1 - q)
                for j in range(TJ):
                    down_proj(b, j)
                    if ahead and j == 1:
                        positions(b + 1)

            give_credit(pe, zT_ready, gu_ready, down_ready)
            transposes(0, 0)
            router(0, 0)
            positions(0)
            with pe.Fori(0, NB // 2 - 1) as i:
                for q in range(2):
                    slot_of(i * 2 + q, q, True)
            slot_of(NB - 2, 0, True)
            slot_of(NB - 1, 1, False)

        @block.scalar
        def _(act):
            def scale_z(b, q):
                for j in range(TJ):
                    act.wait_ge(h_ready, b * TJ + j + 1)
                    if j == 0:
                        at_least(act, zT_ready, KC * (b - 1), CREDIT)
                    nc.scalar.activation(z[:, q, j, :], h[:, j, :], ACT.Copy, scale=rstd[:, q, 1, j:j + 1]).then_inc(z_ready, 1)

            def x_hi_parts(b, q):
                for k in range(KC):
                    act.wait_ge(zT_ready, CREDIT + b * KC + k + 1)
                    if k == 0:
                        at_least(act, gu_ready, GU * (b - 1), CREDIT)
                    nc.scalar.activation(x_hi[:, q, k, :], zT[k][:], ACT.Copy, scale=m.w_norm[:, k:k + 1]).then_inc(hi_ready, 1)

            def silu_of(b, mt):
                act.wait_ge(gu_ready, CREDIT + b * GU + 2 * mt + 1)
                at_least(act, prod_ready, b * MT + max(mt - 1, 0), CREDIT)
                c = 2 * mt
                if mt < MT - 1:
                    nc.scalar.activation(silu[:, mt % 2, :], gu[c % 3][:], ACT.Silu).then_inc(silu_ready, 1)
                else:
                    nc.scalar.activation(silu[LAST:P, mt % 2, :], gu[c % 3][0:LAST, :], ACT.Silu).then_inc(silu_ready, 1)

            def a_hi_part(b, mt):
                act.wait_ge(prod_ready, CREDIT + b * MT + mt + 1)
                at_least(act, down_ready, TJ * b, CREDIT)
                r = slice(0, P if mt < MT - 1 else LAST)
                nc.scalar.copy(a_hi[r, mt, :], act_gu[r, mt % 2, :]).then_inc(a_hi_ready, 1)

            def exponentials(b):
                act.wait_ge(top_ready, b + 1)
                at_least(act, entry_ready, b)
                nc.scalar.activation(exps[:], d[:], ACT.Exp).then_inc(exps_ready, 1)
                nc.scalar.activation(exp_top[:], top[:], ACT.Exp).then_inc(exps_ready, 1)
                nc.scalar.activation(exp_gate[:], gate_in[:], ACT.Exp, scale=-1.0).then_inc(exps_ready, 1)

            def slot_of(b, q, ahead):
                if ahead:
                    scale_z(b + 1, 1 - q)
                silu_of(b, 0)
                for mt in range(1, MT):
                    silu_of(b, mt)
                    a_hi_part(b, mt - 1)
                    if ahead and mt == 1:
                        x_hi_parts(b + 1, 1 - q)
                a_hi_part(b, MT - 1)
                if ahead:
                    exponentials(b + 1)

            give_credit(act, a_hi_ready)
            scale_z(0, 0)
            x_hi_parts(0, 0)
            exponentials(0)
            with act.Fori(0, NB // 2 - 1) as i:
                for q in range(2):
                    slot_of(i * 2 + q, q, True)
            slot_of(NB - 2, 0, True)
            slot_of(NB - 1, 1, False)

        @block.vector
        def _(dve):
            count = [0]

            class Chain:
                start = 0

            def step(ins, apart=False):
                ins.then_inc(stat, 1)
                count[0] += 1
                if apart:
                    wait_apart(dve, stat, Chain.start + count[0], marks)
                else:
                    dve.wait_ge(stat, Chain.start + count[0])

            def statistics(b, q, n):
                dve.wait_ge(x_loaded[q], 16 * (n + 1))
                for j in range(TJ):
                    ins = dve.bn_stats(stats[:, j, :], x[:, q, j, :])
                step(ins, apart=True)
                for j in range(TJ):
                    ins = dve.bn_aggr(moments[:, q, j, :], stats[:, j, :])
                step(ins)
                var = moments[:, q, :, 1]
                step(dve.tensor_scalar(var_in[:, q, 0, :], var, LN_EPS, None, ALU.add))
                step(dve.reciprocal(var_in[:, q, 1, :], var_in[:, q, 0, :]))
                step(dve.tensor_tensor(var_in[:, q, 1, :], var_in[:, q, 1, :], var, ALU.mult))
                dve.tensor_scalar(var_in[:, q, 1, :], var_in[:, q, 1, :], RMS_EPS, None, ALU.add).then_inc(vars_ready, 1)

            def normalise(b, q):
                dve.wait_ge(rstd_ready, b + 1)
                at_least(dve, z_ready, TJ * b)
                for j in range(TJ):
                    dve.tensor_scalar(h[:, j, :], x[:, q, j, :], moments[:, q, j, 0:1], rstd[:, q, 0, j:j + 1],
                                      ALU.subtract, ALU.mult).then_inc(h_ready, 1)
                at_least(dve, base_free, b - 1, CREDIT)
                dve.wait_ge(h_ready, TJ * (b + 1))
                for j in range(TJ):
                    dve.scalar_tensor_tensor(out=base[:, q, j, :], in0=h[:, j, :], scalar=0.5, in1=x[:, q, j, :],
                                             op0=ALU.mult, op1=ALU.add).then_inc(base_ready, 1)

            def x_lo_parts(b, q):
                for k in range(KC):
                    dve.wait_ge(hi_ready, b * KC + k + 1)
                    dve.scalar_tensor_tensor(out=x_lo[:, q, k, :], in0=zT[k][:], scalar=m.w_norm[:, k:k + 1],
                                             in1=x_hi[:, q, k, :].bitcast(F32), op0=ALU.mult,
                                             op1=ALU.subtract).then_inc(lo_ready, 1)

            def top_experts(b):
                dve.wait_ge(logits_ready, b + 1)
                at_least(dve, exps_ready, 3 * b)
                dve.tensor_scalar(gate_in[:], logits[:, :, E], -88.0, None, ALU.max)
                step(dve.reduce_max(row_max[:], logits[:, :, 0:E], AX.X))
                for j in range(TJ):
                    ins = dve.tensor_scalar(d[:, j, :], logits[:, j, 0:E], row_max[:, j:j + 1], UNDERFLOW,
                                            ALU.subtract, ALU.max)
                step(ins, apart=True)
                for j in range(TJ):
                    ins = dve.max(top[:, j, :], d[:, j, :])
                step(ins, apart=True)
                for j in range(TJ):
                    ins = dve.max_index(top_at[:, j, :], top[:, j, :], d[:, j, :])
                ins.then_inc(top_ready, 1)

            def masks(b):
                dve.wait_ge(top_ready, b + 1)
                at_least(dve, pos_ready, b)
                step(dve.tensor_copy(top_f[:], top_at[:, :, 0:TOPK]))
                step(dve.tensor_tensor(
                    chosen[:], m.iota_e[:].unsqueeze(1).to_broadcast([P, TJ * TOPK, E]),
                    top_f[:].rearrange("p j k -> p (j k)").unsqueeze(2).to_broadcast([P, TJ * TOPK, E]), ALU.is_equal))
                with nc.allow_low_precision(reason="zeros and ones"):
                    dve.tensor_reduce(mask[:], chosen[:].rearrange("p (j k) e -> p j e k", k=TOPK), AX.X,
                                      ALU.add).then_inc(mask_ready, 1)

            def entries(b, q):
                dve.wait_ge(pos_ready, b + 1)
                step(dve.tensor_reduce(mask_sum[:], mask[:].rearrange("p j e -> p e j"), AX.X, ALU.add))
                with nc.allow_low_precision(reason="integers up to 32"):
                    dve.tensor_tensor(seen[:], seen[:], mask_sum[:], ALU.add)
                dve.tensor_scalar(past[:], pos, float(CAP), NO_SLOT, ALU.is_ge, ALU.mult)
                step(dve.scalar_tensor_tensor(out=place[:], in0=pos, scalar=float(E),
                                              in1=m.iota_e[:].unsqueeze(1).to_broadcast([P, TJ, E]), op0=ALU.mult,
                                              op1=ALU.add))
                step(dve.tensor_tensor(place_all[:], place[:], past[:], ALU.add))
                step(dve.tensor_tensor(
                    picked[:].rearrange("p (j k) e -> p j k e", k=TOPK), chosen[:].rearrange("p (j k) e -> p j k e", k=TOPK),
                    place_all[:].unsqueeze(2).to_broadcast([P, TJ, TOPK, E]), ALU.mult))
                at_least(dve, entry_ready, b)
                step(dve.tensor_reduce(slot_f[:], picked[:], AX.X, ALU.add))
                dve.tensor_copy(slot[:, q, :], slot_f[:])
                dve.tensor_copy(entry[:, q, :, 0], m.tok_f[:, m.turn, :])
                dve.wait_ge(exps_ready, 3 * (b + 1))
                step(dve.reduce_sum(total[:], exps[:], AX.X))
                step(dve.reciprocal(inv_total[:], total[:]))
                dve.scalar_tensor_tensor(
                    out=entry[:, q, :, 1].bitcast(F32).rearrange("p (j k) -> p j k", k=TOPK), in0=exp_top[:, :, 0:TOPK],
                    scalar=0.5, in1=inv_total[:].unsqueeze(2).to_broadcast([P, TJ, TOPK]), op0=ALU.mult, op1=ALU.mult)
                step(dve.tensor_scalar(gate_den[:], exp_gate[:], 2.0, 2.0, ALU.mult, ALU.add))
                dve.reciprocal(half_gate[:, q, :], gate_den[:]).then_inc(pos_used, 1)
                dve.tensor_scalar(m.tok_f[:, m.turn, :], m.tok_f[:, m.turn, :], float(BLK), None, ALU.add
                                  ).then_inc(entry_ready, 1)

            def product(b, mt):
                dve.wait_ge(silu_ready, b * MT + mt + 1)
                dve.wait_ge(gu_ready, CREDIT + b * GU + min(2 * mt + 2, GU))
                at_least(dve, a_hi_ready, b * MT + max(mt - 1, 0), CREDIT)
                at_least(dve, a_lo_ready, b * MT + max(mt - 1, 0), CREDIT)
                if mt < MT - 1:
                    dve.tensor_tensor(act_gu[:, mt % 2, :], silu[:, mt % 2, :], gu[(2 * mt + 1) % 3][:],
                                      ALU.mult).then_inc(prod_ready, 1)
                else:
                    dve.tensor_tensor(act_gu[0:LAST, mt % 2, :], silu[LAST:P, mt % 2, :], gu[(2 * mt) % 3][LAST:P, :],
                                      ALU.mult).then_inc(prod_ready, 1)

            def a_lo_part(b, mt):
                dve.wait_ge(a_hi_ready, CREDIT + b * MT + mt + 1)
                r = slice(0, P if mt < MT - 1 else LAST)
                dve.tensor_tensor(a_lo[r, mt, :], act_gu[r, mt % 2, :], a_hi[r, mt, :].bitcast(F32),
                                  ALU.subtract).then_inc(a_lo_ready, 1)

            def outputs(b, q):
                for j in range(TJ):
                    dve.wait_ge(down_ready, CREDIT + b * TJ + j // 2 * 2 + 2)
                    dve.scalar_tensor_tensor(out=base[:, q, j, :], in0=down[j // 2][:, j % 2, :],
                                             scalar=half_gate[:, q, j:j + 1], in1=base[:, q, j, :], op0=ALU.mult,
                                             op1=ALU.add).then_inc(out_ready, 1)

            def slot_of(b, q, ahead, further, n_after):
                if ahead:
                    normalise(b + 1, 1 - q)
                product(b, 0)
                for mt in range(1, MT):
                    product(b, mt)
                    a_lo_part(b, mt - 1)
                    if ahead and mt == 1:
                        x_lo_parts(b + 1, 1 - q)
                    if ahead and mt == 3:
                        top_experts(b + 1)
                    if ahead and mt == 4:
                        masks(b + 1)
                a_lo_part(b, MT - 1)
                if further:
                    statistics(b + 2, q, n_after)
                if ahead:
                    entries(b + 1, 1 - q)
                outputs(b, q)

            give_credit(dve, prod_ready, out_ready, a_lo_ready)
            step(dve.memset(seen[:], 0.0))
            statistics(0, 0, 0)
            normalise(0, 0)
            statistics(1, 1, 0)
            x_lo_parts(0, 0)
            top_experts(0)
            masks(0)
            entries(0, 0)
            head, count[0] = count[0], 0
            steps = 5 + 3 + 2 + 8
            with dve.Fori(0, NB // 2 - 1) as i:
                for q in range(2):
                    Chain.start = i * (2 * steps) + (head + q * steps)
                    count[0] = 0
                    slot_of(i * 2 + q, q, True, True, i + 1)
                    assert count[0] == steps, count
            Chain.start, count[0] = head + (NB - 2) * steps, 0
            slot_of(NB - 2, 0, True, False, 0)
            slot_of(NB - 1, 1, False, False, 0)


def experts(nc, m, tag, acc, table, ins):
    ctx = ExitStack()
    with ctx:
        def sb(name, shape, dt):
            return ctx.enter_context(nc.sbuf_tensor(f"{name}_{tag}", shape, dt))

        def psum(name, shape):
            return ctx.enter_context(nc.psum_tensor(f"{name}_{tag}", shape, F32))

        def sem(name):
            return ctx.enter_context(nc.semaphore(f"{name}_{tag}"))

        PAIRS = E // 2
        AHEAD = 2
        w_gu = sb("w_gu", [P, AHEAD, 2, KC, 2, FE], F32)
        w_down = sb("w_down", [FD, AHEAD, 2, 2, C], F32)
        slots = sb("slots", [P, E, 2], I32)
        cur = sb("cur", [P, AHEAD, 2, 2], I32)
        rows = sb("rows", [P, AHEAD, 2, C], F32)
        xT = sb("xT", [P, 2, KC, CAP], F32)
        silu = sb("silu_e", [P, 2, FE], F32)
        prod = sb("prod_e", [P, 2, FE], F32)
        prodT = sb("prodT", [FD, 2, 2, CAP], F32)
        y = sb("y", [P, AHEAD, 2, C], F32)
        xT_ps = [psum(f"xT_ps{s}", [P, KC, CAP]) for s in range(2)]
        gu_ps = [psum(f"gu_ps{s}", [P, 2, FE]) for s in range(2)]
        prodT_ps = [psum(f"prodT_ps{s}", [P, 2, CAP]) for s in range(2)]
        y_ps = [psum(f"y_ps{s}", [P, C]) for s in range(2)]

        table_loaded = sem("table_loaded")
        w_loaded = [sem("w_loaded0"), sem("w_loaded1")]
        cur_ready = sem("cur_ready")
        gathered = [sem("gathered0"), sem("gathered1")]
        xT_ready = sem("xT_ready")
        xT_copied = sem("xT_copied")
        gu_done = sem("gu_done")
        silu_done = sem("silu_done")
        prod_done = sem("prod_done")
        prodT_ready = sem("prodT_ready")
        prodT_copied = sem("prodT_copied")
        y_ready = sem("y_ready")
        y_scaled = sem("y_scaled")
        added = sem("added")
        marks = sem("marks")

        block = ctx.enter_context(nc.Block())

        @block.sync
        def _(sp):
            def load(i, q):
                for s in range(2):
                    e = i * (2 * AHEAD) + (2 * q + s)
                    for half, name in enumerate(("w_gate", "w_up")):
                        sp.dma_start(w_gu[:, q, s, :, half, :],
                                     ins[name][bass.ds(e, 1), :, :].rearrange("a (k p) f -> p (a k) f", p=P)
                                     ).then_inc(w_loaded[q], 16)
                    sp.dma_start(w_down[:, q, s, :, :],
                                 ins["w_down"][bass.ds(e, 1), :, :].rearrange("a (k p) n -> p (a k) n", p=FD)
                                 ).then_inc(w_loaded[q], 16)

            sp.dma_start(slots[:], table.rearrange("(c e) w -> c e w", e=E)).then_inc(table_loaded, 16)
            for q in range(AHEAD):
                load(0, q)
            with sp.Fori(1, PAIRS // AHEAD) as i:
                for q in range(AHEAD):
                    sp.wait_ge(y_ready, CREDIT + i * (2 * AHEAD) + (2 * q + 2 - 2 * AHEAD))
                    load(i, q)

        @block.gpsimd
        def _(pool):
            def fetch(i, q, first):
                pair = i * AHEAD + q
                if not first:
                    pool.wait_ge(y_scaled, CREDIT + pair * 2 - 2 * AHEAD + 2)
                pool.tensor_copy(cur[:, q], slots[:, bass.ds(pair * 2, 2), :]).then_inc(cur_ready, 1)
                if not first:
                    pool.wait_ge(xT_ready, CREDIT + pair * 2 - 2 * AHEAD + 2)
                wait_apart(pool, cur_ready, pair + 1, marks)
                for s in range(2):
                    pool.indirect_dma_start(
                        out=rows[:, q, s, :], out_offset=None, in_=m.z_rows,
                        in_offset=bass.IndirectOffsetOnAxis(ap=cur[:, q, s, 0:1], axis=0),
                        bounds_check=last_row, oob_is_err=False).then_inc(gathered[q], 16)

            def add(i, q):
                for s in range(2):
                    n = i * (2 * AHEAD) + (2 * q + s)
                    if s or isinstance(n, int):
                        at_least(pool, added, n * 16)
                    wait_apart(pool, y_scaled, CREDIT + n + 1, marks)
                    pool.indirect_dma_start(
                        out=acc, out_offset=bass.IndirectOffsetOnAxis(ap=cur[:, q, s, 0:1], axis=0),
                        in_=y[:, q, s, :], in_offset=None, compute_op=ALU.add,
                        bounds_check=last_row, oob_is_err=True).then_inc(added, 16)

            last_row = pool.to_reg(T + PAD - 1)
            pool.wait_ge(table_loaded, 16)
            for q in range(AHEAD):
                fetch(0, q, True)
            with pool.Fori(0, PAIRS // AHEAD - 1) as i:
                for q in range(AHEAD):
                    add(i, q)
                    pool.wait_ge(added, i * (32 * AHEAD) + 32 * (q + 1))
                    fetch(i + 1, q, False)
            for q in range(AHEAD):
                add(PAIRS // AHEAD - 1, q)
            pool.wait_ge(added, 16 * E)

        @block.tensor
        def _(pe):
            give_credit(pe, xT_ready, gu_done, prodT_ready, y_ready)
            with pe.Fori(0, PAIRS // AHEAD) as i:
                for q in range(AHEAD):
                    n0 = i * (2 * AHEAD) + 2 * q
                    pe.wait_ge(gathered[q], i * 32 + 32)
                    pe.wait_ge(xT_copied, CREDIT + n0)
                    for s in range(2):
                        for k in range(KC):
                            last = nc.tensor.transpose(xT_ps[s][:, k, :], rows[:, q, s, k * P:(k + 1) * P], m.ident[:])
                        last.then_inc(xT_ready, 1)
                    pe.wait_ge(w_loaded[q], i * 96 + 96)
                    pe.wait_ge(prod_done, CREDIT + n0)
                    for s in range(2):
                        pe.wait_ge(xT_copied, CREDIT + n0 + (s + 1))
                        for k in range(KC):
                            last = nc.tensor.matmul(gu_ps[s][:].rearrange("p a f -> p (a f)"), xT[:, s, k, :],
                                                    w_gu[:, q, s, k, :, :].rearrange("p a f -> p (a f)"),
                                                    start=k == 0, stop=k == KC - 1)
                        last.then_inc(gu_done, 1)
                    for s in range(2):
                        pe.wait_ge(prod_done, CREDIT + n0 + (s + 1))
                        pe.wait_ge(prodT_copied, CREDIT + n0)
                        for k in range(2):
                            last = nc.tensor.transpose(prodT_ps[s][0:FD, k, :], prod[:, s, k * FD:(k + 1) * FD], m.ident[:])
                        last.then_inc(prodT_ready, 1)
                    for s in range(2):
                        pe.wait_ge(prodT_copied, CREDIT + n0 + (s + 1))
                        pe.wait_ge(y_scaled, CREDIT + n0)
                        for k in range(2):
                            last = nc.tensor.matmul(y_ps[s][:], prodT[:, s, k, :], w_down[:, q, s, k, :], start=k == 0,
                                                    stop=k == 1)
                        last.then_inc(y_ready, 1)

        @block.scalar
        def _(act):
            give_credit(act, y_scaled)
            with act.Fori(0, PAIRS // AHEAD) as i:
                for q in range(AHEAD):
                    n0 = i * (2 * AHEAD) + 2 * q
                    for s in range(2):
                        act.wait_ge(gu_done, CREDIT + n0 + (s + 1))
                        act.wait_ge(prod_done, CREDIT + n0)
                        nc.scalar.activation(silu[:, s, :], gu_ps[s][:, 0, :], ACT.Silu).then_inc(silu_done, 1)
                    for s in range(2):
                        act.wait_ge(y_ready, CREDIT + n0 + (s + 1))
                        act.wait_ge(cur_ready, i * AHEAD + (q + 1))
                        nc.scalar.activation(y[:, q, s, :], y_ps[s][:], ACT.Copy,
                                             scale=cur[:, q, s, 1:2].bitcast(F32)).then_inc(y_scaled, 1)

        @block.vector
        def _(dve):
            give_credit(dve, xT_copied, prod_done, prodT_copied)
            with dve.Fori(0, PAIRS // AHEAD) as i:
                for q in range(AHEAD):
                    n0 = i * (2 * AHEAD) + 2 * q
                    for s in range(2):
                        dve.wait_ge(xT_ready, CREDIT + n0 + (s + 1))
                        dve.wait_ge(gu_done, CREDIT + n0)
                        for k in range(KC):
                            ins_ = dve.tensor_scalar(xT[:, s, k, :], xT_ps[s][:, k, :], m.w_norm[:, k:k + 1], None, ALU.mult)
                        ins_.then_inc(xT_copied, 1)
                    for s in range(2):
                        dve.wait_ge(silu_done, n0 + (s + 1))
                        dve.wait_ge(prodT_ready, CREDIT + n0)
                        dve.tensor_tensor(prod[:, s, :], silu[:, s, :], gu_ps[s][:, 1, :], ALU.mult).then_inc(prod_done, 1)
                    for s in range(2):
                        dve.wait_ge(prodT_ready, CREDIT + n0 + (s + 1))
                        dve.wait_ge(y_ready, CREDIT + n0)
                        dve.tensor_copy(prodT[:, s], prodT_ps[s][0:FD]).then_inc(prodT_copied, 1)


def attention(nc, m, src, dst):
    ctx = ExitStack()
    with ctx:
        def sb(name, shape, dt):
            return ctx.enter_context(nc.sbuf_tensor(f"{name}_at", shape, dt))

        def psum(name, shape):
            return ctx.enter_context(nc.psum_tensor(f"{name}_at", shape, F32))

        def sem(name):
            return ctx.enter_context(nc.semaphore(f"{name}_at"))

        QT = SEQ // P
        GROUPS = 2
        UNITS = GROUPS * QT
        PIECES = 3
        JH = 4
        W = REP * SEQ

        xn = sb("xn", [P, 2, QT, C], F32)
        xr = sb("xr", [P, 2, QT, C], F32)
        a = sb("a", [P, QT, C], F32)
        stats = sb("stats", [P, QT, 6], F32)
        moments = sb("moments", [P, QT, 2], F32)
        var_in = sb("var_in", [P, QT], F32)
        rstd = sb("rstd", [P, QT], F32)
        aT_hi = sb("aT_hi", [P, KC, SEQ], F32R)
        aT_lo = sb("aT_lo", [P, KC, SEQ], F32R)
        turned = sb("turned", [P, PIECES, 2, SEQ], F32)
        by_cos = sb("by_cos", [P, PIECES, 2, SEQ], F32)
        by_sin = sb("by_sin", [P, PIECES, 2, SEQ], F32)
        roped = sb("roped", [P, PIECES, 2, SEQ], F32)
        qk_hi = sb("qkT_hi", [P, 2, 6, SEQ], F32R)
        qk_lo = sb("qkT_lo", [P, 2, 6, SEQ], F32R)
        v = sb("v", [P, 2, QT, C], F32)
        capped = sb("capped", [P, 2, JH, W], F32)
        probs = sb("probs", [P, 2, JH, W], F32)
        inv_den = sb("inv_den", [P, W], F32)
        y = sb("y", [P, W], F32)
        y_hi = sb("y_hi", [P, GROUPS, W], F32R)
        y_lo = sb("y_lo", [P, GROUPS, W], F32R)

        scores = psum("scores", [P, JH, W])
        pv = psum("pv", [P, W])
        den = psum("den", [P, W])
        pj = [psum(f"pj{n}", [P, 2, SEQ]) for n in range(2)]

        xn_loaded = [sem("xn_loaded0"), sem("xn_loaded1")]
        xr_loaded = [sem("xr_loaded0"), sem("xr_loaded1")]
        stored = [sem("stored0"), sem("stored1")]
        stat = sem("stat")
        marks = sem("marks")
        pool_marks = sem("pool_marks")
        var_ready = sem("var_ready")
        rstd_ready = sem("rstd_ready")
        a_ready = sem("a_ready")
        aT_ready = sem("aT_ready")
        aT_hi_ready = sem("aT_hi_ready")
        aT_lo_ready = sem("aT_lo_ready")
        piece_ready = sem("piece_ready")
        turned_ready = sem("turned_ready")
        sin_done = sem("sin_done")
        roped_ready = sem("roped_ready")
        qk_hi_ready = sem("qk_hi_ready")
        qk_lo_ready = sem("qk_lo_ready")
        v_copied = sem("v_copied")
        scores_ready = sem("scores_ready")
        capped_ready = sem("capped_ready")
        exp_ready = sem("exp_ready")
        probs_ready = sem("probs_ready")
        pv_done = sem("pv_done")
        inv_ready = sem("inv_ready")
        y_ready = sem("y_ready")
        y_hi_ready = sem("y_hi_ready")
        y_lo_ready = sem("y_lo_ready")
        out_ready = sem("out_ready")
        x2_ready = sem("x2_ready")

        def seq_rows(dram, b):
            return dram[bass.ds(b * SEQ, SEQ), :].rearrange("(t p) c -> p t c", p=P)

        block = ctx.enter_context(nc.Block())

        @block.sync
        def _(sp):
            def load_norm(b, q):
                at_least(sp, a_ready, b - 1)
                sp.dma_start(xn[:, q], seq_rows(src, b)).then_inc(xn_loaded[q], 16)

            def load_residual(b, q, n):
                at_least(sp, stored[q], 16 * n)
                sp.dma_start(xr[:, q], seq_rows(src, b)).then_inc(xr_loaded[q], 16)

            def store(b, q):
                sp.wait_ge(x2_ready, CREDIT + b + 1)
                sp.dma_start(seq_rows(dst, b), xr[:, q]).then_inc(stored[q], 16)

            load_norm(0, 0)
            load_norm(1, 1)
            for q in range(2):
                load_residual(q, q, 0)
            with sp.Fori(0, SEQS // 2 - 1) as i:
                for q in range(2):
                    load_norm(i * 2 + (q + 2), q)
                    store(i * 2 + q, q)
                    load_residual(i * 2 + (q + 2), q, i + 1)
            for q in range(2):
                store(SEQS - 2 + q, q)
            for q in range(2):
                sp.wait_ge(stored[q], 16 * (SEQS // 2))

        @block.tensor
        def _(pe):
            def transposes(b):
                pe.wait_ge(a_ready, b + 1)
                at_least(pe, v_copied, b, CREDIT)
                for k in range(KC):
                    for t in range(QT):
                        last = nc.tensor.transpose(pj[0][:, k, t * P:(t + 1) * P], a[:, t, k * P:(k + 1) * P], m.ident[:])
                last.then_inc(aT_ready, 1)

            def project(b, q, n):
                bank = pj[1 - n % 2]
                if n == 0:
                    pe.wait_ge(aT_lo_ready, b + 1)
                    at_least(pe, x2_ready, b - 1, CREDIT)
                elif n >= 2:
                    pe.wait_ge(turned_ready, b * PIECES + (n - 1))
                for c in range(2):
                    for k in range(KC):
                        if n < PIECES:
                            chunk = 2 * ((n - 1) % PIECES) + c
                            last = split_matmul(nc, bank[:, c, :], m.qk_hi[:, k, chunk, :], m.qk_lo[:, k, chunk, :],
                                                aT_hi[:, k, :], aT_lo[:, k, :], k == 0, k == KC - 1)
                        else:
                            at = slice(c * P, (c + 1) * P)
                            last = split_matmul(nc, bank[:, c, :], aT_hi[:, k, at], aT_lo[:, k, at],
                                                m.v_hi[:, k, :], m.v_lo[:, k, :], k == 0, k == KC - 1)
                last.then_inc(piece_ready, 1)

            def score_unit(b, q, u):
                g, t = u // QT, u % QT
                at_least(pe, capped_ready, b * UNITS + u, CREDIT)
                if u == 0:
                    pe.wait_ge(qk_lo_ready, b * PIECES + PIECES)
                keys = slice(t * P, (t + 1) * P)
                n = REP * (SEQ - t * P)
                for k_part, q_part in ((qk_hi, qk_hi), (qk_lo, qk_hi), (qk_hi, qk_lo)):
                    for j in range(JH):
                        r = slice(j * HD, (j + 1) * HD)
                        last = nc.tensor.matmul(
                            scores[:, j, 0:n].rearrange("p (r s) -> p r s", r=REP), k_part[r, q, 4 + g, keys],
                            q_part[r, q, REP * g:REP * g + REP, t * P:SEQ],
                            start=k_part is qk_hi and q_part is qk_hi, stop=q_part is qk_lo)
                last.then_inc(scores_ready, 1)

            def weighted_values(b, q, u):
                g, t = u // QT, u % QT
                pe.wait_ge(probs_ready, b * UNITS + u + 1)
                if t == 0:
                    at_least(pe, y_ready, b * GROUPS + g, CREDIT)
                n = REP * (SEQ - t * P)
                for bank, ones in ((pv, False), (den, True)):
                    for j in range(JH):
                        w = m.ones_f[:] if ones else v[:, q, t, (JH * g + j) * HD:(JH * g + j + 1) * HD]
                        out = bank[j * HD:(j + 1) * HD, :].rearrange("p (r s) -> p r s", r=REP)[:, :, t * P:SEQ]
                        last = nc.tensor.matmul(out, w, probs[:, u % 2, j, 0:n].rearrange("p (r s) -> p r s", r=REP),
                                                start=t == 0, stop=t == QT - 1)
                last.then_inc(pv_done, 1)

            def output(b, ahead):
                pe.wait_ge(y_lo_ready, b * GROUPS + GROUPS)
                pe.wait_ge(turned_ready, b * PIECES + (2 * PIECES if ahead else PIECES))
                for t in range(QT):
                    for g in range(GROUPS):
                        for r in range(REP):
                            at = slice(r * SEQ + t * P, r * SEQ + (t + 1) * P)
                            n = REP * g + r
                            last = split_matmul(nc, pj[1][:, t, :], y_hi[:, g, at], y_lo[:, g, at], m.o_hi[:, n, :],
                                                m.o_lo[:, n, :], n == 0, n == 3)
                last.then_inc(out_ready, 1)

            def slot_of(b, q, ahead):
                score_unit(b, q, 0)
                if ahead:
                    transposes(b + 1)
                score_unit(b, q, 1)
                weighted_values(b, q, 0)
                if ahead:
                    project(b + 1, 1 - q, 0)
                score_unit(b, q, 2)
                weighted_values(b, q, 1)
                if ahead:
                    project(b + 1, 1 - q, 1)
                    project(b + 1, 1 - q, 2)
                score_unit(b, q, 3)
                weighted_values(b, q, 2)
                if ahead:
                    project(b + 1, 1 - q, 3)
                weighted_values(b, q, 3)
                output(b, ahead)

            give_credit(pe, scores_ready, pv_done, out_ready, piece_ready, aT_ready)
            transposes(0)
            for n in range(4):
                project(0, 0, n)
            with pe.Fori(0, SEQS // 2 - 1) as i:
                for q in range(2):
                    slot_of(i * 2 + q, q, True)
            slot_of(SEQS - 2, 0, True)
            slot_of(SEQS - 1, 1, False)

        @block.scalar
        def _(act):
            def aT_hi_part(b):
                act.wait_ge(aT_ready, CREDIT + b + 1)
                at_least(act, piece_ready, 4 * b, CREDIT)
                nc.scalar.copy(aT_hi[:], pj[0][:]).then_inc(aT_hi_ready, 1)

            def qk_hi_part(b, q, n):
                act.wait_ge(roped_ready, b * PIECES + n + 1)
                at_least(act, scores_ready, UNITS * (b - 1), CREDIT)
                c = 2 * ((n - 1) % PIECES)
                nc.scalar.copy(qk_hi[:, q, c:c + 2, :], roped[:, n]).then_inc(qk_hi_ready, 1)

            def copy_v(b, q):
                act.wait_ge(piece_ready, CREDIT + 4 * b + 4)
                at_least(act, pv_done, UNITS * (b - 1), CREDIT)
                nc.scalar.copy(v[:, q], pj[0][:]).then_inc(v_copied, 1)

            def cap(b, u):
                act.wait_ge(scores_ready, CREDIT + b * UNITS + u + 1)
                n = REP * (SEQ - u % QT * P)
                at_least(act, exp_ready, b * UNITS + max(u - 1, 0), CREDIT)
                nc.scalar.activation(capped[:, u % 2, :, 0:n], scores[:, :, 0:n], ACT.Tanh,
                                     scale=QK_SCALE / SOFTCAP).then_inc(capped_ready, 1)

            def exponential(b, u):
                act.wait_ge(capped_ready, CREDIT + b * UNITS + u + 1)
                at_least(act, pv_done, b * UNITS + max(u - 1, 0), CREDIT)
                n = REP * (SEQ - u % QT * P)
                nc.scalar.activation(probs[:, u % 2, :, 0:n], capped[:, u % 2, :, 0:n], ACT.Exp,
                                     scale=SOFTCAP).then_inc(exp_ready, 1)

            def y_hi_part(b, g):
                act.wait_ge(y_ready, CREDIT + b * GROUPS + g + 1)
                at_least(act, out_ready, b, CREDIT)
                nc.scalar.copy(y_hi[:, g, :], y[:]).then_inc(y_hi_ready, 1)

            def slot_of(b, q, ahead):
                cap(b, 0)
                if ahead:
                    aT_hi_part(b + 1)
                exponential(b, 0)
                cap(b, 1)
                exponential(b, 1)
                cap(b, 2)
                if ahead:
                    qk_hi_part(b + 1, 1 - q, 0)
                exponential(b, 2)
                y_hi_part(b, 0)
                cap(b, 3)
                if ahead:
                    qk_hi_part(b + 1, 1 - q, 1)
                exponential(b, 3)
                if ahead:
                    qk_hi_part(b + 1, 1 - q, 2)
                    copy_v(b + 1, 1 - q)
                y_hi_part(b, 1)

            give_credit(act, capped_ready, exp_ready, y_hi_ready, v_copied)
            aT_hi_part(0)
            for n in range(PIECES):
                qk_hi_part(0, 0, n)
            copy_v(0, 0)
            with act.Fori(0, SEQS // 2 - 1) as i:
                for q in range(2):
                    slot_of(i * 2 + q, q, True)
            slot_of(SEQS - 2, 0, True)
            slot_of(SEQS - 1, 1, False)

        @block.gpsimd
        def _(pool):
            def root(b):
                pool.wait_ge(var_ready, b + 1)
                pool.tensor_tensor(rstd[:], var_in[:], m.neg_half[:, 0, 0:QT], ALU.pow).then_inc(rstd_ready, 1)

            def rope(b, n):
                pool.wait_ge(turned_ready, b * PIECES + n + 1)
                at_least(pool, qk_lo_ready, b * PIECES + (n + 1 - PIECES))
                sin = m.sin[:].unsqueeze(1).to_broadcast([P, 2, SEQ])
                pool.tensor_tensor(by_sin[:, n], turned[:, n], sin, ALU.mult).then_inc(sin_done, 1)
                pool.wait_ge(sin_done, b * PIECES + n + 1)
                pool.tensor_tensor(roped[:, n], by_cos[:, n], by_sin[:, n], ALU.add).then_inc(roped_ready, 1)

            def causal(b, u):
                wait_apart(pool, exp_ready, CREDIT + b * UNITS + u + 1, pool_marks)
                n = REP * (SEQ - u % QT * P)
                diag = probs[:, u % 2, :, 0:n].rearrange("p j (r s) -> p j r s", r=REP)[:, :, :, 0:P]
                pool.affine_select(out=diag, in_=diag, compare_op=ALU.is_ge, fill=zero, base=0,
                                   pattern=[[0, JH], [0, REP], [1, P]], channel_multiplier=-1).then_inc(probs_ready, 1)

            def slot_of(b, ahead, further):
                causal(b, 0)
                causal(b, 1)
                if ahead:
                    rope(b + 1, 0)
                causal(b, 2)
                if ahead:
                    rope(b + 1, 1)
                    rope(b + 1, 2)
                causal(b, 3)
                if further:
                    root(b + 2)

            zero = pool.to_reg(0.0)
            root(0)
            for n in range(PIECES):
                rope(0, n)
            root(1)
            with pool.Fori(0, SEQS // 2 - 1) as i:
                for q in range(2):
                    slot_of(i * 2 + q, True, True)
            slot_of(SEQS - 2, True, False)
            slot_of(SEQS - 1, False, False)

        @block.vector
        def _(dve):
            def norm(b, q, n):
                dve.wait_ge(xn_loaded[q], 16 * (n + 1))
                for t in range(QT):
                    ins = dve.bn_stats(stats[:, t, :], xn[:, q, t, :])
                ins.then_inc(stat, 1)
                wait_apart(dve, stat, b * 2 + 1, marks)
                for t in range(QT):
                    ins = dve.bn_aggr(moments[:, t, :], stats[:, t, :])
                ins.then_inc(stat, 1)
                dve.wait_ge(stat, b * 2 + 2)
                dve.tensor_scalar(var_in[:], moments[:, :, 1], LN_EPS, None, ALU.add).then_inc(var_ready, 1)
                dve.wait_ge(rstd_ready, b + 1)
                at_least(dve, aT_ready, b, CREDIT)
                for t in range(QT):
                    ins = dve.tensor_scalar(a[:, t, :], xn[:, q, t, :], moments[:, t, 0:1], rstd[:, t:t + 1],
                                            ALU.subtract, ALU.mult)
                ins.then_inc(a_ready, 1)

            def aT_lo_part(b):
                dve.wait_ge(aT_hi_ready, b + 1)
                dve.tensor_tensor(aT_lo[:], pj[0][:], aT_hi[:].bitcast(F32), ALU.subtract).then_inc(aT_lo_ready, 1)

            def turn(b, n):
                dve.wait_ge(piece_ready, CREDIT + b * 4 + n + 1)
                at_least(dve, roped_ready, b * PIECES + (n + 1 - PIECES))
                cos = m.cos[:].unsqueeze(1).to_broadcast([P, 2, SEQ])
                bank = pj[1 - n % 2]
                dve.tensor_tensor(by_cos[:, n], bank[:], cos, ALU.mult)
                dve.stream_shuffle(turned[:, n], bank[:], [(i + HD // 2) % HD for i in range(HD)]).then_inc(turned_ready, 1)

            def qk_lo_part(b, q, n):
                dve.wait_ge(qk_hi_ready, b * PIECES + n + 1)
                c = 2 * ((n - 1) % PIECES)
                dve.tensor_tensor(qk_lo[:, q, c:c + 2, :], roped[:, n], qk_hi[:, q, c:c + 2, :].bitcast(F32),
                                  ALU.subtract).then_inc(qk_lo_ready, 1)

            def divide(b, g):
                dve.wait_ge(pv_done, CREDIT + b * UNITS + QT * (g + 1))
                dve.reciprocal(inv_den[:], den[:]).then_inc(inv_ready, 1)
                dve.wait_ge(inv_ready, b * GROUPS + g + 1)
                at_least(dve, y_hi_ready, b * GROUPS + g, CREDIT)
                dve.tensor_tensor(y[:], pv[:], inv_den[:], ALU.mult).then_inc(y_ready, 1)

            def y_lo_part(b, g):
                dve.wait_ge(y_hi_ready, CREDIT + b * GROUPS + g + 1)
                dve.tensor_tensor(y_lo[:, g, :], y[:], y_hi[:, g, :].bitcast(F32), ALU.subtract).then_inc(y_lo_ready, 1)

            def residual(b, q, n):
                dve.wait_ge(out_ready, CREDIT + b + 1)
                dve.wait_ge(xr_loaded[q], 16 * (n + 1))
                dve.tensor_tensor(xr[:, q], xr[:, q], pj[1][:], ALU.add).then_inc(x2_ready, 1)

            def slot_of(b, q, n, ahead, further):
                if ahead:
                    aT_lo_part(b + 1)
                    turn(b + 1, 0)
                divide(b, 0)
                if ahead:
                    qk_lo_part(b + 1, 1 - q, 0)
                    turn(b + 1, 1)
                    turn(b + 1, 2)
                y_lo_part(b, 0)
                if ahead:
                    qk_lo_part(b + 1, 1 - q, 1)
                    qk_lo_part(b + 1, 1 - q, 2)
                divide(b, 1)
                y_lo_part(b, 1)
                if further:
                    norm(b + 2, q, n + 1)
                residual(b, q, n)

            give_credit(dve, y_ready, x2_ready)
            norm(0, 0, 0)
            aT_lo_part(0)
            for n in range(PIECES):
                turn(0, n)
                qk_lo_part(0, 0, n)
            norm(1, 1, 0)
            with dve.Fori(0, SEQS // 2 - 1) as i:
                for q in range(2):
                    slot_of(i * 2 + q, q, i, True, True)
            slot_of(SEQS - 2, 0, SEQS // 2 - 1, True, False)
            slot_of(SEQS - 1, 1, SEQS // 2 - 1, False, False)


def build(nc, ins, out, stages=("r1", "e1", "att", "r2", "e2")):
    m = Memory()
    ctx = ExitStack()
    with ctx:
        def sb(name, shape, dt):
            return ctx.enter_context(nc.sbuf_tensor(name, shape, dt))

        m.gu_hi = sb("gu_hi", [P, KC, GU, P], F32R)
        m.gu_lo = sb("gu_lo", [P, KC, GU, P], F32R)
        m.down_hi = sb("down_hi", [P, MT, C], F32R)
        m.down_lo = sb("down_lo", [P, MT, C], F32R)
        m.router_hi = sb("router_hi", [P, KC, RW], F32R)
        m.router_lo = sb("router_lo", [P, KC, RW], F32R)
        m.qk_hi = sb("qk_hi", [P, KC, 6, P], F32R)
        m.qk_lo = sb("qk_lo", [P, KC, 6, P], F32R)
        m.v_hi = sb("v_hi", [P, KC, C], F32R)
        m.v_lo = sb("v_lo", [P, KC, C], F32R)
        m.o_hi = sb("o_hi", [P, 4, C], F32R)
        m.o_lo = sb("o_lo", [P, 4, C], F32R)
        m.w_norm = sb("w_norm", [P, KC], F32)
        m.cos = sb("cos", [P, SEQ], F32)
        m.sin = sb("sin", [P, SEQ], F32)
        m.ident = sb("ident", [P, P], F32)
        m.before = sb("before", [P, P], BF16)
        m.ones_b = sb("ones_b", [P, P], BF16)
        m.ones_f = sb("ones_f", [P, HD], F32)
        m.neg_half = sb("neg_half", [P, 2, TJ], F32)
        m.iota_e = sb("iota_e", [P, E], F32)
        m.tok_f = sb("tok_f", [P, 2, TJ * TOPK], F32)
        m.z_rows = nc.dram_tensor("z_rows", [T + PAD, C], F32, kind="Internal").ap()
        m.acc1 = nc.dram_tensor("acc1", [T + PAD, C], F32, kind="Internal").ap()
        m.x2 = nc.dram_tensor("x2", [T, C], F32, kind="Internal").ap()
        m.acc2 = out
        m.table1 = nc.dram_tensor("table1", [E * CAP, 2], I32, kind="Internal").ap()
        m.table2 = nc.dram_tensor("table2", [E * CAP, 2], I32, kind="Internal").ap()

        setup(nc, m, ins)
        m.turn = 0
        if stages == "att":
            attention(nc, m, ins["X"], m.acc2[0:T, :])
            return
        if stages == "ffn":
            route_and_shared(nc, m, "f1", ins["X"], m.acc2, m.table1)
            experts(nc, m, "e1", m.acc2, m.table1, ins)
            return
        route_and_shared(nc, m, "f1", ins["X"], m.acc1, m.table1)
        experts(nc, m, "e1", m.acc1, m.table1, ins)
        attention(nc, m, m.acc1, m.x2)
        m.turn = 1
        route_and_shared(nc, m, "f2", m.x2, m.acc2, m.table2)
        experts(nc, m, "e2", m.acc2, m.table2, ins)


NAMES = {"X": "L0_attn_X", "Wq": "L0_attn_Wq", "Wk": "L0_attn_Wk", "Wv": "L0_attn_Wv", "Wo": "L0_attn_Wo",
         "w_norm": "L0_ffn_w_norm", "w_router": "L0_ffn_w_router", "w_gate": "L0_ffn_w_gate",
         "w_up": "L0_ffn_w_up", "w_down": "L0_ffn_w_down", "sw_gate": "L0_ffn_sw_gate",
         "sw_up": "L0_ffn_sw_up", "sw_down": "L0_ffn_sw_down", "w_sgate": "L0_ffn_w_shared_gate"}


def rotary_tables():
    inv_freq = (np.float32(1.0) / np.float32(10000.0) ** (np.arange(0, HD, 2, dtype=np.float32) / np.float32(HD)))
    freqs = np.arange(SEQ, dtype=np.float32)[:, None] * inv_freq.astype(np.float32)[None, :]
    angle = np.tile(np.concatenate((freqs, freqs), axis=-1).T, (P // HD, 1))
    sign = np.tile(np.repeat(np.array([-1.0, 1.0], np.float32), HD // 2), P // HD)[:, None]
    return np.cos(angle).astype(np.float32), (np.sin(angle) * sign).astype(np.float32)


def kernel(**inputs):
    import concourse.bacc as bacc
    from concourse.bass_utils import run_bass_kernel_spmd

    nc = bacc.Bacc("TRN2", target_bir_lowering=False, num_devices=1)
    arrays = {name: np.ascontiguousarray(inputs[of]) for name, of in NAMES.items()}
    arrays["X"] = arrays["X"].reshape(T, C)
    arrays["cos"], arrays["sin"] = rotary_tables()
    ins = {name: nc.dram_tensor(f"in_{name}", a.shape, mybir.dt.from_np(a.dtype), kind="ExternalInput").ap()
           for name, a in arrays.items()}
    out = nc.dram_tensor("out", [T + PAD, C], F32, kind="ExternalOutput").ap()
    build(nc, ins, out)
    result = run_bass_kernel_spmd(nc, [{f"in_{name}": a for name, a in arrays.items()}], core_ids=[0])
    return result.results[0]["out"][:T].reshape(SEQS, SEQ, C)
```

```python
from contextlib import ExitStack

import numpy as np

import concourse.bass as bass
from concourse import mybir

P = 128
F32 = mybir.dt.float32
F32R = mybir.dt.float32r
BF16 = mybir.dt.bfloat16
I32 = mybir.dt.int32
U32 = mybir.dt.uint32
ALU = mybir.AluOpType
ACT = mybir.ActivationFunctionType
AX = mybir.AxisListType

SEQS, SEQ, C = 16, 256, 256
T = SEQS * SEQ
KC = C // P
HEADS, KV_HEADS, HD = 16, 8, 32
REP = HEADS // KV_HEADS
E, TOPK, FE = 32, 4, 176
FS = 704
CAP = 128
LN_EPS, RMS_EPS = 1e-5, 1e-6
BLK = 512
NB = T // BLK
TJ = BLK // P
MT = 6
LAST = FS - 5 * P
GU = 2 * MT - 1
RW = E + 2
PAD = P
NO_SLOT = float(2 * E * CAP)
UNDERFLOW = -104.0
SOFTCAP = 50.0
QK_SCALE = 256.0 ** -0.5
FD = FE // 2


class Memory:
    pass


CREDIT = 1


def at_least(engine, sem, value, credit=0):
    if isinstance(value, int) and value <= 0:
        return
    engine.wait_ge(sem, value + credit)


def give_credit(engine, *sems):
    for sem in sems:
        engine.sem_inc(sem, CREDIT)


def wait_apart(engine, sem, value, marks):
    engine.wait_ge(sem, value)
    engine.sem_inc(marks, 1)


def split_matmul(nc, out, w_hi, w_lo, x_hi, x_lo, first, last):
    nc.tensor.matmul(out, w_hi, x_hi, start=first, stop=False)
    nc.tensor.matmul(out, w_lo, x_hi, start=False, stop=False)
    return nc.tensor.matmul(out, w_hi, x_lo, start=False, stop=last)


class SharedWeights:

    def __init__(self, nc, m, ins, sb, sem):
        self.ins, self.m, self.nc = ins, m, nc
        self.gate = sb("raw_gate", [P, KC, FS], F32)
        self.up = sb("raw_up", [P, KC, FS], F32)
        self.down = sb("raw_down", [P, MT, C], F32)
        self.gu_loaded = sem("raw_gu_loaded")
        self.down_loaded = sem("raw_down_loaded")
        self.hi_made = sem("shared_hi_made")
        self.lo_made = sem("shared_lo_made")
        self.gu_splits, self.down_splits = [], []
        g, u = self.gate[:], self.up[:]
        for c in range(GU):
            mt = c // 2
            if mt < MT - 1:
                src = (g, u)[c % 2][:, :, mt * P:(mt + 1) * P]
                self.gu_splits.append((m.gu_hi[:, :, c, :], m.gu_lo[:, :, c, :], src))
            else:
                for half, src in enumerate((g, u)):
                    at = slice(half * LAST, (half + 1) * LAST)
                    self.gu_splits.append((m.gu_hi[:, :, c, at], m.gu_lo[:, :, c, at], src[:, :, mt * P:FS]))
        self.down_splits.append((m.down_hi[:, 0:MT - 1, :], m.down_lo[:, 0:MT - 1, :], self.down[:, 0:MT - 1, :]))
        self.down_splits.append((m.down_hi[0:LAST, MT - 1, :], m.down_lo[0:LAST, MT - 1, :],
                                 self.down[0:LAST, MT - 1, :]))
        self.total = len(self.gu_splits) + len(self.down_splits)

    def load(self, sp):
        sp.dma_start(self.gate[:], self.ins["sw_gate"].rearrange("(k p) f -> p k f", p=P)).then_inc(self.gu_loaded, 16)
        sp.dma_start(self.up[:], self.ins["sw_up"].rearrange("(k p) f -> p k f", p=P)).then_inc(self.gu_loaded, 16)
        sp.dma_start(self.down[:, 0:MT - 1, :], self.ins["sw_down"][0:(MT - 1) * P, :].rearrange("(c p) n -> p c n", p=P)
                     ).then_inc(self.down_loaded, 16)
        sp.dma_start(self.down[0:LAST, MT - 1, :], self.ins["sw_down"][(MT - 1) * P:FS, :]).then_inc(self.down_loaded, 16)

    def high_parts(self, act):
        act.wait_ge(self.gu_loaded, 32)
        for hi, lo, raw in self.gu_splits:
            act.copy(hi, raw).then_inc(self.hi_made, 1)
        act.wait_ge(self.down_loaded, 32)
        for hi, lo, raw in self.down_splits:
            act.copy(hi, raw).then_inc(self.hi_made, 1)

    def low_parts(self, dve, splits, done):
        for n, (hi, lo, raw) in enumerate(splits):
            dve.wait_ge(self.hi_made, done + n + 1)
            dve.tensor_tensor(lo, raw, hi.bitcast(F32), ALU.subtract).then_inc(self.lo_made, 1)


class AttentionWeights:

    def __init__(self, nc, m, ins, sb, sem):
        self.ins, self.m = ins, m
        self.q = sb("raw_q", [P, KC, HEADS * HD], F32)
        self.k = sb("raw_k", [P, KC, KV_HEADS * HD], F32)
        self.v = sb("raw_v", [P, KC, KV_HEADS * HD], F32)
        self.o = sb("raw_o", [P, 4, C], F32)
        self.loaded = sem("attention_loaded")
        self.hi_made = sem("attention_hi_made")
        self.splits = []
        for k in range(KC):
            for group in range(2):
                for r in range(REP):
                    q = self.q[:, k, :].rearrange("p (g j r d) -> p g r j d", g=2, r=REP, d=HD)[:, group, r]
                    n = REP * group + r
                    hi = m.qk_hi[:, k, n, :].rearrange("p (j d) -> p j d", d=HD)
                    lo = m.qk_lo[:, k, n, :].rearrange("p (j d) -> p j d", d=HD)
                    self.splits.append((hi, lo, q))
            kk = self.k[:, k, :].rearrange("p (n c) -> p n c", n=2)
            self.splits.append((m.qk_hi[:, k, 4:6, :], m.qk_lo[:, k, 4:6, :], kk))
        self.splits.append((m.v_hi[:], m.v_lo[:], self.v[:]))
        self.splits.append((m.o_hi[:], m.o_lo[:], self.o[:]))

    def load(self, sp):
        loads = [(self.q[:], self.ins["Wq"].rearrange("(k p) n -> p k n", p=P)),
                 (self.k[:], self.ins["Wk"].rearrange("(k p) n -> p k n", p=P)),
                 (self.v[:], self.ins["Wv"].rearrange("(k p) n -> p k n", p=P)),
                 (self.m.cos[:], self.ins["cos"]),
                 (self.m.sin[:], self.ins["sin"])]
        wo = self.ins["Wo"].rearrange("(g j r d) n -> g r j d n", g=2, r=REP, d=HD)
        for group in range(2):
            for r in range(REP):
                for j in range(4):
                    loads.append((self.o[j * HD:(j + 1) * HD, REP * group + r, :], wo[group, r, j]))
        for dst, src in loads:
            sp.dma_start(dst, src).then_inc(self.loaded, 16)
        self.n_loads = len(loads)

    def high_parts(self, act):
        act.wait_ge(self.loaded, 16 * self.n_loads)
        for hi, lo, raw in self.splits:
            act.copy(hi, raw).then_inc(self.hi_made, 1)

    def low_parts(self, dve):
        for n, (hi, lo, raw) in enumerate(self.splits):
            dve.wait_ge(self.hi_made, n + 1)
            dve.tensor_tensor(lo, raw, hi.bitcast(F32), ALU.subtract)


def setup(nc, m, ins):
    ctx = ExitStack()
    with ctx:
        def sb(name, shape, dt):
            return ctx.enter_context(nc.sbuf_tensor(name, shape, dt))

        def sem(name):
            return ctx.enter_context(nc.semaphore(name))

        raw_router = sb("raw_router", [P, KC, RW], F32)
        zeros = sb("zeros", [P, C], F32)
        empty = sb("empty", [P, E, 2], I32)
        iota_i = sb("iota_i", [P, E], I32)
        tok_i = sb("tok_i", [P, TJ * TOPK], I32)
        loaded = sem("setup_loaded")
        ramps_made = sem("setup_ramps_made")
        memset_made = sem("setup_memset_made")
        padded = sem("setup_padded")
        cleared = sem("setup_cleared")
        hi_made = sem("setup_hi_made")

        with nc.Block() as block:
            @block.sync
            def _(sp):
                sp.wait_ge(padded, 1)
                sp.dma_start(raw_router[:, :, 0:E], ins["w_router"].rearrange("(k p) n -> p k n", p=P)).then_inc(loaded, 16)
                sp.dma_start(raw_router[:, :, E:E + 1], ins["w_sgate"].rearrange("(k p) n -> p k n", p=P),
                             allow_slow_non_contiguous=True).then_inc(loaded, 16)
                for k in range(KC):
                    sp.dma_start(m.w_norm[:, k:k + 1], ins["w_norm"][k * P:(k + 1) * P].rearrange("(p a) -> p a", a=1),
                                 allow_slow_non_contiguous=True).then_inc(loaded, 16)
                sp.wait_ge(padded, 4)
                for rows in (m.z_rows, m.acc1, m.acc2):
                    sp.dma_start(rows[T:T + PAD, :], zeros[:]).then_inc(cleared, 16)
                for table in (m.table1, m.table2):
                    sp.dma_start(table.rearrange("(c e) w -> c e w", e=E), empty[:]).then_inc(cleared, 16)
                sp.wait_ge(cleared, 5 * 16)
                sp.wait_ge(loaded, (2 + KC) * 16)

            @block.gpsimd
            def _(pool):
                pool.memset(raw_router[:], 0.0).then_inc(padded, 1)
                pool.memset(zeros[:], 0.0).then_inc(padded, 1)
                pool.iota(empty[:, :, 0], [[0, E]], base=T, channel_multiplier=1).then_inc(padded, 1)
                pool.memset(empty[:, :, 1], 0).then_inc(padded, 1)
                pool.memset(m.ident[:], 0.0).then_inc(memset_made, 1)
                pool.memset(m.before[:], 1.0).then_inc(memset_made, 1)
                pool.iota(iota_i[:], [[1, E]], base=0, channel_multiplier=0).then_inc(ramps_made, 1)
                pool.iota(tok_i[:].rearrange("p (j k) -> p j k", k=TOPK), [[P, TJ], [0, TOPK]], base=0,
                          channel_multiplier=1).then_inc(ramps_made, 1)
                pool.memset(m.ones_b[:], 1.0)
                pool.memset(m.ones_f[:], 1.0)
                pool.memset(m.neg_half[:], -0.5)
                pool.wait_ge(memset_made, 2)
                pool.affine_select(out=m.ident[:], in_=m.ident[:], compare_op=ALU.not_equal, fill=1.0, base=0,
                                   pattern=[[-1, P]], channel_multiplier=1)
                pool.affine_select(out=m.before[:], in_=m.before[:], compare_op=ALU.is_gt, fill=0.0, base=0,
                                   pattern=[[1, P]], channel_multiplier=-1)

            @block.scalar
            def _(act):
                act.wait_ge(loaded, (2 + KC) * 16)
                act.copy(m.router_hi[:], raw_router[:]).then_inc(hi_made, 1)

            @block.vector
            def _(dve):
                dve.wait_ge(ramps_made, 2)
                dve.tensor_copy(m.iota_e[:], iota_i[:])
                for n in range(2):
                    dve.tensor_copy(m.tok_f[:, n, :], tok_i[:])
                dve.wait_ge(hi_made, 1)
                dve.tensor_tensor(m.router_lo[:], raw_router[:], m.router_hi[:].bitcast(F32), ALU.subtract)


def route_and_shared(nc, m, tag, src, acc, table, ins=None):
    ctx = ExitStack()
    with ctx:
        def sb(name, shape, dt):
            return ctx.enter_context(nc.sbuf_tensor(f"{name}_{tag}", shape, dt))

        def psum(name, shape):
            return ctx.enter_context(nc.psum_tensor(f"{name}_{tag}", shape, F32))

        def sem(name):
            return ctx.enter_context(nc.semaphore(f"{name}_{tag}"))

        x = sb("x", [P, 2, TJ, C], F32)
        h = sb("h", [P, TJ, C], F32)
        warm = sb("warm", [P, 1], F32)
        z = sb("z", [P, 2, TJ, C], F32)
        base = sb("base", [P, 2, TJ, C], F32)
        x_hi = sb("x_hi", [P, 2, KC, BLK], F32R)
        x_lo = sb("x_lo", [P, 2, KC, BLK], F32R)
        stats = sb("stats", [P, TJ, 6], F32)
        moments = sb("moments", [P, 2, TJ, 2], F32)
        var_in = sb("var_in", [P, 2, 2, TJ], F32)
        rstd = sb("rstd", [P, 2, 2, TJ], F32)
        row_max = sb("row_max", [P, TJ], F32)
        d = sb("d", [P, TJ, E], F32)
        top = sb("top", [P, TJ, 8], F32)
        top_at = sb("top_at", [P, TJ, 8], U32)
        top_f = sb("top_f", [P, TJ, TOPK], F32)
        chosen = sb("chosen", [P, TJ * TOPK, E], F32)
        mask = sb("mask", [P, TJ, E], BF16)
        mask_sum = sb("mask_sum", [P, E], F32)
        seen = sb("seen", [P, E], BF16)
        exps = sb("exps", [P, TJ, E], F32)
        exp_top = sb("exp_top", [P, TJ, 8], F32)
        gate_in = sb("gate_in", [P, TJ], F32)
        exp_gate = sb("exp_gate", [P, TJ], F32)
        total = sb("total", [P, TJ], F32)
        inv_total = sb("inv_total", [P, TJ], F32)
        gate_den = sb("gate_den", [P, TJ], F32)
        half_gate = sb("half_gate", [P, 2, TJ], F32)
        past = sb("past", [P, TJ, E], F32)
        place = sb("place", [P, TJ, E], F32)
        place_all = sb("place_all", [P, TJ, E], F32)
        picked = sb("picked", [P, TJ * TOPK, E], F32)
        slot_f = sb("slot_f", [P, TJ * TOPK], F32)
        slot = sb("slot", [P, 2, TJ * TOPK], I32)
        entry = sb("entry", [P, 2, TJ * TOPK, 2], I32)
        silu = sb("silu", [P, 2, BLK], F32)
        act_gu = sb("act_gu", [P, 2, BLK], F32)
        a_hi = sb("a_hi", [P, MT, BLK], F32R)
        a_lo = sb("a_lo", [P, MT, BLK], F32R)

        zT = [psum(f"zT{k}", [P, BLK]) for k in range(KC)]
        small = psum("small", [P, BLK])
        logits = small[:, 0:TJ * RW].rearrange("p (j e) -> p j e", e=RW)
        pos = small[:, 256:256 + TJ * E].rearrange("p (j e) -> p j e", e=E)
        gu = [psum(f"gu{n}", [P, BLK]) for n in range(3)]
        down = [psum(f"down{n}", [P, 2, C]) for n in range(2)]

        weights = SharedWeights(nc, m, ins, sb, sem) if ins else None
        x_loaded = [sem("x_loaded0"), sem("x_loaded1")]
        stat = sem("stat")
        marks = sem("marks")
        pool_marks = sem("pool_marks")
        vars_ready = sem("vars_ready")
        rstd_ready = sem("rstd_ready")
        h_ready = sem("h_ready")
        base_ready = sem("base_ready")
        z_ready = sem("z_ready")
        z_stored = [sem("z_stored0"), sem("z_stored1")]
        zT_ready = sem("zT_ready")
        hi_ready = sem("hi_ready")
        lo_ready = sem("lo_ready")
        logits_ready = sem("logits_ready")
        top_ready = sem("top_ready")
        mask_ready = sem("mask_ready")
        exps_ready = sem("exps_ready")
        pos_ready = sem("pos_ready")
        pos_used = sem("pos_used")
        entry_ready = sem("entry_ready")
        warmed = sem("warmed")
        scattered = [sem("scattered0"), sem("scattered1")]
        gu_ready = sem("gu_ready")
        silu_ready = sem("silu_ready")
        prod_ready = sem("prod_ready")
        a_hi_ready = sem("a_hi_ready")
        a_lo_ready = sem("a_lo_ready")
        down_ready = sem("down_ready")
        out_ready = sem("out_ready")
        out_stored = [sem("out_stored0"), sem("out_stored1")]
        base_free = sem("base_free")

        def rows(b):
            return bass.ds(b * BLK, BLK)

        block = ctx.enter_context(nc.Block())

        @block.sync
        def _(sp):
            def load(b, q):
                at_least(sp, base_ready, TJ * (b - 1))
                sp.dma_start(x[:, q], src[rows(b), :].rearrange("(j p) c -> p j c", p=P)).then_inc(x_loaded[q], 16)

            def z_has_been_stored(q, n):
                sp.wait_ge(z_stored[q], 16 * n)

            def free_base(q, n):
                sp.wait_ge(out_stored[q], 16 * n)
                sp.sem_inc(base_free, 1)

            def store_z(b, q):
                sp.wait_ge(z_ready, TJ * (b + 1))
                sp.dma_start(m.z_rows[rows(b), :].rearrange("(j p) c -> p j c", p=P), z[:, q]).then_inc(z_stored[q], 16)

            def store_out(b, q):
                sp.wait_ge(out_ready, CREDIT + TJ * (b + 1))
                sp.dma_start(acc[rows(b), :].rearrange("(j p) c -> p j c", p=P), base[:, q]).then_inc(out_stored[q], 16)

            give_credit(sp, base_free)
            load(0, 0)
            if weights:
                weights.load(sp)
            load(1, 1)
            store_z(0, 0)
            with sp.Fori(0, NB // 2 - 1) as i:
                for q in range(2):
                    b = i * 2 + q
                    z_has_been_stored(q, i + 1)
                    load(b + 2, q)
                    store_z(b + 1, 1 - q)
                    store_out(b, q)
                    free_base(q, i + 1)
            store_z(NB - 1, 1)
            store_out(NB - 2, 0)
            store_out(NB - 1, 1)
            for q in range(2):
                sp.wait_ge(z_stored[q], 16 * (NB // 2))
                sp.wait_ge(out_stored[q], 16 * (NB // 2))

        @block.gpsimd
        def _(pool):
            def roots(b, q, n=0):
                at_least(pool, scattered[q], 16 * TJ * TOPK * n)
                pool.wait_ge(vars_ready, b + 1)
                pool.tensor_tensor(rstd[:, q], var_in[:, q], m.neg_half[:], ALU.pow).then_inc(rstd_ready, 1)

            def scatter(b, q):
                wait_apart(pool, entry_ready, b + 1, pool_marks)
                for n in range(TJ * TOPK):
                    pool.indirect_dma_start(
                        out=table, out_offset=bass.IndirectOffsetOnAxis(ap=slot[:, q, n:n + 1], axis=0),
                        in_=entry[:, q, n, :], in_offset=None, bounds_check=last_slot, oob_is_err=False,
                    ).then_inc(scattered[q], 16)

            last_slot = pool.to_reg(E * CAP - 1)
            roots(0, 0)
            roots(1, 1)
            scatter(0, 0)
            with pool.Fori(0, NB // 2 - 1) as i:
                for q in range(2):
                    b = i * 2 + q
                    roots(b + 2, q, i + 1)
                    scatter(b + 1, 1 - q)
            scatter(NB - 1, 1)
            for q in range(2):
                pool.wait_ge(scattered[q], 16 * TJ * TOPK * (NB // 2))

        @block.tensor
        def _(pe):
            def transposes(b, q):
                pe.wait_ge(z_ready, TJ * (b + 1))
                at_least(pe, lo_ready, KC * b)
                for k in range(KC):
                    for j in range(TJ):
                        last = nc.tensor.transpose(zT[k][:, j * P:(j + 1) * P], z[:, q, j, k * P:(k + 1) * P], m.ident[:])
                    last.then_inc(zT_ready, 1)

            def router(b, q):
                pe.wait_ge(lo_ready, KC * (b + 1))
                at_least(pe, pos_used, b)
                for j in range(TJ):
                    for k in range(KC):
                        at = slice(j * P, (j + 1) * P)
                        last = split_matmul(nc, logits[:, j, :], x_hi[:, q, k, at], x_lo[:, q, k, at],
                                            m.router_hi[:, k, :], m.router_lo[:, k, :], k == 0, k == KC - 1)
                last.then_inc(logits_ready, 1)

            def positions(b):
                pe.wait_ge(mask_ready, b + 1)
                for j in range(TJ):
                    nc.tensor.matmul(pos[:, j, :], m.before[:], mask[:, j, :], start=True, stop=False)
                    for i in range(j):
                        nc.tensor.matmul(pos[:, j, :], m.ones_b[:], mask[:, i, :], start=False, stop=False)
                    last = nc.tensor.matmul(pos[:, j, :], m.ones_b[:], seen[:], start=False, stop=True)
                last.then_inc(pos_ready, 1)

            def gate_up(b, q, c):
                if c < 3:
                    at_least(pe, prod_ready, MT * b, CREDIT)
                elif c % 2:
                    pe.wait_ge(silu_ready, b * MT + (c - 3) // 2 + 1)
                else:
                    pe.wait_ge(prod_ready, CREDIT + b * MT + (c - 3) // 2 + 1)
                for k in range(KC):
                    last = split_matmul(nc, gu[c % 3][:], m.gu_hi[:, k, c, :], m.gu_lo[:, k, c, :],
                                        x_hi[:, q, k, :], x_lo[:, q, k, :], k == 0, k == KC - 1)
                last.then_inc(gu_ready, 1)

            def down_proj(b, j):
                at_least(pe, out_ready, TJ * b, CREDIT)
                for mt in range(MT):
                    if j == 0:
                        pe.wait_ge(a_lo_ready, CREDIT + b * MT + mt + 1)
                    rows_ = slice(0, P if mt < MT - 1 else LAST)
                    at = slice(j * P, (j + 1) * P)
                    last = split_matmul(nc, down[j // 2][:, j % 2, :], a_hi[rows_, mt, at], a_lo[rows_, mt, at],
                                        m.down_hi[rows_, mt, :], m.down_lo[rows_, mt, :], mt == 0, mt == MT - 1)
                last.then_inc(down_ready, 1)

            def slot_of(b, q, ahead):
                for c in range(GU):
                    gate_up(b, q, c)
                    if ahead and c == 6:
                        transposes(b + 1, 1 - q)
                if ahead:
                    router(b + 1, 1 - q)
                for j in range(TJ):
                    down_proj(b, j)
                    if ahead and j == 2:
                        positions(b + 1)

            give_credit(pe, zT_ready, gu_ready, down_ready)
            transposes(0, 0)
            router(0, 0)
            positions(0)
            if weights:
                pe.wait_ge(weights.lo_made, weights.total)
            with pe.Fori(0, NB // 2 - 1) as i:
                for q in range(2):
                    slot_of(i * 2 + q, q, True)
            slot_of(NB - 2, 0, True)
            slot_of(NB - 1, 1, False)

        @block.scalar
        def _(act):
            def scale_z(b, q):
                for j in range(TJ):
                    act.wait_ge(h_ready, b * TJ + j + 1)
                    if j == 0:
                        at_least(act, zT_ready, KC * (b - 1), CREDIT)
                    nc.scalar.activation(z[:, q, j, :], h[:, j, :], ACT.Copy, scale=rstd[:, q, 1, j:j + 1]).then_inc(z_ready, 1)

            def x_hi_parts(b, q):
                for k in range(KC):
                    act.wait_ge(zT_ready, CREDIT + b * KC + k + 1)
                    if k == 0:
                        at_least(act, gu_ready, GU * (b - 1), CREDIT)
                    nc.scalar.activation(x_hi[:, q, k, :], zT[k][:], ACT.Copy, scale=m.w_norm[:, k:k + 1]).then_inc(hi_ready, 1)

            def silu_of(b, mt):
                act.wait_ge(gu_ready, CREDIT + b * GU + 2 * mt + 1)
                at_least(act, prod_ready, b * MT + max(mt - 1, 0), CREDIT)
                c = 2 * mt
                if mt < MT - 1:
                    nc.scalar.activation(silu[:, mt % 2, :], gu[c % 3][:], ACT.Silu).then_inc(silu_ready, 1)
                else:
                    nc.scalar.activation(silu[LAST:P, mt % 2, :], gu[c % 3][0:LAST, :], ACT.Silu).then_inc(silu_ready, 1)

            def a_hi_part(b, mt):
                act.wait_ge(prod_ready, CREDIT + b * MT + mt + 1)
                at_least(act, down_ready, TJ * b, CREDIT)
                r = slice(0, P if mt < MT - 1 else LAST)
                nc.scalar.copy(a_hi[r, mt, :], act_gu[r, mt % 2, :]).then_inc(a_hi_ready, 1)

            def exponentials(b):
                act.wait_ge(top_ready, b + 1)
                at_least(act, entry_ready, b)
                nc.scalar.activation(exps[:], d[:], ACT.Exp).then_inc(exps_ready, 1)
                nc.scalar.activation(exp_top[:], top[:], ACT.Exp).then_inc(exps_ready, 1)
                nc.scalar.activation(exp_gate[:], gate_in[:], ACT.Exp, scale=-1.0).then_inc(exps_ready, 1)
                at_least(act, warmed, b)
                nc.scalar.activation(warm[:], m.w_norm[:, 0:1], ACT.Silu).then_inc(warmed, 1)

            def slot_of(b, q, ahead):
                silu_of(b, 0)
                for mt in range(1, MT):
                    silu_of(b, mt)
                    if ahead and mt == 1:
                        scale_z(b + 1, 1 - q)
                    a_hi_part(b, mt - 1)
                    if ahead and mt == 2:
                        x_hi_parts(b + 1, 1 - q)
                a_hi_part(b, MT - 1)
                if ahead:
                    exponentials(b + 1)

            give_credit(act, a_hi_ready)
            scale_z(0, 0)
            x_hi_parts(0, 0)
            if weights:
                weights.high_parts(act)
            exponentials(0)
            with act.Fori(0, NB // 2 - 1) as i:
                for q in range(2):
                    slot_of(i * 2 + q, q, True)
            slot_of(NB - 2, 0, True)
            slot_of(NB - 1, 1, False)

        @block.vector
        def _(dve):
            count = [0]

            class Chain:
                start = 0

            def step(ins, apart=False):
                ins.then_inc(stat, 1)
                count[0] += 1
                if apart:
                    wait_apart(dve, stat, Chain.start + count[0], marks)
                else:
                    dve.wait_ge(stat, Chain.start + count[0])

            def statistics(b, q, n):
                dve.wait_ge(x_loaded[q], 16 * (n + 1))
                for j in range(TJ):
                    ins = dve.bn_stats(stats[:, j, :], x[:, q, j, :])
                step(ins, apart=True)
                for j in range(TJ):
                    ins = dve.bn_aggr(moments[:, q, j, :], stats[:, j, :])
                step(ins)
                var = moments[:, q, :, 1]
                step(dve.tensor_scalar(var_in[:, q, 0, :], var, LN_EPS, None, ALU.add))
                step(dve.reciprocal(var_in[:, q, 1, :], var_in[:, q, 0, :]))
                step(dve.tensor_tensor(var_in[:, q, 1, :], var_in[:, q, 1, :], var, ALU.mult))
                dve.tensor_scalar(var_in[:, q, 1, :], var_in[:, q, 1, :], RMS_EPS, None, ALU.add).then_inc(vars_ready, 1)

            def normalise(b, q):
                dve.wait_ge(rstd_ready, b + 1)
                at_least(dve, z_ready, TJ * b)
                for j in range(TJ):
                    dve.tensor_scalar(h[:, j, :], x[:, q, j, :], moments[:, q, j, 0:1], rstd[:, q, 0, j:j + 1],
                                      ALU.subtract, ALU.mult).then_inc(h_ready, 1)

            def make_base(b, q):
                at_least(dve, base_free, b - 1, CREDIT)
                dve.wait_ge(h_ready, TJ * (b + 1))
                for j in range(TJ):
                    dve.scalar_tensor_tensor(out=base[:, q, j, :], in0=h[:, j, :], scalar=0.5, in1=x[:, q, j, :],
                                             op0=ALU.mult, op1=ALU.add).then_inc(base_ready, 1)

            def x_lo_parts(b, q):
                for k in range(KC):
                    dve.wait_ge(hi_ready, b * KC + k + 1)
                    dve.scalar_tensor_tensor(out=x_lo[:, q, k, :], in0=zT[k][:], scalar=m.w_norm[:, k:k + 1],
                                             in1=x_hi[:, q, k, :].bitcast(F32), op0=ALU.mult,
                                             op1=ALU.subtract).then_inc(lo_ready, 1)

            def top_experts(b):
                dve.wait_ge(logits_ready, b + 1)
                at_least(dve, exps_ready, 3 * b)
                dve.tensor_scalar(gate_in[:], logits[:, :, E], -88.0, None, ALU.max)
                step(dve.reduce_max(row_max[:], logits[:, :, 0:E], AX.X))
                for j in range(TJ):
                    ins = dve.tensor_scalar(d[:, j, :], logits[:, j, 0:E], row_max[:, j:j + 1], UNDERFLOW,
                                            ALU.subtract, ALU.max)
                step(ins, apart=True)
                for j in range(TJ):
                    ins = dve.max(top[:, j, :], d[:, j, :])
                step(ins, apart=True)
                for j in range(TJ):
                    ins = dve.max_index(top_at[:, j, :], top[:, j, :], d[:, j, :])
                ins.then_inc(top_ready, 1)

            def masks(b):
                dve.wait_ge(top_ready, b + 1)
                at_least(dve, pos_ready, b)
                step(dve.tensor_copy(top_f[:], top_at[:, :, 0:TOPK]))
                step(dve.tensor_tensor(
                    chosen[:], m.iota_e[:].unsqueeze(1).to_broadcast([P, TJ * TOPK, E]),
                    top_f[:].rearrange("p j k -> p (j k)").unsqueeze(2).to_broadcast([P, TJ * TOPK, E]), ALU.is_equal))
                with nc.allow_low_precision(reason="zeros and ones"):
                    dve.tensor_reduce(mask[:], chosen[:].rearrange("p (j k) e -> p j e k", k=TOPK), AX.X,
                                      ALU.add).then_inc(mask_ready, 1)

            def entries(b, q):
                dve.wait_ge(pos_ready, b + 1)
                step(dve.tensor_reduce(mask_sum[:], mask[:].rearrange("p j e -> p e j"), AX.X, ALU.add))
                with nc.allow_low_precision(reason="integers up to 32"):
                    dve.tensor_tensor(seen[:], seen[:], mask_sum[:], ALU.add)
                dve.tensor_scalar(past[:], pos, float(CAP), NO_SLOT, ALU.is_ge, ALU.mult)
                step(dve.scalar_tensor_tensor(out=place[:], in0=pos, scalar=float(E),
                                              in1=m.iota_e[:].unsqueeze(1).to_broadcast([P, TJ, E]), op0=ALU.mult,
                                              op1=ALU.add))
                step(dve.tensor_tensor(place_all[:], place[:], past[:], ALU.add))
                step(dve.tensor_tensor(
                    picked[:].rearrange("p (j k) e -> p j k e", k=TOPK), chosen[:].rearrange("p (j k) e -> p j k e", k=TOPK),
                    place_all[:].unsqueeze(2).to_broadcast([P, TJ, TOPK, E]), ALU.mult))
                at_least(dve, entry_ready, b)
                step(dve.tensor_reduce(slot_f[:], picked[:], AX.X, ALU.add))
                dve.tensor_copy(slot[:, q, :], slot_f[:])
                dve.tensor_copy(entry[:, q, :, 0], m.tok_f[:, m.turn, :])
                dve.wait_ge(exps_ready, 3 * (b + 1))
                step(dve.reduce_sum(total[:], exps[:], AX.X))
                step(dve.reciprocal(inv_total[:], total[:]))
                dve.scalar_tensor_tensor(
                    out=entry[:, q, :, 1].bitcast(F32).rearrange("p (j k) -> p j k", k=TOPK), in0=exp_top[:, :, 0:TOPK],
                    scalar=0.5, in1=inv_total[:].unsqueeze(2).to_broadcast([P, TJ, TOPK]), op0=ALU.mult, op1=ALU.mult)
                step(dve.tensor_scalar(gate_den[:], exp_gate[:], 2.0, 2.0, ALU.mult, ALU.add))
                dve.reciprocal(half_gate[:, q, :], gate_den[:]).then_inc(pos_used, 1)
                dve.tensor_scalar(m.tok_f[:, m.turn, :], m.tok_f[:, m.turn, :], float(BLK), None, ALU.add
                                  ).then_inc(entry_ready, 1)

            def product(b, mt):
                dve.wait_ge(silu_ready, b * MT + mt + 1)
                dve.wait_ge(gu_ready, CREDIT + b * GU + min(2 * mt + 2, GU))
                at_least(dve, a_hi_ready, b * MT + max(mt - 1, 0), CREDIT)
                at_least(dve, a_lo_ready, b * MT + max(mt - 1, 0), CREDIT)
                if mt < MT - 1:
                    dve.tensor_tensor(act_gu[:, mt % 2, :], silu[:, mt % 2, :], gu[(2 * mt + 1) % 3][:],
                                      ALU.mult).then_inc(prod_ready, 1)
                else:
                    dve.tensor_tensor(act_gu[0:LAST, mt % 2, :], silu[LAST:P, mt % 2, :], gu[(2 * mt) % 3][LAST:P, :],
                                      ALU.mult).then_inc(prod_ready, 1)

            def a_lo_part(b, mt):
                dve.wait_ge(a_hi_ready, CREDIT + b * MT + mt + 1)
                r = slice(0, P if mt < MT - 1 else LAST)
                dve.tensor_tensor(a_lo[r, mt, :], act_gu[r, mt % 2, :], a_hi[r, mt, :].bitcast(F32),
                                  ALU.subtract).then_inc(a_lo_ready, 1)

            def outputs(b, q, tiles):
                for j in tiles:
                    dve.wait_ge(down_ready, CREDIT + b * TJ + j // 2 * 2 + 2)
                    dve.scalar_tensor_tensor(out=base[:, q, j, :], in0=down[j // 2][:, j % 2, :],
                                             scalar=half_gate[:, q, j:j + 1], in1=base[:, q, j, :], op0=ALU.mult,
                                             op1=ALU.add).then_inc(out_ready, 1)

            def slot_of(b, q, ahead, further, n_after):
                product(b, 0)
                for mt in range(1, MT):
                    product(b, mt)
                    if ahead and mt == 1:
                        normalise(b + 1, 1 - q)
                    a_lo_part(b, mt - 1)
                    if ahead and mt == 1:
                        make_base(b + 1, 1 - q)
                    if ahead and mt == 2:
                        x_lo_parts(b + 1, 1 - q)
                a_lo_part(b, MT - 1)
                if ahead:
                    top_experts(b + 1)
                    masks(b + 1)
                if further:
                    statistics(b + 2, q, n_after)
                outputs(b, q, (0, 1))
                if ahead:
                    entries(b + 1, 1 - q)
                outputs(b, q, (2, 3))

            give_credit(dve, prod_ready, out_ready, a_lo_ready)
            step(dve.memset(seen[:], 0.0))
            statistics(0, 0, 0)
            normalise(0, 0)
            statistics(1, 1, 0)
            x_lo_parts(0, 0)
            if weights:
                weights.low_parts(dve, weights.gu_splits, 0)
            top_experts(0)
            masks(0)
            make_base(0, 0)
            if weights:
                weights.low_parts(dve, weights.down_splits, len(weights.gu_splits))
            entries(0, 0)
            head, count[0] = count[0], 0
            steps = 5 + 3 + 2 + 8
            with dve.Fori(0, NB // 2 - 1) as i:
                for q in range(2):
                    Chain.start = i * (2 * steps) + (head + q * steps)
                    count[0] = 0
                    slot_of(i * 2 + q, q, True, True, i + 1)
                    assert count[0] == steps, count
            Chain.start, count[0] = head + (NB - 2) * steps, 0
            slot_of(NB - 2, 0, True, False, 0)
            slot_of(NB - 1, 1, False, False, 0)


def experts(nc, m, tag, acc, table, ins, attention_next=False):
    ctx = ExitStack()
    with ctx:
        def sb(name, shape, dt):
            return ctx.enter_context(nc.sbuf_tensor(f"{name}_{tag}", shape, dt))

        def psum(name, shape):
            return ctx.enter_context(nc.psum_tensor(f"{name}_{tag}", shape, F32))

        def sem(name):
            return ctx.enter_context(nc.semaphore(f"{name}_{tag}"))

        PAIRS = E // 2
        w_gu = sb("w_gu", [P, 2, 2, KC, 2, FE], F32)
        w_down = sb("w_down", [FD, 2, 2, 2, C], F32)
        slots = sb("slots", [P, E, 2], I32)
        source = sb("source", [P, 2, 2, 2], I32)
        target = sb("target", [P, 2, 2, 2], I32)
        rows = sb("rows", [P, 2, 2, C], F32)
        xT = sb("xT", [P, 2, KC, CAP], F32)
        silu = sb("silu_e", [P, 2, FE], F32)
        prod = sb("prod_e", [P, 2, FE], F32)
        prodT = sb("prodT", [FD, 2, 2, CAP], F32)
        y = sb("y", [P, 2, 2, C], F32)
        xT_ps = [psum(f"xT_ps{s}", [P, KC, CAP]) for s in range(2)]
        gu_ps = [psum(f"gu_ps{s}", [P, 2, FE]) for s in range(2)]
        prodT_ps = [psum(f"prodT_ps{s}", [P, 2, CAP]) for s in range(2)]
        y_ps = [psum(f"y_ps{s}", [P, C]) for s in range(2)]

        weights = AttentionWeights(nc, m, ins, sb, sem) if attention_next else None
        table_loaded = sem("table_loaded")
        gu_loaded = [sem("gu_loaded0"), sem("gu_loaded1")]
        down_loaded = [sem("down_loaded0"), sem("down_loaded1")]
        source_ready = sem("source_ready")
        target_ready = sem("target_ready")
        gathered = [sem("gathered0"), sem("gathered1")]
        xT_ready = sem("xT_ready")
        xT_copied = sem("xT_copied")
        gu_done = sem("gu_done")
        silu_done = sem("silu_done")
        prod_done = sem("prod_done")
        prodT_ready = sem("prodT_ready")
        prodT_copied = sem("prodT_copied")
        y_ready = sem("y_ready")
        y_scaled = sem("y_scaled")
        added = sem("added")
        marks = sem("marks")

        block = ctx.enter_context(nc.Block())

        @block.sync
        def _(sp):
            def load_gate_up(p, q):
                for half, name in enumerate(("w_gate", "w_up")):
                    for s in range(2):
                        sp.dma_start(w_gu[:, q, s, :, half, :],
                                     ins[name][bass.ds(p * 2 + s, 1), :, :].rearrange("a (k p) f -> p (a k) f", p=P)
                                     ).then_inc(gu_loaded[q], 16)

            def load_down(p, q):
                for s in range(2):
                    sp.dma_start(w_down[:, q, s, :, :],
                                 ins["w_down"][bass.ds(p * 2 + s, 1), :, :].rearrange("a (k p) n -> p (a k) n", p=FD)
                                 ).then_inc(down_loaded[q], 16)

            sp.dma_start(slots[:], table.rearrange("(c e) w -> c e w", e=E)).then_inc(table_loaded, 16)
            for q in range(2):
                load_gate_up(q, q)
                load_down(q, q)
            if weights:
                weights.load(sp)
            with sp.Fori(0, PAIRS // 2 - 1) as i:
                for q in range(2):
                    p = i * 2 + q
                    sp.wait_ge(gu_done, CREDIT + p * 2 + 2)
                    load_gate_up(p + 2, q)
                    sp.wait_ge(y_ready, CREDIT + p * 2 + 2)
                    load_down(p + 2, q)

        @block.gpsimd
        def _(pool):
            def copy_source(p, q):
                at_least(pool, xT_ready, p * 2 - 2, CREDIT)
                pool.tensor_copy(source[:, q], slots[:, bass.ds(p * 2, 2), :]).then_inc(source_ready, 1)
                wait_apart(pool, source_ready, p + 1, marks)

            def gather(q, s):
                pool.indirect_dma_start(
                    out=rows[:, q, s, :], out_offset=None, in_=m.z_rows,
                    in_offset=bass.IndirectOffsetOnAxis(ap=source[:, q, s, 0:1], axis=0),
                    bounds_check=last_row, oob_is_err=False).then_inc(gathered[q], 16)

            def copy_target(p, q):
                pool.tensor_copy(target[:, q], slots[:, bass.ds(p * 2, 2), :]).then_inc(target_ready, 1)

            def add(p, q, s):
                pool.wait_ge(target_ready, p + 1)
                at_least(pool, added, (p * 2 + s) * 16)
                wait_apart(pool, y_scaled, CREDIT + p * 2 + (s + 1), marks)
                pool.indirect_dma_start(
                    out=acc, out_offset=bass.IndirectOffsetOnAxis(ap=target[:, q, s, 0:1], axis=0),
                    in_=y[:, q, s, :], in_offset=None, compute_op=ALU.add,
                    bounds_check=last_row, oob_is_err=True).then_inc(added, 16)

            def slot_of(p, q, ahead=True, further=True):
                add(p, q, 0)
                if ahead:
                    copy_target(p + 1, 1 - q)
                if further:
                    copy_source(p + 3, 1 - q)
                    gather(1 - q, 0)
                add(p, q, 1)
                if further:
                    gather(1 - q, 1)

            last_row = pool.to_reg(T + PAD - 1)
            pool.wait_ge(table_loaded, 16)
            for p in range(3):
                copy_source(p, p % 2)
                for s in range(2):
                    gather(p % 2, s)
                if p == 0:
                    copy_target(0, 0)
            slot_of(0, 0)
            with pool.Fori(0, PAIRS // 2 - 2) as i:
                for q in range(2):
                    slot_of(i * 2 + (q + 1), 1 - q)
            slot_of(PAIRS - 3, 1, further=False)
            slot_of(PAIRS - 2, 0, further=False)
            slot_of(PAIRS - 1, 1, ahead=False, further=False)
            pool.wait_ge(added, 16 * E)

        @block.tensor
        def _(pe):
            def turn_rows(p, q, n):
                pe.wait_ge(gathered[q], (n + 1) * 32)
                pe.wait_ge(xT_copied, CREDIT + p * 2)
                for s in range(2):
                    for k in range(KC):
                        last = nc.tensor.transpose(xT_ps[s][:, k, :], rows[:, q, s, k * P:(k + 1) * P], m.ident[:])
                    last.then_inc(xT_ready, 1)

            def gate_up(p, q, n, s):
                pe.wait_ge(gu_loaded[q], (n + 1) * 64)
                pe.wait_ge(prod_done, CREDIT + p * 2)
                pe.wait_ge(xT_copied, CREDIT + p * 2 + (s + 1))
                for k in range(KC):
                    last = nc.tensor.matmul(gu_ps[s][:].rearrange("p a f -> p (a f)"), xT[:, s, k, :],
                                            w_gu[:, q, s, k, :, :].rearrange("p a f -> p (a f)"),
                                            start=k == 0, stop=k == KC - 1)
                last.then_inc(gu_done, 1)

            def turn_products(p, s):
                pe.wait_ge(prod_done, CREDIT + p * 2 + (s + 1))
                pe.wait_ge(prodT_copied, CREDIT + p * 2)
                for k in range(2):
                    last = nc.tensor.transpose(prodT_ps[s][0:FD, k, :], prod[:, s, k * FD:(k + 1) * FD], m.ident[:])
                last.then_inc(prodT_ready, 1)

            def down_proj(p, q, n, s):
                pe.wait_ge(down_loaded[q], (n + 1) * 32)
                pe.wait_ge(prodT_copied, CREDIT + p * 2 + (s + 1))
                pe.wait_ge(y_scaled, CREDIT + p * 2)
                for k in range(2):
                    last = nc.tensor.matmul(y_ps[s][:], prodT[:, s, k, :], w_down[:, q, s, k, :], start=k == 0,
                                            stop=k == 1)
                last.then_inc(y_ready, 1)

            def slot_of(p, q, n, n_next, ahead=True):
                if ahead:
                    turn_rows(p + 1, 1 - q, n_next)
                for s in range(2):
                    turn_products(p, s)
                if ahead:
                    gate_up(p + 1, 1 - q, n_next, 0)
                for s in range(2):
                    down_proj(p, q, n, s)
                if ahead:
                    gate_up(p + 1, 1 - q, n_next, 1)

            give_credit(pe, xT_ready, gu_done, prodT_ready, y_ready)
            turn_rows(0, 0, 0)
            for s in range(2):
                gate_up(0, 0, 0, s)
            with pe.Fori(0, PAIRS // 2 - 1) as i:
                for q in range(2):
                    slot_of(i * 2 + q, q, i, i + q)
            slot_of(PAIRS - 2, 0, PAIRS // 2 - 1, PAIRS // 2 - 1)
            slot_of(PAIRS - 1, 1, PAIRS // 2 - 1, 0, ahead=False)

        @block.scalar
        def _(act):
            def silu_of(p, s):
                act.wait_ge(gu_done, CREDIT + p * 2 + (s + 1))
                act.wait_ge(prod_done, CREDIT + p * 2)
                nc.scalar.activation(silu[:, s, :], gu_ps[s][:, 0, :], ACT.Silu).then_inc(silu_done, 1)

            def scale(p, q, s):
                act.wait_ge(y_ready, CREDIT + p * 2 + (s + 1))
                act.wait_ge(target_ready, p + 1)
                nc.scalar.activation(y[:, q, s, :], y_ps[s][:], ACT.Copy,
                                     scale=target[:, q, s, 1:2].bitcast(F32)).then_inc(y_scaled, 1)

            def slot_of(p, q, ahead=True):
                if ahead:
                    silu_of(p + 1, 0)
                for s in range(2):
                    scale(p, q, s)
                if ahead:
                    silu_of(p + 1, 1)

            give_credit(act, y_scaled)
            for s in range(2):
                silu_of(0, s)
            with act.Fori(0, PAIRS // 2 - 1) as i:
                for q in range(2):
                    slot_of(i * 2 + q, q)
            slot_of(PAIRS - 2, 0)
            slot_of(PAIRS - 1, 1, ahead=False)
            if weights:
                weights.high_parts(act)

        @block.vector
        def _(dve):
            def copy_rows(p):
                dve.wait_ge(gu_done, CREDIT + p * 2)
                for s in range(2):
                    dve.wait_ge(xT_ready, CREDIT + p * 2 + (s + 1))
                    for k in range(KC):
                        last = dve.tensor_scalar(xT[:, s, k, :], xT_ps[s][:, k, :], m.w_norm[:, k:k + 1], None, ALU.mult)
                    last.then_inc(xT_copied, 1)

            def product(p, s):
                dve.wait_ge(silu_done, p * 2 + (s + 1))
                dve.wait_ge(prodT_ready, CREDIT + p * 2)
                dve.tensor_tensor(prod[:, s, :], silu[:, s, :], gu_ps[s][:, 1, :], ALU.mult).then_inc(prod_done, 1)

            def copy_products(p, s):
                dve.wait_ge(prodT_ready, CREDIT + p * 2 + (s + 1))
                dve.wait_ge(y_ready, CREDIT + p * 2)
                dve.tensor_copy(prodT[:, s], prodT_ps[s][0:FD]).then_inc(prodT_copied, 1)

            def slot_of(p, ahead=True):
                if ahead:
                    copy_rows(p + 1)
                for s in range(2):
                    copy_products(p, s)
                if ahead:
                    for s in range(2):
                        product(p + 1, s)

            give_credit(dve, xT_copied, prod_done, prodT_copied)
            copy_rows(0)
            for s in range(2):
                product(0, s)
            with dve.Fori(0, PAIRS // 2 - 1) as i:
                for q in range(2):
                    slot_of(i * 2 + q)
            slot_of(PAIRS - 2)
            slot_of(PAIRS - 1, ahead=False)
            if weights:
                weights.low_parts(dve)


def attention(nc, m, src, dst):
    ctx = ExitStack()
    with ctx:
        def sb(name, shape, dt):
            return ctx.enter_context(nc.sbuf_tensor(f"{name}_at", shape, dt))

        def psum(name, shape):
            return ctx.enter_context(nc.psum_tensor(f"{name}_at", shape, F32))

        def sem(name):
            return ctx.enter_context(nc.semaphore(f"{name}_at"))

        QT = SEQ // P
        GROUPS = 2
        UNITS = GROUPS * QT
        PIECES = 3
        JH = 4
        PIECE_BANK = (1, 0, 1, 1)
        W = REP * SEQ

        xn = sb("xn", [P, 2, QT, C], F32)
        xr = sb("xr", [P, 2, QT, C], F32)
        a = sb("a", [P, QT, C], F32)
        stats = sb("stats", [P, QT, 6], F32)
        moments = sb("moments", [P, QT, 2], F32)
        var_in = sb("var_in", [P, QT], F32)
        rstd = sb("rstd", [P, QT], F32)
        aT_hi = sb("aT_hi", [P, KC, SEQ], F32R)
        aT_lo = sb("aT_lo", [P, KC, SEQ], F32R)
        turned = sb("turned", [P, PIECES, 2, SEQ], F32)
        by_cos = sb("by_cos", [P, PIECES, 2, SEQ], F32)
        by_sin = sb("by_sin", [P, PIECES, 2, SEQ], F32)
        roped = sb("roped", [P, PIECES, 2, SEQ], F32)
        qk_hi = sb("qkT_hi", [P, 2, 6, SEQ], F32R)
        qk_lo = sb("qkT_lo", [P, 2, 6, SEQ], F32R)
        v = sb("v", [P, 2, QT, C], F32)
        capped = sb("capped", [P, 2, JH, W], F32)
        probs = sb("probs", [P, 2, JH, W], F32)
        pv_sb = sb("pv_sb", [P, GROUPS, W], F32)
        den_sb = sb("den_sb", [P, GROUPS, W], F32)
        inv_den = sb("inv_den", [P, W], F32)
        y = sb("y", [P, W], F32)
        y_hi = sb("y_hi", [P, GROUPS, W], F32R)
        y_lo = sb("y_lo", [P, GROUPS, W], F32R)

        scores = psum("scores", [P, JH, W])
        pv = psum("pv", [P, W])
        den = psum("den", [P, W])
        pj = [psum(f"pj{n}", [P, 2, SEQ]) for n in range(2)]

        xn_loaded = [sem("xn_loaded0"), sem("xn_loaded1")]
        xr_loaded = [sem("xr_loaded0"), sem("xr_loaded1")]
        stored = [sem("stored0"), sem("stored1")]
        stat = sem("stat")
        marks = sem("marks")
        pool_marks = sem("pool_marks")
        var_ready = sem("var_ready")
        rstd_ready = sem("rstd_ready")
        a_ready = sem("a_ready")
        aT_ready = sem("aT_ready")
        aT_hi_ready = sem("aT_hi_ready")
        aT_lo_ready = sem("aT_lo_ready")
        piece_ready = sem("piece_ready")
        turned_ready = sem("turned_ready")
        sin_done = sem("sin_done")
        roped_ready = sem("roped_ready")
        qk_hi_ready = sem("qk_hi_ready")
        qk_lo_ready = sem("qk_lo_ready")
        v_copied = sem("v_copied")
        scores_ready = sem("scores_ready")
        capped_ready = sem("capped_ready")
        exp_ready = sem("exp_ready")
        probs_ready = sem("probs_ready")
        pv_done = sem("pv_done")
        taken = sem("taken")
        inv_ready = sem("inv_ready")
        y_ready = sem("y_ready")
        y_hi_ready = sem("y_hi_ready")
        y_lo_ready = sem("y_lo_ready")
        out_ready = sem("out_ready")
        x2_ready = sem("x2_ready")

        def seq_rows(dram, b):
            return dram[bass.ds(b * SEQ, SEQ), :].rearrange("(t p) c -> p t c", p=P)

        block = ctx.enter_context(nc.Block())

        @block.sync
        def _(sp):
            def load_norm(b, q):
                at_least(sp, a_ready, b - 1)
                sp.dma_start(xn[:, q], seq_rows(src, b)).then_inc(xn_loaded[q], 16)

            def load_residual(b, q, n):
                at_least(sp, stored[q], 16 * n)
                sp.dma_start(xr[:, q], seq_rows(src, b)).then_inc(xr_loaded[q], 16)

            def store(b, q):
                sp.wait_ge(x2_ready, b + 1)
                sp.dma_start(seq_rows(dst, b), xr[:, q]).then_inc(stored[q], 16)

            for q in range(2):
                load_norm(q, q)
            for q in range(2):
                load_residual(q, q, 0)
            for q in range(2):
                load_norm(q + 2, q)
            with sp.Fori(0, SEQS // 2 - 2) as i:
                for q in range(2):
                    store(i * 2 + q, q)
                    load_residual(i * 2 + (q + 2), q, i + 1)
                    load_norm(i * 2 + (q + 4), q)
            for q in range(2):
                store(SEQS - 4 + q, q)
                load_residual(SEQS - 2 + q, q, SEQS // 2 - 1)
            for q in range(2):
                store(SEQS - 2 + q, q)
            for q in range(2):
                sp.wait_ge(stored[q], 16 * (SEQS // 2))

        @block.tensor
        def _(pe):
            def transposes(b):
                pe.wait_ge(a_ready, b + 1)
                at_least(pe, x2_ready, b - 2)
                for k in range(KC):
                    for t in range(QT):
                        last = nc.tensor.transpose(pj[0][:, k, t * P:(t + 1) * P], a[:, t, k * P:(k + 1) * P], m.ident[:])
                last.then_inc(aT_ready, 1)

            def project(b, q, n):
                bank = pj[PIECE_BANK[n]]
                if n == 0:
                    at_least(pe, v_copied, b)
                    pe.wait_ge(aT_lo_ready, b + 1)
                elif n >= 2:
                    pe.wait_ge(turned_ready, b * PIECES + (1 if n == 2 else 3))
                for c in range(2):
                    for k in range(KC):
                        if n < PIECES:
                            chunk = 2 * ((n - 1) % PIECES) + c
                            last = split_matmul(nc, bank[:, c, :], m.qk_hi[:, k, chunk, :], m.qk_lo[:, k, chunk, :],
                                                aT_hi[:, k, :], aT_lo[:, k, :], k == 0, k == KC - 1)
                        else:
                            at = slice(c * P, (c + 1) * P)
                            last = split_matmul(nc, bank[:, c, :], aT_hi[:, k, at], aT_lo[:, k, at],
                                                m.v_hi[:, k, :], m.v_lo[:, k, :], k == 0, k == KC - 1)
                last.then_inc(piece_ready, 1)

            def score_unit(b, q, u):
                g, t = u // QT, u % QT
                at_least(pe, capped_ready, b * UNITS + u)
                if t == 0:
                    pe.wait_ge(qk_lo_ready, b * PIECES + (2 + g))
                keys = slice(t * P, (t + 1) * P)
                n = REP * (SEQ - t * P)
                for k_part, q_part in ((qk_hi, qk_hi), (qk_lo, qk_hi), (qk_hi, qk_lo)):
                    for j in range(JH):
                        r = slice(j * HD, (j + 1) * HD)
                        last = nc.tensor.matmul(
                            scores[:, j, 0:n].rearrange("p (r s) -> p r s", r=REP), k_part[r, q, 4 + g, keys],
                            q_part[r, q, REP * g:REP * g + REP, t * P:SEQ],
                            start=k_part is qk_hi and q_part is qk_hi, stop=q_part is qk_lo)
                last.then_inc(scores_ready, 1)

            def weighted_values(b, q, u):
                g, t = u // QT, u % QT
                pe.wait_ge(probs_ready, b * UNITS + u + 1)
                if t == 0:
                    at_least(pe, taken, b * GROUPS + g)
                n = REP * (SEQ - t * P)
                for bank, ones in ((den, True), (pv, False)):
                    for j in range(JH):
                        w = m.ones_f[:] if ones else v[:, q, t, (JH * g + j) * HD:(JH * g + j + 1) * HD]
                        out = bank[j * HD:(j + 1) * HD, :].rearrange("p (r s) -> p r s", r=REP)[:, :, t * P:SEQ]
                        last = nc.tensor.matmul(out, w, probs[:, u % 2, j, 0:n].rearrange("p (r s) -> p r s", r=REP),
                                                start=t == 0, stop=t == QT - 1)
                last.then_inc(pv_done, 1)

            def output(b):
                pe.wait_ge(y_lo_ready, b * GROUPS + GROUPS)
                pe.wait_ge(turned_ready, (b + 2) * PIECES + 2 if not isinstance(b, int) else min(
                    (b + 2) * PIECES + 2, SEQS * PIECES))
                for t in range(QT):
                    for g in range(GROUPS):
                        for r in range(REP):
                            at = slice(r * SEQ + t * P, r * SEQ + (t + 1) * P)
                            n = REP * g + r
                            last = split_matmul(nc, pj[0][:, t, :], y_hi[:, g, at], y_lo[:, g, at], m.o_hi[:, n, :],
                                                m.o_lo[:, n, :], n == 0, n == 3)
                last.then_inc(out_ready, 1)

            def slot_of(b, q, behind=True, ahead=True):
                score_unit(b, q, 0)
                if ahead:
                    transposes(b + 1)
                if behind:
                    weighted_values(b - 1, 1 - q, 3)
                if ahead:
                    project(b + 1, 1 - q, 0)
                score_unit(b, q, 1)
                if ahead:
                    project(b + 1, 1 - q, 1)
                weighted_values(b, q, 0)
                score_unit(b, q, 2)
                if ahead:
                    project(b + 1, 1 - q, 2)
                weighted_values(b, q, 1)
                score_unit(b, q, 3)
                if behind:
                    output(b - 1)
                weighted_values(b, q, 2)
                if ahead:
                    project(b + 1, 1 - q, 3)

            transposes(0)
            for n in range(4):
                project(0, 0, n)
            slot_of(0, 0, behind=False)
            with pe.Fori(0, SEQS // 2 - 2) as i:
                for q in range(2):
                    slot_of(i * 2 + (q + 1), 1 - q)
            slot_of(SEQS - 3, 1)
            slot_of(SEQS - 2, 0)
            slot_of(SEQS - 1, 1, ahead=False)
            weighted_values(SEQS - 1, 1, 3)
            output(SEQS - 1)

        @block.scalar
        def _(act):
            def aT_hi_part(b):
                act.wait_ge(aT_ready, b + 1)
                at_least(act, piece_ready, 4 * b)
                nc.scalar.copy(aT_hi[:], pj[0][:]).then_inc(aT_hi_ready, 1)

            def qk_hi_part(b, q, n):
                act.wait_ge(roped_ready, b * PIECES + n + 1)
                at_least(act, scores_ready, UNITS * (b - 1))
                c = 2 * ((n - 1) % PIECES)
                nc.scalar.copy(qk_hi[:, q, c:c + 2, :], roped[:, n]).then_inc(qk_hi_ready, 1)

            def copy_v(b, q):
                act.wait_ge(piece_ready, 4 * b + 4)
                at_least(act, pv_done, UNITS * (b - 1))
                nc.scalar.copy(v[:, q], pj[PIECE_BANK[3]][:]).then_inc(v_copied, 1)

            def cap(b, u):
                act.wait_ge(scores_ready, b * UNITS + u + 1)
                n = REP * (SEQ - u % QT * P)
                at_least(act, exp_ready, b * UNITS + max(u - 1, 0))
                nc.scalar.activation(capped[:, u % 2, :, 0:n], scores[:, :, 0:n], ACT.Tanh,
                                     scale=QK_SCALE / SOFTCAP).then_inc(capped_ready, 1)

            def exponential(b, u):
                act.wait_ge(capped_ready, b * UNITS + u + 1)
                at_least(act, pv_done, b * UNITS + max(u - 1, 0))
                n = REP * (SEQ - u % QT * P)
                nc.scalar.activation(probs[:, u % 2, :, 0:n], capped[:, u % 2, :, 0:n], ACT.Exp,
                                     scale=SOFTCAP).then_inc(exp_ready, 1)

            def take_values(b, g):
                act.wait_ge(pv_done, b * UNITS + QT * (g + 1))
                at_least(act, y_ready, b * GROUPS + (g - 1))
                nc.scalar.copy(den_sb[:, g, :], den[:])
                nc.scalar.copy(pv_sb[:, g, :], pv[:]).then_inc(taken, 1)

            def y_hi_part(b, g):
                act.wait_ge(y_ready, b * GROUPS + g + 1)
                at_least(act, out_ready, b)
                nc.scalar.copy(y_hi[:, g, :], y[:]).then_inc(y_hi_ready, 1)

            def slot_of(b, q, behind=True, ahead=True):
                if ahead:
                    aT_hi_part(b + 1)
                cap(b, 0)
                exponential(b, 0)
                if behind:
                    take_values(b - 1, 1)
                cap(b, 1)
                exponential(b, 1)
                if behind:
                    y_hi_part(b - 1, 1)
                cap(b, 2)
                if ahead:
                    qk_hi_part(b + 1, 1 - q, 0)
                exponential(b, 2)
                take_values(b, 0)
                if ahead:
                    qk_hi_part(b + 1, 1 - q, 1)
                cap(b, 3)
                exponential(b, 3)
                if ahead:
                    qk_hi_part(b + 1, 1 - q, 2)
                    copy_v(b + 1, 1 - q)
                y_hi_part(b, 0)

            aT_hi_part(0)
            for n in range(PIECES):
                qk_hi_part(0, 0, n)
            copy_v(0, 0)
            slot_of(0, 0, behind=False)
            with act.Fori(0, SEQS // 2 - 2) as i:
                for q in range(2):
                    slot_of(i * 2 + (q + 1), 1 - q)
            slot_of(SEQS - 3, 1)
            slot_of(SEQS - 2, 0)
            slot_of(SEQS - 1, 1, ahead=False)
            take_values(SEQS - 1, 1)
            y_hi_part(SEQS - 1, 1)

        @block.gpsimd
        def _(pool):
            def root(b):
                pool.wait_ge(var_ready, b + 1)
                pool.tensor_tensor(rstd[:], var_in[:], m.neg_half[:, 0, 0:QT], ALU.pow).then_inc(rstd_ready, 1)

            def rope(b, n):
                pool.wait_ge(turned_ready, b * PIECES + n + 1)
                at_least(pool, qk_lo_ready, b * PIECES + (n + 1 - PIECES))
                sin = m.sin[:].unsqueeze(1).to_broadcast([P, 2, SEQ])
                pool.tensor_tensor(by_sin[:, n], turned[:, n], sin, ALU.mult).then_inc(sin_done, 1)
                pool.wait_ge(sin_done, b * PIECES + n + 1)
                pool.tensor_tensor(roped[:, n], by_cos[:, n], by_sin[:, n], ALU.add).then_inc(roped_ready, 1)

            def causal(b, u):
                wait_apart(pool, exp_ready, b * UNITS + u + 1, pool_marks)
                n = REP * (SEQ - u % QT * P)
                diag = probs[:, u % 2, :, 0:n].rearrange("p j (r s) -> p j r s", r=REP)[:, :, :, 0:P]
                pool.affine_select(out=diag, in_=diag, compare_op=ALU.is_ge, fill=zero, base=0,
                                   pattern=[[0, JH], [0, REP], [1, P]], channel_multiplier=-1).then_inc(probs_ready, 1)

            def slot_of(b, ahead=True, further=True):
                causal(b, 0)
                causal(b, 1)
                if ahead:
                    rope(b + 1, 0)
                    rope(b + 1, 1)
                if further:
                    root(b + 2)
                causal(b, 2)
                if ahead:
                    rope(b + 1, 2)
                causal(b, 3)

            zero = pool.to_reg(0.0)
            root(0)
            root(1)
            for n in range(PIECES):
                rope(0, n)
            slot_of(0)
            with pool.Fori(0, SEQS // 2 - 2) as i:
                for q in range(2):
                    slot_of(i * 2 + (q + 1))
            slot_of(SEQS - 3)
            slot_of(SEQS - 2, further=False)
            slot_of(SEQS - 1, ahead=False, further=False)

        @block.vector
        def _(dve):
            def statistics(b, q, n):
                dve.wait_ge(xn_loaded[q], 16 * (n + 1))
                for t in range(QT):
                    ins = dve.bn_stats(stats[:, t, :], xn[:, q, t, :])
                ins.then_inc(stat, 1)
                wait_apart(dve, stat, b * 2 + 1, marks)
                for t in range(QT):
                    ins = dve.bn_aggr(moments[:, t, :], stats[:, t, :])
                ins.then_inc(stat, 1)
                dve.wait_ge(stat, b * 2 + 2)
                dve.tensor_scalar(var_in[:], moments[:, :, 1], LN_EPS, None, ALU.add).then_inc(var_ready, 1)

            def normalise(b, q):
                dve.wait_ge(rstd_ready, b + 1)
                at_least(dve, aT_ready, b)
                for t in range(QT):
                    ins = dve.tensor_scalar(a[:, t, :], xn[:, q, t, :], moments[:, t, 0:1], rstd[:, t:t + 1],
                                            ALU.subtract, ALU.mult)
                ins.then_inc(a_ready, 1)

            def aT_lo_part(b):
                dve.wait_ge(aT_hi_ready, b + 1)
                dve.tensor_tensor(aT_lo[:], pj[0][:], aT_hi[:].bitcast(F32), ALU.subtract).then_inc(aT_lo_ready, 1)

            def turn(b, n):
                dve.wait_ge(piece_ready, b * 4 + n + 1)
                at_least(dve, roped_ready, b * PIECES + (n + 1 - PIECES))
                cos = m.cos[:].unsqueeze(1).to_broadcast([P, 2, SEQ])
                bank = pj[PIECE_BANK[n]]
                dve.tensor_tensor(by_cos[:, n], bank[:], cos, ALU.mult)
                dve.stream_shuffle(turned[:, n], bank[:], [(i + HD // 2) % HD for i in range(HD)]).then_inc(turned_ready, 1)

            def qk_lo_part(b, q, n):
                dve.wait_ge(qk_hi_ready, b * PIECES + n + 1)
                c = 2 * ((n - 1) % PIECES)
                dve.tensor_tensor(qk_lo[:, q, c:c + 2, :], roped[:, n], qk_hi[:, q, c:c + 2, :].bitcast(F32),
                                  ALU.subtract).then_inc(qk_lo_ready, 1)

            def invert(b, g):
                dve.wait_ge(taken, b * GROUPS + g + 1)
                dve.reciprocal(inv_den[:], den_sb[:, g, :]).then_inc(inv_ready, 1)

            def divide(b, g):
                dve.wait_ge(inv_ready, b * GROUPS + g + 1)
                at_least(dve, y_hi_ready, b * GROUPS + g)
                dve.tensor_tensor(y[:], pv_sb[:, g, :], inv_den[:], ALU.mult).then_inc(y_ready, 1)

            def y_lo_part(b, g):
                dve.wait_ge(y_hi_ready, b * GROUPS + g + 1)
                dve.tensor_tensor(y_lo[:, g, :], y[:], y_hi[:, g, :].bitcast(F32), ALU.subtract).then_inc(y_lo_ready, 1)

            def residual(b, q, n):
                dve.wait_ge(out_ready, b + 1)
                dve.wait_ge(xr_loaded[q], 16 * (n + 1))
                dve.tensor_tensor(xr[:, q], xr[:, q], pj[0][:], ALU.add).then_inc(x2_ready, 1)

            def slot_of(b, q, n_behind, n_further, behind=True, ahead=True, further=True):
                if ahead:
                    aT_lo_part(b + 1)
                    turn(b + 1, 0)
                if behind:
                    invert(b - 1, 1)
                    divide(b - 1, 1)
                    y_lo_part(b - 1, 1)
                if ahead:
                    turn(b + 1, 1)
                if further:
                    statistics(b + 2, q, n_further)
                if ahead:
                    qk_lo_part(b + 1, 1 - q, 0)
                    turn(b + 1, 2)
                if further:
                    normalise(b + 2, q)
                if ahead:
                    qk_lo_part(b + 1, 1 - q, 1)
                invert(b, 0)
                if ahead:
                    qk_lo_part(b + 1, 1 - q, 2)
                divide(b, 0)
                if behind:
                    residual(b - 1, 1 - q, n_behind)
                y_lo_part(b, 0)

            statistics(0, 0, 0)
            normalise(0, 0)
            statistics(1, 1, 0)
            aT_lo_part(0)
            normalise(1, 1)
            for n in range(PIECES):
                turn(0, n)
                qk_lo_part(0, 0, n)
            slot_of(0, 0, 0, 1, behind=False)
            with dve.Fori(0, SEQS // 2 - 2) as i:
                slot_of(i * 2 + 1, 1, i, i + 1)
                slot_of(i * 2 + 2, 0, i, i + 2)
            slot_of(SEQS - 3, 1, SEQS // 2 - 2, SEQS // 2 - 1)
            slot_of(SEQS - 2, 0, SEQS // 2 - 2, 0, further=False)
            slot_of(SEQS - 1, 1, SEQS // 2 - 1, 0, ahead=False, further=False)
            invert(SEQS - 1, 1)
            divide(SEQS - 1, 1)
            y_lo_part(SEQS - 1, 1)
            residual(SEQS - 1, 1, SEQS // 2 - 1)


def build(nc, ins, out, stages=("r1", "e1", "att", "r2", "e2")):
    m = Memory()
    ctx = ExitStack()
    with ctx:
        def sb(name, shape, dt):
            return ctx.enter_context(nc.sbuf_tensor(name, shape, dt))

        m.gu_hi = sb("gu_hi", [P, KC, GU, P], F32R)
        m.gu_lo = sb("gu_lo", [P, KC, GU, P], F32R)
        m.down_hi = sb("down_hi", [P, MT, C], F32R)
        m.down_lo = sb("down_lo", [P, MT, C], F32R)
        m.router_hi = sb("router_hi", [P, KC, RW], F32R)
        m.router_lo = sb("router_lo", [P, KC, RW], F32R)
        m.qk_hi = sb("qk_hi", [P, KC, 6, P], F32R)
        m.qk_lo = sb("qk_lo", [P, KC, 6, P], F32R)
        m.v_hi = sb("v_hi", [P, KC, C], F32R)
        m.v_lo = sb("v_lo", [P, KC, C], F32R)
        m.o_hi = sb("o_hi", [P, 4, C], F32R)
        m.o_lo = sb("o_lo", [P, 4, C], F32R)
        m.w_norm = sb("w_norm", [P, KC], F32)
        m.cos = sb("cos", [P, SEQ], F32)
        m.sin = sb("sin", [P, SEQ], F32)
        m.ident = sb("ident", [P, P], F32)
        m.before = sb("before", [P, P], BF16)
        m.ones_b = sb("ones_b", [P, P], BF16)
        m.ones_f = sb("ones_f", [P, HD], F32)
        m.neg_half = sb("neg_half", [P, 2, TJ], F32)
        m.iota_e = sb("iota_e", [P, E], F32)
        m.tok_f = sb("tok_f", [P, 2, TJ * TOPK], F32)
        m.z_rows = nc.dram_tensor("z_rows", [T + PAD, C], F32, kind="Internal").ap()
        m.acc1 = nc.dram_tensor("acc1", [T + PAD, C], F32, kind="Internal").ap()
        m.x2 = nc.dram_tensor("x2", [T, C], F32, kind="Internal").ap()
        m.acc2 = out
        m.table1 = nc.dram_tensor("table1", [E * CAP, 2], I32, kind="Internal").ap()
        m.table2 = nc.dram_tensor("table2", [E * CAP, 2], I32, kind="Internal").ap()

        setup(nc, m, ins)
        m.turn = 0
        if stages == "att":
            with nc.semaphore("prep") as prep, nc.Block() as block:
                w = AttentionWeights(nc, m, ins, sb, lambda name: ctx.enter_context(nc.semaphore(name)))
                block.sync(lambda sp: w.load(sp))
                block.scalar(lambda act: w.high_parts(act))
                block.vector(lambda dve: w.low_parts(dve))
            attention(nc, m, ins["X"], m.acc2[0:T, :])
            return
        if stages == "ffn":
            route_and_shared(nc, m, "f1", ins["X"], m.acc2, m.table1, ins)
            experts(nc, m, "e1", m.acc2, m.table1, ins)
            return
        route_and_shared(nc, m, "f1", ins["X"], m.acc1, m.table1, ins)
        experts(nc, m, "e1", m.acc1, m.table1, ins, attention_next=True)
        attention(nc, m, m.acc1, m.x2)
        m.turn = 1
        route_and_shared(nc, m, "f2", m.x2, m.acc2, m.table2)
        experts(nc, m, "e2", m.acc2, m.table2, ins)


NAMES = {"X": "L0_attn_X", "Wq": "L0_attn_Wq", "Wk": "L0_attn_Wk", "Wv": "L0_attn_Wv", "Wo": "L0_attn_Wo",
         "w_norm": "L0_ffn_w_norm", "w_router": "L0_ffn_w_router", "w_gate": "L0_ffn_w_gate",
         "w_up": "L0_ffn_w_up", "w_down": "L0_ffn_w_down", "sw_gate": "L0_ffn_sw_gate",
         "sw_up": "L0_ffn_sw_up", "sw_down": "L0_ffn_sw_down", "w_sgate": "L0_ffn_w_shared_gate"}


def rotary_tables():
    inv_freq = (np.float32(1.0) / np.float32(10000.0) ** (np.arange(0, HD, 2, dtype=np.float32) / np.float32(HD)))
    freqs = np.arange(SEQ, dtype=np.float32)[:, None] * inv_freq.astype(np.float32)[None, :]
    angle = np.tile(np.concatenate((freqs, freqs), axis=-1).T, (P // HD, 1))
    sign = np.tile(np.repeat(np.array([-1.0, 1.0], np.float32), HD // 2), P // HD)[:, None]
    return np.cos(angle).astype(np.float32), (np.sin(angle) * sign).astype(np.float32)


def kernel(**inputs):
    import concourse.bacc as bacc
    from concourse.bass_utils import run_bass_kernel_spmd

    nc = bacc.Bacc("TRN2", target_bir_lowering=False, num_devices=1)
    arrays = {name: np.ascontiguousarray(inputs[of]) for name, of in NAMES.items()}
    arrays["X"] = arrays["X"].reshape(T, C)
    arrays["cos"], arrays["sin"] = rotary_tables()
    ins = {name: nc.dram_tensor(f"in_{name}", a.shape, mybir.dt.from_np(a.dtype), kind="ExternalInput").ap()
           for name, a in arrays.items()}
    out = nc.dram_tensor("out", [T + PAD, C], F32, kind="ExternalOutput").ap()
    build(nc, ins, out)
    result = run_bass_kernel_spmd(nc, [{f"in_{name}": a for name, a in arrays.items()}], core_ids=[0])
    return result.results[0]["out"][:T].reshape(SEQS, SEQ, C)
```

```python
from contextlib import ExitStack

import numpy as np

import concourse.bass as bass
from concourse import mybir

P = 128
F32 = mybir.dt.float32
F32R = mybir.dt.float32r
BF16 = mybir.dt.bfloat16
I32 = mybir.dt.int32
U32 = mybir.dt.uint32
ALU = mybir.AluOpType
ACT = mybir.ActivationFunctionType
AX = mybir.AxisListType

SEQS, SEQ, C = 16, 256, 256
T = SEQS * SEQ
KC = C // P
HEADS, KV_HEADS, HD = 16, 8, 32
REP = HEADS // KV_HEADS
E, TOPK, FE = 32, 4, 176
FS = 704
CAP = 128
LN_EPS, RMS_EPS = 1e-5, 1e-6
BLK = 512
NB = T // BLK
TJ = BLK // P
MT = 6
LAST = FS - 5 * P
GU = 2 * MT - 1
RW = E + 2
PAD = P
NO_SLOT = float(2 * E * CAP)
UNDERFLOW = -104.0
SOFTCAP = 50.0
QK_SCALE = 256.0 ** -0.5
FD = FE // 2


class Memory:
    pass


CREDIT = 1


def at_least(engine, sem, value, credit=0):
    if isinstance(value, int) and value <= 0:
        return
    engine.wait_ge(sem, value + credit)


def give_credit(engine, *sems):
    for sem in sems:
        engine.sem_inc(sem, CREDIT)


def wait_apart(engine, sem, value, marks):
    engine.wait_ge(sem, value)
    engine.sem_inc(marks, 1)


def split_matmul(nc, out, w_hi, w_lo, x_hi, x_lo, first, last):
    nc.tensor.matmul(out, w_hi, x_hi, start=first, stop=False)
    nc.tensor.matmul(out, w_lo, x_hi, start=False, stop=False)
    return nc.tensor.matmul(out, w_hi, x_lo, start=False, stop=last)


class SharedWeights:

    def __init__(self, nc, m, ins, sb, sem):
        self.ins, self.m, self.nc = ins, m, nc
        self.gate = sb("raw_gate", [P, KC, FS], F32)
        self.up = sb("raw_up", [P, KC, FS], F32)
        self.down = sb("raw_down", [P, MT, C], F32)
        self.gu_loaded = sem("raw_gu_loaded")
        self.down_loaded = sem("raw_down_loaded")
        self.hi_made = sem("shared_hi_made")
        self.lo_made = sem("shared_lo_made")
        self.gu_splits, self.down_splits = [], []
        g, u = self.gate[:], self.up[:]
        for c in range(GU):
            mt = c // 2
            if mt < MT - 1:
                src = (g, u)[c % 2][:, :, mt * P:(mt + 1) * P]
                self.gu_splits.append((m.gu_hi[:, :, c, :], m.gu_lo[:, :, c, :], src))
            else:
                for half, src in enumerate((g, u)):
                    at = slice(half * LAST, (half + 1) * LAST)
                    self.gu_splits.append((m.gu_hi[:, :, c, at], m.gu_lo[:, :, c, at], src[:, :, mt * P:FS]))
        self.down_splits.append((m.down_hi[:, 0:MT - 1, :], m.down_lo[:, 0:MT - 1, :], self.down[:, 0:MT - 1, :]))
        self.down_splits.append((m.down_hi[0:LAST, MT - 1, :], m.down_lo[0:LAST, MT - 1, :],
                                 self.down[0:LAST, MT - 1, :]))
        self.total = len(self.gu_splits) + len(self.down_splits)

    def load(self, sp):
        sp.dma_start(self.gate[:], self.ins["sw_gate"].rearrange("(k p) f -> p k f", p=P)).then_inc(self.gu_loaded, 16)
        sp.dma_start(self.up[:], self.ins["sw_up"].rearrange("(k p) f -> p k f", p=P)).then_inc(self.gu_loaded, 16)
        sp.dma_start(self.down[:, 0:MT - 1, :], self.ins["sw_down"][0:(MT - 1) * P, :].rearrange("(c p) n -> p c n", p=P)
                     ).then_inc(self.down_loaded, 16)
        sp.dma_start(self.down[0:LAST, MT - 1, :], self.ins["sw_down"][(MT - 1) * P:FS, :]).then_inc(self.down_loaded, 16)

    def high_parts(self, act):
        act.wait_ge(self.gu_loaded, 32)
        for hi, lo, raw in self.gu_splits:
            act.copy(hi, raw).then_inc(self.hi_made, 1)
        act.wait_ge(self.down_loaded, 32)
        for hi, lo, raw in self.down_splits:
            act.copy(hi, raw).then_inc(self.hi_made, 1)

    def low_parts(self, dve, splits, done):
        for n, (hi, lo, raw) in enumerate(splits):
            dve.wait_ge(self.hi_made, done + n + 1)
            dve.tensor_tensor(lo, raw, hi.bitcast(F32), ALU.subtract).then_inc(self.lo_made, 1)


class AttentionWeights:

    def __init__(self, nc, m, ins, sb, sem):
        self.ins, self.m = ins, m
        self.q = sb("raw_q", [P, KC, HEADS * HD], F32)
        self.k = sb("raw_k", [P, KC, KV_HEADS * HD], F32)
        self.v = sb("raw_v", [P, KC, KV_HEADS * HD], F32)
        self.o = sb("raw_o", [P, 4, C], F32)
        self.loaded = sem("attention_loaded")
        self.hi_made = sem("attention_hi_made")
        self.splits = []
        for k in range(KC):
            for group in range(2):
                for r in range(REP):
                    q = self.q[:, k, :].rearrange("p (g j r d) -> p g r j d", g=2, r=REP, d=HD)[:, group, r]
                    n = REP * group + r
                    hi = m.qk_hi[:, k, n, :].rearrange("p (j d) -> p j d", d=HD)
                    lo = m.qk_lo[:, k, n, :].rearrange("p (j d) -> p j d", d=HD)
                    self.splits.append((hi, lo, q))
            kk = self.k[:, k, :].rearrange("p (n c) -> p n c", n=2)
            self.splits.append((m.qk_hi[:, k, 4:6, :], m.qk_lo[:, k, 4:6, :], kk))
        self.splits.append((m.v_hi[:], m.v_lo[:], self.v[:]))
        self.splits.append((m.o_hi[:], m.o_lo[:], self.o[:]))

    def load(self, sp):
        loads = [(self.q[:], self.ins["Wq"].rearrange("(k p) n -> p k n", p=P)),
                 (self.k[:], self.ins["Wk"].rearrange("(k p) n -> p k n", p=P)),
                 (self.v[:], self.ins["Wv"].rearrange("(k p) n -> p k n", p=P)),
                 (self.m.cos[:], self.ins["cos"]),
                 (self.m.sin[:], self.ins["sin"])]
        wo = self.ins["Wo"].rearrange("(g j r d) n -> g r j d n", g=2, r=REP, d=HD)
        for group in range(2):
            for r in range(REP):
                for j in range(4):
                    loads.append((self.o[j * HD:(j + 1) * HD, REP * group + r, :], wo[group, r, j]))
        for dst, src in loads:
            sp.dma_start(dst, src).then_inc(self.loaded, 16)
        self.n_loads = len(loads)

    def high_parts(self, act):
        act.wait_ge(self.loaded, 16 * self.n_loads)
        for hi, lo, raw in self.splits:
            act.copy(hi, raw).then_inc(self.hi_made, 1)

    def low_parts(self, dve):
        for n, (hi, lo, raw) in enumerate(self.splits):
            dve.wait_ge(self.hi_made, n + 1)
            dve.tensor_tensor(lo, raw, hi.bitcast(F32), ALU.subtract)


class Front:

    def __init__(self, nc, m, src, sb, sem):
        self.m, self.src = m, src
        self.x = sb("x", [P, 2, TJ, C], F32)
        self.moments = sb("moments", [P, 2, TJ, 2], F32)
        self.var_in = sb("var_in", [P, 2, 2, TJ], F32)
        self.rstd = sb("rstd", [P, 2, 2, TJ], F32)
        self.stats = sb("stats", [P, TJ, 6], F32)
        self.x_loaded = [sem("x_loaded0"), sem("x_loaded1")]
        self.stat = sem("stat")
        self.marks = sem("marks")
        self.vars_ready = sem("vars_ready")
        self.rstd_ready = sem("rstd_ready")
        self.steps, self.base = 0, 0

    def load(self, sp, b, q):
        sp.dma_start(self.x[:, q], self.src[bass.ds(b * BLK, BLK), :].rearrange("(j p) c -> p j c", p=P)
                     ).then_inc(self.x_loaded[q], 16)

    def step(self, dve, ins, apart=False):
        ins.then_inc(self.stat, 1)
        self.steps += 1
        if apart:
            wait_apart(dve, self.stat, self.base + self.steps, self.marks)
        else:
            dve.wait_ge(self.stat, self.base + self.steps)

    def statistics(self, dve, b, q, n):
        dve.wait_ge(self.x_loaded[q], 16 * (n + 1))
        for j in range(TJ):
            ins = dve.bn_stats(self.stats[:, j, :], self.x[:, q, j, :])
        self.step(dve, ins, apart=True)
        for j in range(TJ):
            ins = dve.bn_aggr(self.moments[:, q, j, :], self.stats[:, j, :])
        self.step(dve, ins)
        var, var_in = self.moments[:, q, :, 1], self.var_in
        self.step(dve, dve.tensor_scalar(var_in[:, q, 0, :], var, LN_EPS, None, ALU.add))
        self.step(dve, dve.reciprocal(var_in[:, q, 1, :], var_in[:, q, 0, :]))
        self.step(dve, dve.tensor_tensor(var_in[:, q, 1, :], var_in[:, q, 1, :], var, ALU.mult))
        dve.tensor_scalar(var_in[:, q, 1, :], var_in[:, q, 1, :], RMS_EPS, None, ALU.add).then_inc(self.vars_ready, 1)

    def roots(self, pool, b, q):
        pool.wait_ge(self.vars_ready, b + 1)
        pool.tensor_tensor(self.rstd[:, q], self.var_in[:, q], self.m.neg_half[:], ALU.pow).then_inc(self.rstd_ready, 1)


class ExpertInputs:

    def __init__(self, nc, m, table, ins, sb, sem):
        self.ins, self.table = ins, table
        self.w_gu = sb("w_gu", [P, 2, 2, KC, 2, FE], F32)
        self.w_down = sb("w_down", [FD, 2, 2, 2, C], F32)
        self.slots = sb("slots", [P, E, 2], I32)
        self.base = sb("base", [P, 2, TJ, C], F32)
        self.pool_marks = sem("pool_marks")
        self.table_loaded = sem("table_loaded")
        self.gu_loaded = [sem("gu_loaded0"), sem("gu_loaded1")]
        self.down_loaded = [sem("down_loaded0"), sem("down_loaded1")]
        self.acc_stored = [sem("acc_stored0"), sem("acc_stored1")]

    def load_gate_up(self, sp, p, q):
        for half, name in enumerate(("w_gate", "w_up")):
            for s in range(2):
                sp.dma_start(self.w_gu[:, q, s, :, half, :],
                             self.ins[name][bass.ds(p * 2 + s, 1), :, :].rearrange("a (k p) f -> p (a k) f", p=P)
                             ).then_inc(self.gu_loaded[q], 16)

    def load_down(self, sp, p, q):
        for s in range(2):
            sp.dma_start(self.w_down[:, q, s, :, :],
                         self.ins["w_down"][bass.ds(p * 2 + s, 1), :, :].rearrange("a (k p) n -> p (a k) n", p=FD)
                         ).then_inc(self.down_loaded[q], 16)

    def load_slots(self, sp):
        sp.dma_start(self.slots[:], self.table.rearrange("(c e) w -> c e w", e=E)).then_inc(self.table_loaded, 16)


def setup(nc, m, ins, front, weights):
    ctx = ExitStack()
    with ctx:
        def sb(name, shape, dt):
            return ctx.enter_context(nc.sbuf_tensor(name, shape, dt))

        def sem(name):
            return ctx.enter_context(nc.semaphore(name))

        raw_router = sb("raw_router", [P, KC, RW], F32)
        zeros = m.zeros
        empty = sb("empty", [P, E, 2], I32)
        iota_i = sb("iota_i", [P, E], I32)
        tok_i = sb("tok_i", [P, TJ * TOPK], I32)
        loaded = sem("setup_loaded")
        made = sem("setup_made")
        cleared = sem("setup_cleared")
        hi_made = sem("setup_hi_made")

        with nc.Block() as block:
            @block.sync
            def _(sp):
                sp.wait_ge(made, 1)
                sp.dma_start(raw_router[:, :, 0:E], ins["w_router"].rearrange("(k p) n -> p k n", p=P)).then_inc(loaded, 16)
                sp.dma_start(raw_router[:, :, E:E + 1], ins["w_sgate"].rearrange("(k p) n -> p k n", p=P),
                             allow_slow_non_contiguous=True).then_inc(loaded, 16)
                for k in range(KC):
                    sp.dma_start(m.w_norm[:, k:k + 1], ins["w_norm"][k * P:(k + 1) * P].rearrange("(p a) -> p a", a=1),
                                 allow_slow_non_contiguous=True).then_inc(loaded, 16)
                front.load(sp, 0, 0)
                sp.wait_ge(made, 4)
                for rows in (m.z_rows, m.acc1, m.odd1, m.acc2):
                    sp.dma_start(rows[T:T + PAD, :], zeros[:]).then_inc(cleared, 16)
                for table in (m.table1, m.table2):
                    sp.dma_start(table.rearrange("(c e) w -> c e w", e=E), empty[:]).then_inc(cleared, 16)
                weights.load(sp)
                front.load(sp, 1, 1)
                sp.wait_ge(cleared, 6 * 16)
                sp.wait_ge(loaded, (2 + KC) * 16)

            @block.gpsimd
            def _(pool):
                pool.memset(raw_router[:], 0.0).then_inc(made, 1)
                pool.memset(zeros[:], 0.0).then_inc(made, 1)
                pool.iota(empty[:, :, 0], [[0, E]], base=T, channel_multiplier=1).then_inc(made, 1)
                pool.memset(empty[:, :, 1], 0).then_inc(made, 1)
                pool.iota(iota_i[:], [[1, E]], base=0, channel_multiplier=0).then_inc(made, 1)
                pool.iota(tok_i[:].rearrange("p (j k) -> p j k", k=TOPK), [[P, TJ], [0, TOPK]], base=0,
                          channel_multiplier=1).then_inc(made, 1)
                pool.memset(m.ident[:], 0.0).then_inc(made, 1)
                pool.memset(m.before[:], 1.0).then_inc(made, 1)
                pool.memset(m.neg_half[:], -0.5).then_inc(made, 1)
                pool.memset(m.ones_b[:], 1.0)
                pool.memset(m.ones_f[:], 1.0)
                pool.wait_ge(made, 9)
                pool.affine_select(out=m.ident[:], in_=m.ident[:], compare_op=ALU.not_equal, fill=1.0, base=0,
                                   pattern=[[-1, P]], channel_multiplier=1)
                pool.affine_select(out=m.before[:], in_=m.before[:], compare_op=ALU.is_gt, fill=0.0, base=0,
                                   pattern=[[1, P]], channel_multiplier=-1)
                front.roots(pool, 0, 0)

            @block.scalar
            def _(act):
                act.wait_ge(loaded, (2 + KC) * 16)
                act.copy(m.router_hi[:], raw_router[:]).then_inc(hi_made, 1)

            @block.vector
            def _(dve):
                dve.wait_ge(made, 6)
                dve.tensor_copy(m.iota_e[:], iota_i[:])
                for n in range(2):
                    dve.tensor_copy(m.tok_f[:, n, :], tok_i[:])
                dve.wait_ge(hi_made, 1)
                dve.tensor_tensor(m.router_lo[:], raw_router[:], m.router_hi[:].bitcast(F32), ALU.subtract)
                front.statistics(dve, 0, 0, 0)


def route_and_shared(nc, m, tag, acc, table, front, experts_in, weights=None, odd=None):
    ctx = ExitStack()
    with ctx:
        def sb(name, shape, dt):
            return ctx.enter_context(nc.sbuf_tensor(f"{name}_{tag}", shape, dt))

        def psum(name, shape):
            return ctx.enter_context(nc.psum_tensor(f"{name}_{tag}", shape, F32))

        def sem(name):
            return ctx.enter_context(nc.semaphore(f"{name}_{tag}"))

        x, moments, rstd = front.x, front.moments, front.rstd
        h = sb("h", [P, TJ, C], F32)
        warm = sb("warm", [P, 1], F32)
        z = sb("z", [P, 2, TJ, C], F32)
        base = experts_in.base
        x_hi = sb("x_hi", [P, 2, KC, BLK], F32R)
        x_lo = sb("x_lo", [P, 2, KC, BLK], F32R)
        row_max = sb("row_max", [P, TJ], F32)
        d = sb("d", [P, TJ, E], F32)
        top = sb("top", [P, TJ, 8], F32)
        top_at = sb("top_at", [P, TJ, 8], U32)
        top_f = sb("top_f", [P, TJ, TOPK], F32)
        chosen = sb("chosen", [P, TJ * TOPK, E], F32)
        mask = sb("mask", [P, TJ, E], BF16)
        mask_sum = sb("mask_sum", [P, E], F32)
        seen = sb("seen", [P, E], BF16)
        exps = sb("exps", [P, TJ, E], F32)
        exp_top = sb("exp_top", [P, TJ, 8], F32)
        gate_in = sb("gate_in", [P, TJ], F32)
        exp_gate = sb("exp_gate", [P, TJ], F32)
        total = sb("total", [P, TJ], F32)
        inv_total = sb("inv_total", [P, TJ], F32)
        gate_den = sb("gate_den", [P, TJ], F32)
        half_gate = sb("half_gate", [P, 2, TJ], F32)
        past = sb("past", [P, TJ, E], F32)
        place = sb("place", [P, TJ, E], F32)
        place_all = sb("place_all", [P, TJ, E], F32)
        picked = sb("picked", [P, TJ * TOPK, E], F32)
        slot_f = sb("slot_f", [P, TJ * TOPK], F32)
        slot = sb("slot", [P, 2, TJ * TOPK], I32)
        entry = sb("entry", [P, 2, TJ * TOPK, 2], I32)
        silu = sb("silu", [P, 2, BLK], F32)
        act_gu = sb("act_gu", [P, 2, BLK], F32)
        a_hi = sb("a_hi", [P, MT, BLK], F32R)
        a_lo = sb("a_lo", [P, MT, BLK], F32R)

        zT = [psum(f"zT{k}", [P, BLK]) for k in range(KC)]
        small = psum("small", [P, BLK])
        logits = small[:, 0:TJ * RW].rearrange("p (j e) -> p j e", e=RW)
        pos = small[:, 256:256 + TJ * E].rearrange("p (j e) -> p j e", e=E)
        gu = [psum(f"gu{n}", [P, BLK]) for n in range(3)]
        down = [psum(f"down{n}", [P, 2, C]) for n in range(2)]

        pool_marks = experts_in.pool_marks
        rstd_ready = front.rstd_ready
        h_ready = sem("h_ready")
        base_ready = sem("base_ready")
        z_ready = sem("z_ready")
        z_stored = [sem("z_stored0"), sem("z_stored1")]
        zT_ready = sem("zT_ready")
        hi_ready = sem("hi_ready")
        lo_ready = sem("lo_ready")
        logits_ready = sem("logits_ready")
        top_ready = sem("top_ready")
        mask_ready = sem("mask_ready")
        exps_ready = sem("exps_ready")
        pos_ready = sem("pos_ready")
        pos_used = sem("pos_used")
        entry_ready = sem("entry_ready")
        warmed = sem("warmed")
        scattered = [sem("scattered0"), sem("scattered1")]
        gu_ready = sem("gu_ready")
        silu_ready = sem("silu_ready")
        prod_ready = sem("prod_ready")
        a_hi_ready = sem("a_hi_ready")
        a_lo_ready = sem("a_lo_ready")
        down_ready = sem("down_ready")
        out_ready = sem("out_ready")
        out_stored = experts_in.acc_stored
        base_free = sem("base_free")
        odd_cleared = sem("odd_cleared") if odd is not None else None

        def rows(b):
            return bass.ds(b * BLK, BLK)

        block = ctx.enter_context(nc.Block())

        @block.sync
        def _(sp):
            def load(b, q):
                sp.wait_ge(base_ready, TJ * (b - 1))
                front.load(sp, b, q)

            def z_has_been_stored(q, n):
                sp.wait_ge(z_stored[q], 16 * n)

            def free_base(q, n):
                sp.wait_ge(out_stored[q], 16 * n)
                sp.sem_inc(base_free, 1)

            def store_z(b, q):
                sp.wait_ge(z_ready, TJ * (b + 1))
                sp.dma_start(m.z_rows[rows(b), :].rearrange("(j p) c -> p j c", p=P), z[:, q]).then_inc(z_stored[q], 16)

            def store_out(b, q):
                sp.wait_ge(out_ready, CREDIT + TJ * (b + 1))
                sp.dma_start(acc[rows(b), :].rearrange("(j p) c -> p j c", p=P), base[:, q]).then_inc(out_stored[q], 16)

            def clear_odd(b):
                if odd is not None:
                    sp.dma_start(odd[rows(b), :].rearrange("(j p) c -> p j c", p=P),
                                 m.zeros[:].unsqueeze(1).to_broadcast([P, TJ, C])).then_inc(odd_cleared, 16)

            give_credit(sp, base_free)
            store_z(0, 0)
            with sp.Fori(0, NB // 2 - 1) as i:
                for q in range(2):
                    b = i * 2 + q
                    z_has_been_stored(q, i + 1)
                    load(b + 2, q)
                    store_z(b + 1, 1 - q)
                    store_out(b, q)
                    clear_odd(b)
                    free_base(q, i + 1)
            store_z(NB - 1, 1)
            clear_odd(NB - 2)
            clear_odd(NB - 1)
            store_out(NB - 2, 0)
            for q in range(2):
                experts_in.load_gate_up(sp, q, q)
                experts_in.load_down(sp, q, q)
            for q in range(2):
                sp.wait_ge(scattered[q], 16 * TJ * TOPK * (NB // 2))
            experts_in.load_slots(sp)
            store_out(NB - 1, 1)
            for q in range(2):
                sp.wait_ge(z_stored[q], 16 * (NB // 2))
            if odd is not None:
                sp.wait_ge(odd_cleared, 16 * NB)

        @block.gpsimd
        def _(pool):
            def roots(b, q, n):
                at_least(pool, scattered[q], 16 * TJ * TOPK * n)
                front.roots(pool, b, q)

            def scatter(b, q):
                wait_apart(pool, entry_ready, b + 1, pool_marks)
                for n in range(TJ * TOPK):
                    pool.indirect_dma_start(
                        out=table, out_offset=bass.IndirectOffsetOnAxis(ap=slot[:, q, n:n + 1], axis=0),
                        in_=entry[:, q, n, :], in_offset=None, bounds_check=last_slot, oob_is_err=False,
                    ).then_inc(scattered[q], 16)

            last_slot = pool.to_reg(E * CAP - 1)
            front.roots(pool, 1, 1)
            scatter(0, 0)
            with pool.Fori(0, NB // 2 - 1) as i:
                for q in range(2):
                    b = i * 2 + q
                    roots(b + 2, q, i + 1)
                    scatter(b + 1, 1 - q)
            scatter(NB - 1, 1)
            for q in range(2):
                pool.wait_ge(scattered[q], 16 * TJ * TOPK * (NB // 2))

        @block.tensor
        def _(pe):
            def transposes(b, q):
                pe.wait_ge(z_ready, TJ * (b + 1))
                at_least(pe, lo_ready, KC * b)
                for k in range(KC):
                    for j in range(TJ):
                        last = nc.tensor.transpose(zT[k][:, j * P:(j + 1) * P], z[:, q, j, k * P:(k + 1) * P], m.ident[:])
                    last.then_inc(zT_ready, 1)

            def router(b, q):
                pe.wait_ge(lo_ready, KC * (b + 1))
                at_least(pe, pos_used, b)
                for j in range(TJ):
                    for k in range(KC):
                        at = slice(j * P, (j + 1) * P)
                        last = split_matmul(nc, logits[:, j, :], x_hi[:, q, k, at], x_lo[:, q, k, at],
                                            m.router_hi[:, k, :], m.router_lo[:, k, :], k == 0, k == KC - 1)
                last.then_inc(logits_ready, 1)

            def positions(b):
                pe.wait_ge(mask_ready, b + 1)
                for j in range(TJ):
                    nc.tensor.matmul(pos[:, j, :], m.before[:], mask[:, j, :], start=True, stop=False)
                    for i in range(j):
                        nc.tensor.matmul(pos[:, j, :], m.ones_b[:], mask[:, i, :], start=False, stop=False)
                    last = nc.tensor.matmul(pos[:, j, :], m.ones_b[:], seen[:], start=False, stop=True)
                last.then_inc(pos_ready, 1)

            def gate_up(b, q, c):
                if c < 3:
                    at_least(pe, prod_ready, MT * b, CREDIT)
                elif c % 2:
                    pe.wait_ge(silu_ready, b * MT + (c - 3) // 2 + 1)
                else:
                    pe.wait_ge(prod_ready, CREDIT + b * MT + (c - 3) // 2 + 1)
                for k in range(KC):
                    last = split_matmul(nc, gu[c % 3][:], m.gu_hi[:, k, c, :], m.gu_lo[:, k, c, :],
                                        x_hi[:, q, k, :], x_lo[:, q, k, :], k == 0, k == KC - 1)
                last.then_inc(gu_ready, 1)

            def down_proj(b, j):
                at_least(pe, out_ready, TJ * b, CREDIT)
                for mt in range(MT):
                    if j == 0:
                        pe.wait_ge(a_lo_ready, CREDIT + b * MT + mt + 1)
                    rows_ = slice(0, P if mt < MT - 1 else LAST)
                    at = slice(j * P, (j + 1) * P)
                    last = split_matmul(nc, down[j // 2][:, j % 2, :], a_hi[rows_, mt, at], a_lo[rows_, mt, at],
                                        m.down_hi[rows_, mt, :], m.down_lo[rows_, mt, :], mt == 0, mt == MT - 1)
                last.then_inc(down_ready, 1)

            def slot_of(b, q, ahead):
                for c in range(GU):
                    gate_up(b, q, c)
                    if ahead and c == 6:
                        transposes(b + 1, 1 - q)
                if ahead:
                    router(b + 1, 1 - q)
                for j in range(TJ):
                    down_proj(b, j)
                    if ahead and j == 2:
                        positions(b + 1)

            give_credit(pe, zT_ready, gu_ready, down_ready)
            transposes(0, 0)
            router(0, 0)
            positions(0)
            if weights:
                pe.wait_ge(weights.lo_made, weights.total)
            with pe.Fori(0, NB // 2 - 1) as i:
                for q in range(2):
                    slot_of(i * 2 + q, q, True)
            slot_of(NB - 2, 0, True)
            slot_of(NB - 1, 1, False)

        @block.scalar
        def _(act):
            def scale_z(b, q):
                for j in range(TJ):
                    act.wait_ge(h_ready, b * TJ + j + 1)
                    if j == 0:
                        at_least(act, zT_ready, KC * (b - 1), CREDIT)
                    nc.scalar.activation(z[:, q, j, :], h[:, j, :], ACT.Copy, scale=rstd[:, q, 1, j:j + 1]).then_inc(z_ready, 1)

            def x_hi_parts(b, q):
                for k in range(KC):
                    act.wait_ge(zT_ready, CREDIT + b * KC + k + 1)
                    if k == 0:
                        at_least(act, gu_ready, GU * (b - 1), CREDIT)
                    nc.scalar.activation(x_hi[:, q, k, :], zT[k][:], ACT.Copy, scale=m.w_norm[:, k:k + 1]).then_inc(hi_ready, 1)

            def silu_of(b, mt):
                act.wait_ge(gu_ready, CREDIT + b * GU + 2 * mt + 1)
                at_least(act, prod_ready, b * MT + max(mt - 1, 0), CREDIT)
                c = 2 * mt
                if mt < MT - 1:
                    nc.scalar.activation(silu[:, mt % 2, :], gu[c % 3][:], ACT.Silu).then_inc(silu_ready, 1)
                else:
                    nc.scalar.activation(silu[LAST:P, mt % 2, :], gu[c % 3][0:LAST, :], ACT.Silu).then_inc(silu_ready, 1)

            def a_hi_part(b, mt):
                act.wait_ge(prod_ready, CREDIT + b * MT + mt + 1)
                at_least(act, down_ready, TJ * b, CREDIT)
                r = slice(0, P if mt < MT - 1 else LAST)
                nc.scalar.copy(a_hi[r, mt, :], act_gu[r, mt % 2, :]).then_inc(a_hi_ready, 1)

            def exponentials(b):
                act.wait_ge(top_ready, b + 1)
                at_least(act, entry_ready, b)
                nc.scalar.activation(exps[:], d[:], ACT.Exp).then_inc(exps_ready, 1)
                nc.scalar.activation(exp_top[:], top[:], ACT.Exp).then_inc(exps_ready, 1)
                nc.scalar.activation(exp_gate[:], gate_in[:], ACT.Exp, scale=-1.0).then_inc(exps_ready, 1)
                at_least(act, warmed, b)
                nc.scalar.activation(warm[:], m.w_norm[:, 0:1], ACT.Silu).then_inc(warmed, 1)

            def slot_of(b, q, ahead):
                silu_of(b, 0)
                for mt in range(1, MT):
                    silu_of(b, mt)
                    if ahead and mt == 1:
                        scale_z(b + 1, 1 - q)
                    a_hi_part(b, mt - 1)
                    if ahead and mt == 2:
                        x_hi_parts(b + 1, 1 - q)
                a_hi_part(b, MT - 1)
                if ahead:
                    exponentials(b + 1)

            give_credit(act, a_hi_ready)
            scale_z(0, 0)
            x_hi_parts(0, 0)
            if weights:
                weights.high_parts(act)
            exponentials(0)
            with act.Fori(0, NB // 2 - 1) as i:
                for q in range(2):
                    slot_of(i * 2 + q, q, True)
            slot_of(NB - 2, 0, True)
            slot_of(NB - 1, 1, False)

        @block.vector
        def _(dve):
            def step(ins, apart=False):
                front.step(dve, ins, apart)

            def normalise(b, q):
                dve.wait_ge(rstd_ready, b + 1)
                at_least(dve, z_ready, TJ * b)
                for j in range(TJ):
                    dve.tensor_scalar(h[:, j, :], x[:, q, j, :], moments[:, q, j, 0:1], rstd[:, q, 0, j:j + 1],
                                      ALU.subtract, ALU.mult).then_inc(h_ready, 1)

            def make_base(b, q):
                at_least(dve, base_free, b - 1, CREDIT)
                dve.wait_ge(h_ready, TJ * (b + 1))
                for j in range(TJ):
                    dve.scalar_tensor_tensor(out=base[:, q, j, :], in0=h[:, j, :], scalar=0.5, in1=x[:, q, j, :],
                                             op0=ALU.mult, op1=ALU.add).then_inc(base_ready, 1)

            def x_lo_parts(b, q):
                for k in range(KC):
                    dve.wait_ge(hi_ready, b * KC + k + 1)
                    dve.scalar_tensor_tensor(out=x_lo[:, q, k, :], in0=zT[k][:], scalar=m.w_norm[:, k:k + 1],
                                             in1=x_hi[:, q, k, :].bitcast(F32), op0=ALU.mult,
                                             op1=ALU.subtract).then_inc(lo_ready, 1)

            def top_experts(b):
                dve.wait_ge(logits_ready, b + 1)
                at_least(dve, exps_ready, 3 * b)
                dve.tensor_scalar(gate_in[:], logits[:, :, E], -88.0, None, ALU.max)
                step(dve.reduce_max(row_max[:], logits[:, :, 0:E], AX.X))
                for j in range(TJ):
                    ins = dve.tensor_scalar(d[:, j, :], logits[:, j, 0:E], row_max[:, j:j + 1], UNDERFLOW,
                                            ALU.subtract, ALU.max)
                step(ins, apart=True)
                for j in range(TJ):
                    ins = dve.max(top[:, j, :], d[:, j, :])
                step(ins, apart=True)
                for j in range(TJ):
                    ins = dve.max_index(top_at[:, j, :], top[:, j, :], d[:, j, :])
                ins.then_inc(top_ready, 1)

            def masks(b):
                dve.wait_ge(top_ready, b + 1)
                at_least(dve, pos_ready, b)
                step(dve.tensor_copy(top_f[:], top_at[:, :, 0:TOPK]))
                step(dve.tensor_tensor(
                    chosen[:], m.iota_e[:].unsqueeze(1).to_broadcast([P, TJ * TOPK, E]),
                    top_f[:].rearrange("p j k -> p (j k)").unsqueeze(2).to_broadcast([P, TJ * TOPK, E]), ALU.is_equal))
                with nc.allow_low_precision(reason="zeros and ones"):
                    dve.tensor_reduce(mask[:], chosen[:].rearrange("p (j k) e -> p j e k", k=TOPK), AX.X,
                                      ALU.add).then_inc(mask_ready, 1)

            def entries(b, q):
                dve.wait_ge(pos_ready, b + 1)
                step(dve.tensor_reduce(mask_sum[:], mask[:].rearrange("p j e -> p e j"), AX.X, ALU.add))
                with nc.allow_low_precision(reason="integers up to 32"):
                    dve.tensor_tensor(seen[:], seen[:], mask_sum[:], ALU.add)
                dve.tensor_scalar(past[:], pos, float(CAP), NO_SLOT, ALU.is_ge, ALU.mult)
                step(dve.scalar_tensor_tensor(out=place[:], in0=pos, scalar=float(E),
                                              in1=m.iota_e[:].unsqueeze(1).to_broadcast([P, TJ, E]), op0=ALU.mult,
                                              op1=ALU.add))
                step(dve.tensor_tensor(place_all[:], place[:], past[:], ALU.add))
                step(dve.tensor_tensor(
                    picked[:].rearrange("p (j k) e -> p j k e", k=TOPK), chosen[:].rearrange("p (j k) e -> p j k e", k=TOPK),
                    place_all[:].unsqueeze(2).to_broadcast([P, TJ, TOPK, E]), ALU.mult))
                at_least(dve, entry_ready, b)
                step(dve.tensor_reduce(slot_f[:], picked[:], AX.X, ALU.add))
                dve.tensor_copy(slot[:, q, :], slot_f[:])
                dve.tensor_copy(entry[:, q, :, 0], m.tok_f[:, m.turn, :])
                dve.wait_ge(exps_ready, 3 * (b + 1))
                step(dve.reduce_sum(total[:], exps[:], AX.X))
                step(dve.reciprocal(inv_total[:], total[:]))
                dve.scalar_tensor_tensor(
                    out=entry[:, q, :, 1].bitcast(F32).rearrange("p (j k) -> p j k", k=TOPK), in0=exp_top[:, :, 0:TOPK],
                    scalar=0.5, in1=inv_total[:].unsqueeze(2).to_broadcast([P, TJ, TOPK]), op0=ALU.mult, op1=ALU.mult)
                step(dve.tensor_scalar(gate_den[:], exp_gate[:], 2.0, 2.0, ALU.mult, ALU.add))
                dve.reciprocal(half_gate[:, q, :], gate_den[:]).then_inc(pos_used, 1)
                dve.tensor_scalar(m.tok_f[:, m.turn, :], m.tok_f[:, m.turn, :], float(BLK), None, ALU.add
                                  ).then_inc(entry_ready, 1)

            def product(b, mt):
                dve.wait_ge(silu_ready, b * MT + mt + 1)
                dve.wait_ge(gu_ready, CREDIT + b * GU + min(2 * mt + 2, GU))
                at_least(dve, a_hi_ready, b * MT + max(mt - 1, 0), CREDIT)
                at_least(dve, a_lo_ready, b * MT + max(mt - 1, 0), CREDIT)
                if mt < MT - 1:
                    dve.tensor_tensor(act_gu[:, mt % 2, :], silu[:, mt % 2, :], gu[(2 * mt + 1) % 3][:],
                                      ALU.mult).then_inc(prod_ready, 1)
                else:
                    dve.tensor_tensor(act_gu[0:LAST, mt % 2, :], silu[LAST:P, mt % 2, :], gu[(2 * mt) % 3][LAST:P, :],
                                      ALU.mult).then_inc(prod_ready, 1)

            def a_lo_part(b, mt):
                dve.wait_ge(a_hi_ready, CREDIT + b * MT + mt + 1)
                r = slice(0, P if mt < MT - 1 else LAST)
                dve.tensor_tensor(a_lo[r, mt, :], act_gu[r, mt % 2, :], a_hi[r, mt, :].bitcast(F32),
                                  ALU.subtract).then_inc(a_lo_ready, 1)

            def outputs(b, q, tiles):
                for j in tiles:
                    dve.wait_ge(down_ready, CREDIT + b * TJ + j // 2 * 2 + 2)
                    dve.scalar_tensor_tensor(out=base[:, q, j, :], in0=down[j // 2][:, j % 2, :],
                                             scalar=half_gate[:, q, j:j + 1], in1=base[:, q, j, :], op0=ALU.mult,
                                             op1=ALU.add).then_inc(out_ready, 1)

            def slot_of(b, q, ahead, further, n_after):
                product(b, 0)
                for mt in range(1, MT):
                    product(b, mt)
                    if ahead and mt == 1:
                        normalise(b + 1, 1 - q)
                    a_lo_part(b, mt - 1)
                    if ahead and mt == 1:
                        make_base(b + 1, 1 - q)
                    if ahead and mt == 2:
                        x_lo_parts(b + 1, 1 - q)
                a_lo_part(b, MT - 1)
                if ahead:
                    top_experts(b + 1)
                    masks(b + 1)
                if further:
                    front.statistics(dve, b + 2, q, n_after)
                outputs(b, q, (0, 1))
                if ahead:
                    entries(b + 1, 1 - q)
                outputs(b, q, (2, 3))

            give_credit(dve, prod_ready, out_ready, a_lo_ready)
            step(dve.memset(seen[:], 0.0))
            normalise(0, 0)
            x_lo_parts(0, 0)
            if weights:
                weights.low_parts(dve, weights.gu_splits, 0)
            front.statistics(dve, 1, 1, 0)
            top_experts(0)
            masks(0)
            make_base(0, 0)
            if weights:
                weights.low_parts(dve, weights.down_splits, len(weights.gu_splits))
            entries(0, 0)
            head, front.steps = front.steps, 0
            steps = 5 + 3 + 2 + 8
            with dve.Fori(0, NB // 2 - 1) as i:
                for q in range(2):
                    front.base = i * (2 * steps) + (head + q * steps)
                    front.steps = 0
                    slot_of(i * 2 + q, q, True, True, i + 1)
                    assert front.steps == steps
            front.base, front.steps = head + (NB - 2) * steps, 0
            slot_of(NB - 2, 0, True, False, 0)
            slot_of(NB - 1, 1, False, False, 0)


def experts(nc, m, tag, acc, inp, ins, attention_next=False, odd=None):
    ctx = ExitStack()
    with ctx:
        def sb(name, shape, dt):
            return ctx.enter_context(nc.sbuf_tensor(f"{name}_{tag}", shape, dt))

        def psum(name, shape):
            return ctx.enter_context(nc.psum_tensor(f"{name}_{tag}", shape, F32))

        def sem(name):
            return ctx.enter_context(nc.semaphore(f"{name}_{tag}"))

        PAIRS = E // 2
        w_gu, w_down, slots = inp.w_gu, inp.w_down, inp.slots
        table_loaded, gu_loaded, down_loaded = inp.table_loaded, inp.gu_loaded, inp.down_loaded
        source = sb("source", [P, 2, 2, 2], I32)
        target = sb("target", [P, 2, 2, 2], I32)
        rows = sb("rows", [P, 2, 2, C], F32)
        xT = sb("xT", [P, 2, KC, CAP], F32)
        silu = sb("silu_e", [P, 2, FE], F32)
        prod = sb("prod_e", [P, 2, FE], F32)
        prodT = sb("prodT", [FD, 2, 2, CAP], F32)
        y = sb("y", [P, 2, 2, C], F32)
        xT_ps = [psum(f"xT_ps{s}", [P, KC, CAP]) for s in range(2)]
        gu_ps = [psum(f"gu_ps{s}", [P, 2, FE]) for s in range(2)]
        prodT_ps = [psum(f"prodT_ps{s}", [P, 2, CAP]) for s in range(2)]
        y_ps = [psum(f"y_ps{s}", [P, C]) for s in range(2)]

        weights = AttentionWeights(nc, m, ins, sb, sem) if attention_next else None
        source_ready = sem("source_ready")
        target_ready = sem("target_ready")
        gathered = [sem("gathered0"), sem("gathered1")]
        xT_ready = sem("xT_ready")
        xT_copied = sem("xT_copied")
        gu_done = sem("gu_done")
        silu_done = sem("silu_done")
        prod_done = sem("prod_done")
        prodT_ready = sem("prodT_ready")
        prodT_copied = sem("prodT_copied")
        y_ready = sem("y_ready")
        y_scaled = sem("y_scaled")
        added = [sem("added0"), sem("added1")] if odd is not None else [sem("added")] * 2
        marks = inp.pool_marks

        block = ctx.enter_context(nc.Block())

        @block.sync
        def _(sp):
            if weights:
                weights.load(sp)
            with sp.Fori(0, PAIRS // 2 - 1) as i:
                for q in range(2):
                    p = i * 2 + q
                    sp.wait_ge(gu_done, CREDIT + p * 2 + 2)
                    inp.load_gate_up(sp, p + 2, q)
                    sp.wait_ge(y_ready, CREDIT + p * 2 + 2)
                    inp.load_down(sp, p + 2, q)

        @block.gpsimd
        def _(pool):
            def copy_source(p, q):
                at_least(pool, xT_ready, p * 2 - 2, CREDIT)
                pool.tensor_copy(source[:, q], slots[:, bass.ds(p * 2, 2), :]).then_inc(source_ready, 1)
                wait_apart(pool, source_ready, p + 1, marks)

            def gather(q, s):
                pool.indirect_dma_start(
                    out=rows[:, q, s, :], out_offset=None, in_=m.z_rows,
                    in_offset=bass.IndirectOffsetOnAxis(ap=source[:, q, s, 0:1], axis=0),
                    bounds_check=last_row, oob_is_err=False).then_inc(gathered[q], 16)

            def copy_target(p, q):
                pool.tensor_copy(target[:, q], slots[:, bass.ds(p * 2, 2), :]).then_inc(target_ready, 1)

            def add(p, q, s):
                pool.wait_ge(target_ready, p + 1)
                at_least(pool, added[s], p * 16 if odd is not None else (p * 2 + s) * 16)
                wait_apart(pool, y_scaled, CREDIT + p * 2 + (s + 1), marks)
                pool.indirect_dma_start(
                    out=odd if s and odd is not None else acc,
                    out_offset=bass.IndirectOffsetOnAxis(ap=target[:, q, s, 0:1], axis=0),
                    in_=y[:, q, s, :], in_offset=None, compute_op=ALU.add,
                    bounds_check=last_row, oob_is_err=True).then_inc(added[s], 16)

            def slot_of(p, q, ahead=True, further=True):
                add(p, q, 0)
                if ahead and odd is None:
                    copy_target(p + 1, 1 - q)
                if further:
                    copy_source(p + 3, 1 - q)
                    gather(1 - q, 0)
                add(p, q, 1)
                if ahead and odd is not None:
                    copy_target(p + 1, 1 - q)
                if further:
                    gather(1 - q, 1)

            last_row = pool.to_reg(T + PAD - 1)
            pool.wait_ge(table_loaded, 16)
            for p in range(3):
                copy_source(p, p % 2)
                for s in range(2):
                    gather(p % 2, s)
                if p == 0:
                    copy_target(0, 0)
            for q in range(2):
                pool.wait_ge(inp.acc_stored[q], 16 * (NB // 2))
            slot_of(0, 0)
            with pool.Fori(0, PAIRS // 2 - 2) as i:
                for q in range(2):
                    slot_of(i * 2 + (q + 1), 1 - q)
            slot_of(PAIRS - 3, 1, further=False)
            slot_of(PAIRS - 2, 0, further=False)
            slot_of(PAIRS - 1, 1, ahead=False, further=False)
            for s in range(2):
                pool.wait_ge(added[s], 16 * (PAIRS if odd is not None else E))

        @block.tensor
        def _(pe):
            def turn_rows(p, q, n):
                pe.wait_ge(gathered[q], (n + 1) * 32)
                pe.wait_ge(xT_copied, CREDIT + p * 2)
                for s in range(2):
                    for k in range(KC):
                        last = nc.tensor.transpose(xT_ps[s][:, k, :], rows[:, q, s, k * P:(k + 1) * P], m.ident[:])
                    last.then_inc(xT_ready, 1)

            def gate_up(p, q, n, s):
                pe.wait_ge(gu_loaded[q], (n + 1) * 64)
                pe.wait_ge(prod_done, CREDIT + p * 2)
                pe.wait_ge(xT_copied, CREDIT + p * 2 + (s + 1))
                for k in range(KC):
                    last = nc.tensor.matmul(gu_ps[s][:].rearrange("p a f -> p (a f)"), xT[:, s, k, :],
                                            w_gu[:, q, s, k, :, :].rearrange("p a f -> p (a f)"),
                                            start=k == 0, stop=k == KC - 1)
                last.then_inc(gu_done, 1)

            def turn_products(p, s):
                pe.wait_ge(prod_done, CREDIT + p * 2 + (s + 1))
                pe.wait_ge(prodT_copied, CREDIT + p * 2)
                for k in range(2):
                    last = nc.tensor.transpose(prodT_ps[s][0:FD, k, :], prod[:, s, k * FD:(k + 1) * FD], m.ident[:])
                last.then_inc(prodT_ready, 1)

            def down_proj(p, q, n, s):
                pe.wait_ge(down_loaded[q], (n + 1) * 32)
                pe.wait_ge(prodT_copied, CREDIT + p * 2 + (s + 1))
                pe.wait_ge(y_scaled, CREDIT + p * 2)
                for k in range(2):
                    last = nc.tensor.matmul(y_ps[s][:], prodT[:, s, k, :], w_down[:, q, s, k, :], start=k == 0,
                                            stop=k == 1)
                last.then_inc(y_ready, 1)

            def slot_of(p, q, n, n_next, ahead=True):
                if ahead:
                    turn_rows(p + 1, 1 - q, n_next)
                for s in range(2):
                    turn_products(p, s)
                if ahead:
                    gate_up(p + 1, 1 - q, n_next, 0)
                for s in range(2):
                    down_proj(p, q, n, s)
                if ahead:
                    gate_up(p + 1, 1 - q, n_next, 1)

            give_credit(pe, xT_ready, gu_done, prodT_ready, y_ready)
            turn_rows(0, 0, 0)
            for s in range(2):
                gate_up(0, 0, 0, s)
            with pe.Fori(0, PAIRS // 2 - 1) as i:
                for q in range(2):
                    slot_of(i * 2 + q, q, i, i + q)
            slot_of(PAIRS - 2, 0, PAIRS // 2 - 1, PAIRS // 2 - 1)
            slot_of(PAIRS - 1, 1, PAIRS // 2 - 1, 0, ahead=False)

        @block.scalar
        def _(act):
            def silu_of(p, s):
                act.wait_ge(gu_done, CREDIT + p * 2 + (s + 1))
                act.wait_ge(prod_done, CREDIT + p * 2)
                nc.scalar.activation(silu[:, s, :], gu_ps[s][:, 0, :], ACT.Silu).then_inc(silu_done, 1)

            def scale(p, q, s):
                act.wait_ge(y_ready, CREDIT + p * 2 + (s + 1))
                act.wait_ge(target_ready, p + 1)
                nc.scalar.activation(y[:, q, s, :], y_ps[s][:], ACT.Copy,
                                     scale=target[:, q, s, 1:2].bitcast(F32)).then_inc(y_scaled, 1)

            def slot_of(p, q, ahead=True):
                if ahead:
                    silu_of(p + 1, 0)
                for s in range(2):
                    scale(p, q, s)
                if ahead:
                    silu_of(p + 1, 1)

            give_credit(act, y_scaled)
            for s in range(2):
                silu_of(0, s)
            with act.Fori(0, PAIRS // 2 - 1) as i:
                for q in range(2):
                    slot_of(i * 2 + q, q)
            slot_of(PAIRS - 2, 0)
            slot_of(PAIRS - 1, 1, ahead=False)
            if weights:
                weights.high_parts(act)

        @block.vector
        def _(dve):
            def copy_rows(p):
                dve.wait_ge(gu_done, CREDIT + p * 2)
                for s in range(2):
                    dve.wait_ge(xT_ready, CREDIT + p * 2 + (s + 1))
                    for k in range(KC):
                        last = dve.tensor_scalar(xT[:, s, k, :], xT_ps[s][:, k, :], m.w_norm[:, k:k + 1], None, ALU.mult)
                    last.then_inc(xT_copied, 1)

            def product(p, s):
                dve.wait_ge(silu_done, p * 2 + (s + 1))
                dve.wait_ge(prodT_ready, CREDIT + p * 2)
                dve.tensor_tensor(prod[:, s, :], silu[:, s, :], gu_ps[s][:, 1, :], ALU.mult).then_inc(prod_done, 1)

            def copy_products(p, s):
                dve.wait_ge(prodT_ready, CREDIT + p * 2 + (s + 1))
                dve.wait_ge(y_ready, CREDIT + p * 2)
                dve.tensor_copy(prodT[:, s], prodT_ps[s][0:FD]).then_inc(prodT_copied, 1)

            def slot_of(p, ahead=True):
                if ahead:
                    copy_rows(p + 1)
                for s in range(2):
                    copy_products(p, s)
                if ahead:
                    for s in range(2):
                        product(p + 1, s)

            give_credit(dve, xT_copied, prod_done, prodT_copied)
            copy_rows(0)
            for s in range(2):
                product(0, s)
            with dve.Fori(0, PAIRS // 2 - 1) as i:
                for q in range(2):
                    slot_of(i * 2 + q)
            slot_of(PAIRS - 2)
            slot_of(PAIRS - 1, ahead=False)
            if weights:
                weights.low_parts(dve)


def attention(nc, m, src, odd, dst, front):
    ctx = ExitStack()
    with ctx:
        def sb(name, shape, dt):
            return ctx.enter_context(nc.sbuf_tensor(f"{name}_at", shape, dt))

        def psum(name, shape):
            return ctx.enter_context(nc.psum_tensor(f"{name}_at", shape, F32))

        def sem(name):
            return ctx.enter_context(nc.semaphore(f"{name}_at"))

        QT = SEQ // P
        GROUPS = 2
        UNITS = GROUPS * QT
        PIECES = 3
        JH = 4
        PIECE_BANK = (1, 0, 1, 1)
        W = REP * SEQ

        xn = sb("xn", [P, 2, QT, C], F32)
        xr = sb("xr", [P, 2, QT, C], F32)
        warm = sb("warm", [P, 1], F32)
        xn_odd = sb("xn_odd", [P, 2, QT, C], F32)
        xr_odd = sb("xr_odd", [P, 2, QT, C], F32)
        a = sb("a", [P, QT, C], F32)
        stats = sb("stats", [P, QT, 6], F32)
        moments = sb("moments", [P, QT, 2], F32)
        var_in = sb("var_in", [P, QT], F32)
        rstd = sb("rstd", [P, QT], F32)
        aT_hi = sb("aT_hi", [P, KC, SEQ], F32R)
        aT_lo = sb("aT_lo", [P, KC, SEQ], F32R)
        turned = sb("turned", [P, PIECES, 2, SEQ], F32)
        by_cos = sb("by_cos", [P, PIECES, 2, SEQ], F32)
        by_sin = sb("by_sin", [P, PIECES, 2, SEQ], F32)
        roped = sb("roped", [P, PIECES, 2, SEQ], F32)
        qk_hi = sb("qkT_hi", [P, 2, 6, SEQ], F32R)
        qk_lo = sb("qkT_lo", [P, 2, 6, SEQ], F32R)
        v = sb("v", [P, 2, QT, C], F32)
        capped = sb("capped", [P, 2, JH, W], F32)
        probs = sb("probs", [P, 2, JH, W], F32)
        pv_sb = sb("pv_sb", [P, GROUPS, W], F32)
        den_sb = sb("den_sb", [P, GROUPS, W], F32)
        inv_den = sb("inv_den", [P, W], F32)
        y = sb("y", [P, W], F32)
        y_hi = sb("y_hi", [P, GROUPS, W], F32R)
        y_lo = sb("y_lo", [P, GROUPS, W], F32R)

        scores = psum("scores", [P, JH, W])
        pv = psum("pv", [P, W])
        den = psum("den", [P, W])
        pj = [psum(f"pj{n}", [P, 2, SEQ]) for n in range(2)]

        xn_loaded = [sem("xn_loaded0"), sem("xn_loaded1")]
        xr_loaded = [sem("xr_loaded0"), sem("xr_loaded1")]
        xn_summed = sem("xn_summed")
        xr_summed = sem("xr_summed")
        stored = [sem("stored0"), sem("stored1")]
        stat = sem("stat")
        marks = sem("marks")
        pool_marks = sem("pool_marks")
        var_ready = sem("var_ready")
        rstd_ready = sem("rstd_ready")
        a_ready = sem("a_ready")
        aT_ready = sem("aT_ready")
        aT_hi_ready = sem("aT_hi_ready")
        aT_lo_ready = sem("aT_lo_ready")
        piece_ready = sem("piece_ready")
        turned_ready = sem("turned_ready")
        sin_done = sem("sin_done")
        roped_ready = sem("roped_ready")
        qk_hi_ready = sem("qk_hi_ready")
        qk_lo_ready = sem("qk_lo_ready")
        v_copied = sem("v_copied")
        scores_ready = sem("scores_ready")
        capped_ready = sem("capped_ready")
        exp_ready = sem("exp_ready")
        probs_ready = sem("probs_ready")
        pv_done = sem("pv_done")
        taken = sem("taken")
        inv_ready = sem("inv_ready")
        y_ready = sem("y_ready")
        y_hi_ready = sem("y_hi_ready")
        y_lo_ready = sem("y_lo_ready")
        out_ready = sem("out_ready")
        x2_ready = sem("x2_ready")

        def seq_rows(dram, b):
            return dram[bass.ds(b * SEQ, SEQ), :].rearrange("(t p) c -> p t c", p=P)

        block = ctx.enter_context(nc.Block())

        @block.sync
        def _(sp):
            def load_norm(b, q):
                at_least(sp, a_ready, b - 1)
                sp.dma_start(xn[:, q], seq_rows(src, b)).then_inc(xn_loaded[q], 16)
                sp.dma_start(xn_odd[:, q], seq_rows(odd, b)).then_inc(xn_loaded[q], 16)

            def load_residual(b, q, n):
                at_least(sp, stored[q], 16 * n)
                sp.dma_start(xr[:, q], seq_rows(src, b)).then_inc(xr_loaded[q], 16)
                sp.dma_start(xr_odd[:, q], seq_rows(odd, b)).then_inc(xr_loaded[q], 16)

            def store(b, q):
                sp.wait_ge(x2_ready, b + 1)
                sp.dma_start(seq_rows(dst, b), xr[:, q]).then_inc(stored[q], 16)

            for q in range(2):
                load_norm(q, q)
            for q in range(2):
                load_residual(q, q, 0)
            for q in range(2):
                load_norm(q + 2, q)
            with sp.Fori(0, SEQS // 2 - 2) as i:
                for q in range(2):
                    store(i * 2 + q, q)
                    load_residual(i * 2 + (q + 2), q, i + 1)
                    load_norm(i * 2 + (q + 4), q)
            for q in range(2):
                store(SEQS - 4 + q, q)
                load_residual(SEQS - 2 + q, q, SEQS // 2 - 1)
            for b in range(2):
                for q in range(2):
                    sp.wait_ge(stored[q], 16 * (b + 1) * (BLK // SEQ // 2))
                front.load(sp, b, b)
            for q in range(2):
                store(SEQS - 2 + q, q)
            for q in range(2):
                sp.wait_ge(stored[q], 16 * (SEQS // 2))

        @block.tensor
        def _(pe):
            def transposes(b):
                pe.wait_ge(a_ready, b + 1)
                at_least(pe, x2_ready, b - 2)
                for k in range(KC):
                    for t in range(QT):
                        last = nc.tensor.transpose(pj[0][:, k, t * P:(t + 1) * P], a[:, t, k * P:(k + 1) * P], m.ident[:])
                last.then_inc(aT_ready, 1)

            def project(b, q, n):
                bank = pj[PIECE_BANK[n]]
                if n == 0:
                    at_least(pe, v_copied, b)
                    pe.wait_ge(aT_lo_ready, b + 1)
                elif n >= 2:
                    pe.wait_ge(turned_ready, b * PIECES + (1 if n == 2 else 3))
                for c in range(2):
                    for k in range(KC):
                        if n < PIECES:
                            chunk = 2 * ((n - 1) % PIECES) + c
                            last = split_matmul(nc, bank[:, c, :], m.qk_hi[:, k, chunk, :], m.qk_lo[:, k, chunk, :],
                                                aT_hi[:, k, :], aT_lo[:, k, :], k == 0, k == KC - 1)
                        else:
                            at = slice(c * P, (c + 1) * P)
                            last = split_matmul(nc, bank[:, c, :], aT_hi[:, k, at], aT_lo[:, k, at],
                                                m.v_hi[:, k, :], m.v_lo[:, k, :], k == 0, k == KC - 1)
                last.then_inc(piece_ready, 1)

            def score_unit(b, q, u):
                g, t = u // QT, u % QT
                at_least(pe, capped_ready, b * UNITS + u)
                if t == 0:
                    pe.wait_ge(qk_lo_ready, b * PIECES + (2 + g))
                keys = slice(t * P, (t + 1) * P)
                n = REP * (SEQ - t * P)
                for k_part, q_part in ((qk_hi, qk_hi), (qk_lo, qk_hi), (qk_hi, qk_lo)):
                    for j in range(JH):
                        r = slice(j * HD, (j + 1) * HD)
                        last = nc.tensor.matmul(
                            scores[:, j, 0:n].rearrange("p (r s) -> p r s", r=REP), k_part[r, q, 4 + g, keys],
                            q_part[r, q, REP * g:REP * g + REP, t * P:SEQ],
                            start=k_part is qk_hi and q_part is qk_hi, stop=q_part is qk_lo)
                last.then_inc(scores_ready, 1)

            def weighted_values(b, q, u):
                g, t = u // QT, u % QT
                pe.wait_ge(probs_ready, b * UNITS + u + 1)
                if t == 0:
                    at_least(pe, taken, b * GROUPS + g)
                n = REP * (SEQ - t * P)
                for bank, ones in ((den, True), (pv, False)):
                    for j in range(JH):
                        w = m.ones_f[:] if ones else v[:, q, t, (JH * g + j) * HD:(JH * g + j + 1) * HD]
                        out = bank[j * HD:(j + 1) * HD, :].rearrange("p (r s) -> p r s", r=REP)[:, :, t * P:SEQ]
                        last = nc.tensor.matmul(out, w, probs[:, u % 2, j, 0:n].rearrange("p (r s) -> p r s", r=REP),
                                                start=t == 0, stop=t == QT - 1)
                last.then_inc(pv_done, 1)

            def output(b):
                pe.wait_ge(y_lo_ready, b * GROUPS + GROUPS)
                pe.wait_ge(turned_ready, (b + 2) * PIECES + 2 if not isinstance(b, int) else min(
                    (b + 2) * PIECES + 2, SEQS * PIECES))
                for t in range(QT):
                    for g in range(GROUPS):
                        for r in range(REP):
                            at = slice(r * SEQ + t * P, r * SEQ + (t + 1) * P)
                            n = REP * g + r
                            last = split_matmul(nc, pj[0][:, t, :], y_hi[:, g, at], y_lo[:, g, at], m.o_hi[:, n, :],
                                                m.o_lo[:, n, :], n == 0, n == 3)
                last.then_inc(out_ready, 1)

            def slot_of(b, q, behind=True, ahead=True):
                score_unit(b, q, 0)
                if ahead:
                    transposes(b + 1)
                if behind:
                    weighted_values(b - 1, 1 - q, 3)
                if ahead:
                    project(b + 1, 1 - q, 0)
                score_unit(b, q, 1)
                if ahead:
                    project(b + 1, 1 - q, 1)
                weighted_values(b, q, 0)
                score_unit(b, q, 2)
                if ahead:
                    project(b + 1, 1 - q, 2)
                weighted_values(b, q, 1)
                score_unit(b, q, 3)
                if behind:
                    output(b - 1)
                if ahead:
                    project(b + 1, 1 - q, 3)
                weighted_values(b, q, 2)

            transposes(0)
            for n in range(4):
                project(0, 0, n)
            slot_of(0, 0, behind=False)
            with pe.Fori(0, SEQS // 2 - 2) as i:
                for q in range(2):
                    slot_of(i * 2 + (q + 1), 1 - q)
            slot_of(SEQS - 3, 1)
            slot_of(SEQS - 2, 0)
            slot_of(SEQS - 1, 1, ahead=False)
            weighted_values(SEQS - 1, 1, 3)
            output(SEQS - 1)

        @block.scalar
        def _(act):
            def aT_hi_part(b):
                act.wait_ge(aT_ready, b + 1)
                at_least(act, piece_ready, 4 * b)
                nc.scalar.copy(aT_hi[:], pj[0][:]).then_inc(aT_hi_ready, 1)

            def qk_hi_part(b, q, n):
                act.wait_ge(roped_ready, b * PIECES + n + 1)
                at_least(act, scores_ready, UNITS * (b - 1))
                c = 2 * ((n - 1) % PIECES)
                nc.scalar.copy(qk_hi[:, q, c:c + 2, :], roped[:, n]).then_inc(qk_hi_ready, 1)

            def copy_v(b, q):
                act.wait_ge(piece_ready, 4 * b + 4)
                at_least(act, pv_done, UNITS * (b - 1))
                nc.scalar.copy(v[:, q], pj[PIECE_BANK[3]][:]).then_inc(v_copied, 1)

            def cap(b, u):
                act.wait_ge(scores_ready, b * UNITS + u + 1)
                n = REP * (SEQ - u % QT * P)
                at_least(act, exp_ready, b * UNITS + max(u - 1, 0))
                nc.scalar.activation(capped[:, u % 2, :, 0:n], scores[:, :, 0:n], ACT.Tanh,
                                     scale=QK_SCALE / SOFTCAP).then_inc(capped_ready, 1)

            def exponential(b, u):
                act.wait_ge(capped_ready, b * UNITS + u + 1)
                at_least(act, pv_done, b * UNITS + max(u - 1, 0))
                n = REP * (SEQ - u % QT * P)
                nc.scalar.activation(probs[:, u % 2, :, 0:n], capped[:, u % 2, :, 0:n], ACT.Exp,
                                     scale=SOFTCAP).then_inc(exp_ready, 1)

            def take_values(b, g):
                act.wait_ge(pv_done, b * UNITS + QT * (g + 1))
                at_least(act, y_ready, b * GROUPS + (g - 1))
                nc.scalar.copy(den_sb[:, g, :], den[:])
                nc.scalar.copy(pv_sb[:, g, :], pv[:]).then_inc(taken, 1)

            def y_hi_part(b, g):
                act.wait_ge(y_ready, b * GROUPS + g + 1)
                at_least(act, out_ready, b)
                nc.scalar.copy(y_hi[:, g, :], y[:]).then_inc(y_hi_ready, 1)

            def slot_of(b, q, behind=True, ahead=True):
                if ahead:
                    aT_hi_part(b + 1)
                cap(b, 0)
                exponential(b, 0)
                if behind:
                    take_values(b - 1, 1)
                cap(b, 1)
                exponential(b, 1)
                if behind:
                    y_hi_part(b - 1, 1)
                cap(b, 2)
                if ahead:
                    qk_hi_part(b + 1, 1 - q, 0)
                exponential(b, 2)
                take_values(b, 0)
                if ahead:
                    qk_hi_part(b + 1, 1 - q, 1)
                cap(b, 3)
                exponential(b, 3)
                if ahead:
                    qk_hi_part(b + 1, 1 - q, 2)
                    copy_v(b + 1, 1 - q)
                y_hi_part(b, 0)

            nc.scalar.activation(warm[:], m.w_norm[:, 0:1], ACT.Exp)
            aT_hi_part(0)
            for n in range(PIECES):
                qk_hi_part(0, 0, n)
            copy_v(0, 0)
            slot_of(0, 0, behind=False)
            with act.Fori(0, SEQS // 2 - 2) as i:
                for q in range(2):
                    slot_of(i * 2 + (q + 1), 1 - q)
            slot_of(SEQS - 3, 1)
            slot_of(SEQS - 2, 0)
            slot_of(SEQS - 1, 1, ahead=False)
            take_values(SEQS - 1, 1)
            y_hi_part(SEQS - 1, 1)

        @block.gpsimd
        def _(pool):
            def root(b):
                pool.wait_ge(var_ready, b + 1)
                pool.tensor_tensor(rstd[:], var_in[:], m.neg_half[:, 0, 0:QT], ALU.pow).then_inc(rstd_ready, 1)

            def rope(b, n):
                pool.wait_ge(turned_ready, b * PIECES + n + 1)
                at_least(pool, qk_lo_ready, b * PIECES + (n + 1 - PIECES))
                sin = m.sin[:].unsqueeze(1).to_broadcast([P, 2, SEQ])
                pool.tensor_tensor(by_sin[:, n], turned[:, n], sin, ALU.mult).then_inc(sin_done, 1)
                pool.wait_ge(sin_done, b * PIECES + n + 1)
                pool.tensor_tensor(roped[:, n], by_cos[:, n], by_sin[:, n], ALU.add).then_inc(roped_ready, 1)

            def causal(b, u):
                wait_apart(pool, exp_ready, b * UNITS + u + 1, pool_marks)
                n = REP * (SEQ - u % QT * P)
                diag = probs[:, u % 2, :, 0:n].rearrange("p j (r s) -> p j r s", r=REP)[:, :, :, 0:P]
                pool.affine_select(out=diag, in_=diag, compare_op=ALU.is_ge, fill=zero, base=0,
                                   pattern=[[0, JH], [0, REP], [1, P]], channel_multiplier=-1).then_inc(probs_ready, 1)

            def sum_residual(b, q, n):
                pool.wait_ge(xr_loaded[q], 32 * (n + 1))
                pool.tensor_tensor(xr[:, q], xr[:, q], xr_odd[:, q], ALU.add).then_inc(xr_summed, 1)

            def slot_of(b, q, n, ahead=True, further=True):
                causal(b, 0)
                causal(b, 1)
                if ahead:
                    rope(b + 1, 0)
                    rope(b + 1, 1)
                if further:
                    root(b + 2)
                causal(b, 2)
                if ahead:
                    rope(b + 1, 2)
                causal(b, 3)
                sum_residual(b, q, n)

            zero = pool.to_reg(0.0)
            root(0)
            root(1)
            for n in range(PIECES):
                rope(0, n)
            slot_of(0, 0, 0)
            with pool.Fori(0, SEQS // 2 - 2) as i:
                for q in range(2):
                    slot_of(i * 2 + (q + 1), 1 - q, i + q)
            slot_of(SEQS - 3, 1, SEQS // 2 - 2)
            slot_of(SEQS - 2, 0, SEQS // 2 - 1, further=False)
            slot_of(SEQS - 1, 1, SEQS // 2 - 1, ahead=False, further=False)
            front.roots(pool, 0, 0)

        @block.vector
        def _(dve):
            def statistics(b, q, n):
                dve.wait_ge(xn_loaded[q], 32 * (n + 1))
                dve.tensor_tensor(xn[:, q], xn[:, q], xn_odd[:, q], ALU.add).then_inc(xn_summed, 1)
                dve.wait_ge(xn_summed, b + 1)
                for t in range(QT):
                    ins = dve.bn_stats(stats[:, t, :], xn[:, q, t, :])
                ins.then_inc(stat, 1)
                wait_apart(dve, stat, b * 2 + 1, marks)
                for t in range(QT):
                    ins = dve.bn_aggr(moments[:, t, :], stats[:, t, :])
                ins.then_inc(stat, 1)
                dve.wait_ge(stat, b * 2 + 2)
                dve.tensor_scalar(var_in[:], moments[:, :, 1], LN_EPS, None, ALU.add).then_inc(var_ready, 1)

            def normalise(b, q):
                dve.wait_ge(rstd_ready, b + 1)
                at_least(dve, aT_ready, b)
                for t in range(QT):
                    ins = dve.tensor_scalar(a[:, t, :], xn[:, q, t, :], moments[:, t, 0:1], rstd[:, t:t + 1],
                                            ALU.subtract, ALU.mult)
                ins.then_inc(a_ready, 1)

            def aT_lo_part(b):
                dve.wait_ge(aT_hi_ready, b + 1)
                dve.tensor_tensor(aT_lo[:], pj[0][:], aT_hi[:].bitcast(F32), ALU.subtract).then_inc(aT_lo_ready, 1)

            def turn(b, n):
                dve.wait_ge(piece_ready, b * 4 + n + 1)
                at_least(dve, roped_ready, b * PIECES + (n + 1 - PIECES))
                cos = m.cos[:].unsqueeze(1).to_broadcast([P, 2, SEQ])
                bank = pj[PIECE_BANK[n]]
                dve.tensor_tensor(by_cos[:, n], bank[:], cos, ALU.mult)
                dve.stream_shuffle(turned[:, n], bank[:], [(i + HD // 2) % HD for i in range(HD)]).then_inc(turned_ready, 1)

            def qk_lo_part(b, q, n):
                dve.wait_ge(qk_hi_ready, b * PIECES + n + 1)
                c = 2 * ((n - 1) % PIECES)
                dve.tensor_tensor(qk_lo[:, q, c:c + 2, :], roped[:, n], qk_hi[:, q, c:c + 2, :].bitcast(F32),
                                  ALU.subtract).then_inc(qk_lo_ready, 1)

            def invert(b, g):
                dve.wait_ge(taken, b * GROUPS + g + 1)
                dve.reciprocal(inv_den[:], den_sb[:, g, :]).then_inc(inv_ready, 1)

            def divide(b, g):
                dve.wait_ge(inv_ready, b * GROUPS + g + 1)
                at_least(dve, y_hi_ready, b * GROUPS + g)
                dve.tensor_tensor(y[:], pv_sb[:, g, :], inv_den[:], ALU.mult).then_inc(y_ready, 1)

            def y_lo_part(b, g):
                dve.wait_ge(y_hi_ready, b * GROUPS + g + 1)
                dve.tensor_tensor(y_lo[:, g, :], y[:], y_hi[:, g, :].bitcast(F32), ALU.subtract).then_inc(y_lo_ready, 1)

            def residual(b, q):
                dve.wait_ge(out_ready, b + 1)
                dve.wait_ge(xr_summed, b + 1)
                dve.tensor_tensor(xr[:, q], xr[:, q], pj[0][:], ALU.add).then_inc(x2_ready, 1)

            def slot_of(b, q, n_further, behind=True, ahead=True, further=True):
                if ahead:
                    aT_lo_part(b + 1)
                    turn(b + 1, 0)
                if behind:
                    invert(b - 1, 1)
                    divide(b - 1, 1)
                    y_lo_part(b - 1, 1)
                if ahead:
                    turn(b + 1, 1)
                if further:
                    statistics(b + 2, q, n_further)
                if ahead:
                    qk_lo_part(b + 1, 1 - q, 0)
                    turn(b + 1, 2)
                if further:
                    normalise(b + 2, q)
                if ahead:
                    qk_lo_part(b + 1, 1 - q, 1)
                invert(b, 0)
                if ahead:
                    qk_lo_part(b + 1, 1 - q, 2)
                divide(b, 0)
                if behind:
                    residual(b - 1, 1 - q)
                y_lo_part(b, 0)

            statistics(0, 0, 0)
            normalise(0, 0)
            statistics(1, 1, 0)
            aT_lo_part(0)
            normalise(1, 1)
            for n in range(PIECES):
                turn(0, n)
            for n in range(PIECES):
                qk_lo_part(0, 0, n)
            slot_of(0, 0, 1, behind=False)
            with dve.Fori(0, SEQS // 2 - 2) as i:
                slot_of(i * 2 + 1, 1, i + 1)
                slot_of(i * 2 + 2, 0, i + 2)
            slot_of(SEQS - 3, 1, SEQS // 2 - 1)
            slot_of(SEQS - 2, 0, 0, further=False)
            slot_of(SEQS - 1, 1, 0, ahead=False, further=False)
            invert(SEQS - 1, 1)
            divide(SEQS - 1, 1)
            y_lo_part(SEQS - 1, 1)
            front.statistics(dve, 0, 0, 0)
            residual(SEQS - 1, 1)


def build(nc, ins, out):
    m = Memory()
    ctx = ExitStack()
    with ctx:
        def sb(name, shape, dt):
            return ctx.enter_context(nc.sbuf_tensor(name, shape, dt))

        m.gu_hi = sb("gu_hi", [P, KC, GU, P], F32R)
        m.gu_lo = sb("gu_lo", [P, KC, GU, P], F32R)
        m.down_hi = sb("down_hi", [P, MT, C], F32R)
        m.down_lo = sb("down_lo", [P, MT, C], F32R)
        m.router_hi = sb("router_hi", [P, KC, RW], F32R)
        m.router_lo = sb("router_lo", [P, KC, RW], F32R)
        m.qk_hi = sb("qk_hi", [P, KC, 6, P], F32R)
        m.qk_lo = sb("qk_lo", [P, KC, 6, P], F32R)
        m.v_hi = sb("v_hi", [P, KC, C], F32R)
        m.v_lo = sb("v_lo", [P, KC, C], F32R)
        m.o_hi = sb("o_hi", [P, 4, C], F32R)
        m.o_lo = sb("o_lo", [P, 4, C], F32R)
        m.w_norm = sb("w_norm", [P, KC], F32)
        m.zeros = sb("zeros", [P, C], F32)
        m.cos = sb("cos", [P, SEQ], F32)
        m.sin = sb("sin", [P, SEQ], F32)
        m.ident = sb("ident", [P, P], F32)
        m.before = sb("before", [P, P], BF16)
        m.ones_b = sb("ones_b", [P, P], BF16)
        m.ones_f = sb("ones_f", [P, HD], F32)
        m.neg_half = sb("neg_half", [P, 2, TJ], F32)
        m.iota_e = sb("iota_e", [P, E], F32)
        m.tok_f = sb("tok_f", [P, 2, TJ * TOPK], F32)
        m.z_rows = nc.dram_tensor("z_rows", [T + PAD, C], F32, kind="Internal").ap()
        m.acc1 = nc.dram_tensor("acc1", [T + PAD, C], F32, kind="Internal").ap()
        m.odd1 = nc.dram_tensor("odd1", [T + PAD, C], F32, kind="Internal").ap()
        m.x2 = nc.dram_tensor("x2", [T, C], F32, kind="Internal").ap()
        m.acc2 = out
        m.table1 = nc.dram_tensor("table1", [E * CAP, 2], I32, kind="Internal").ap()
        m.table2 = nc.dram_tensor("table2", [E * CAP, 2], I32, kind="Internal").ap()

        def tools(stack, tag):
            return (lambda name, shape, dt: stack.enter_context(nc.sbuf_tensor(f"{name}_{tag}", shape, dt)),
                    lambda name: stack.enter_context(nc.semaphore(f"{name}_{tag}")))

        m.turn = 0
        with ExitStack() as until_experts:
            inputs = ExpertInputs(nc, m, m.table1, ins, *tools(until_experts, "1"))
            with ExitStack() as until_route:
                front = Front(nc, m, ins["X"], *tools(until_route, "f1"))
                weights = SharedWeights(nc, m, ins, *tools(until_route, "1"))
                setup(nc, m, ins, front, weights)
                route_and_shared(nc, m, "r1", m.acc1, m.table1, front, inputs, weights, odd=m.odd1)
            experts(nc, m, "e1", m.acc1, inputs, ins, attention_next=True, odd=m.odd1)
        m.turn = 1
        with ExitStack() as until_route:
            front = Front(nc, m, m.x2, *tools(until_route, "f2"))
            attention(nc, m, m.acc1, m.odd1, m.x2, front)
            with ExitStack() as until_experts:
                inputs = ExpertInputs(nc, m, m.table2, ins, *tools(until_experts, "2"))
                route_and_shared(nc, m, "r2", m.acc2, m.table2, front, inputs)
                experts(nc, m, "e2", m.acc2, inputs, ins)


NAMES = {"X": "L0_attn_X", "Wq": "L0_attn_Wq", "Wk": "L0_attn_Wk", "Wv": "L0_attn_Wv", "Wo": "L0_attn_Wo",
         "w_norm": "L0_ffn_w_norm", "w_router": "L0_ffn_w_router", "w_gate": "L0_ffn_w_gate",
         "w_up": "L0_ffn_w_up", "w_down": "L0_ffn_w_down", "sw_gate": "L0_ffn_sw_gate",
         "sw_up": "L0_ffn_sw_up", "sw_down": "L0_ffn_sw_down", "w_sgate": "L0_ffn_w_shared_gate"}


def rotary_tables():
    inv_freq = (np.float32(1.0) / np.float32(10000.0) ** (np.arange(0, HD, 2, dtype=np.float32) / np.float32(HD)))
    freqs = np.arange(SEQ, dtype=np.float32)[:, None] * inv_freq.astype(np.float32)[None, :]
    angle = np.tile(np.concatenate((freqs, freqs), axis=-1).T, (P // HD, 1))
    sign = np.tile(np.repeat(np.array([-1.0, 1.0], np.float32), HD // 2), P // HD)[:, None]
    return np.cos(angle).astype(np.float32), (np.sin(angle) * sign).astype(np.float32)


def kernel(**inputs):
    import concourse.bacc as bacc
    from concourse.bass_utils import run_bass_kernel_spmd

    nc = bacc.Bacc("TRN2", target_bir_lowering=False, num_devices=1)
    arrays = {name: np.ascontiguousarray(inputs[of]) for name, of in NAMES.items()}
    arrays["X"] = arrays["X"].reshape(T, C)
    arrays["cos"], arrays["sin"] = rotary_tables()
    ins = {name: nc.dram_tensor(f"in_{name}", a.shape, mybir.dt.from_np(a.dtype), kind="ExternalInput").ap()
           for name, a in arrays.items()}
    out = nc.dram_tensor("out", [T + PAD, C], F32, kind="ExternalOutput").ap()
    build(nc, ins, out)
    result = run_bass_kernel_spmd(nc, [{f"in_{name}": a for name, a in arrays.items()}], core_ids=[0])
    return result.results[0]["out"][:T].reshape(SEQS, SEQ, C)
```
